# Optimizing a Trainium2 kernel written in Bass

```python
import numpy as np
import jax
import jax.numpy as jnp

def _softmax(x, axis=-1):
    return jax.nn.softmax(x, axis=axis)

def _gelu(x):
    return jax.nn.gelu(x, approximate=True)

def _silu(x):
    return jax.nn.silu(x)

def _sigmoid(x):
    return jax.nn.sigmoid(x)

def _layernorm(x, axis=-1, eps=1e-05):
    m = jnp.mean(x, axis=axis, keepdims=True)
    v = jnp.var(x, axis=axis, keepdims=True)
    return (x - m) / jnp.sqrt(v + eps)

def _scatter_add(tgt, idx, src, axis=0):
    return tgt.at[idx].add(src)

def _segment_sum(src, seg, n):
    return jax.ops.segment_sum(src, seg, n)
kernel_name = 'mk_vit_tower_cls_d1_tok_img768_r4_6a9a7d'

def setup_inputs(seed: int=0):
    np.random.seed(seed)
    _w = jnp.asarray

    def _rec_inputs():
        import jax
        import jax.numpy as jnp
        _rk = jax.random.key(seed)
        x = -0.00016672 + 0.999947 * jax.random.normal(jax.random.fold_in(_rk, 1), (32, 3, 84, 84), jnp.float32)
        cls_tok = 0.02 * jax.random.normal(jax.random.fold_in(_rk, 5), (1, 1, 192), jnp.float32)
        return (x, cls_tok)
    x, cls_tok = _rec_inputs()

    def _L0_tok_setup():
        import math
        import jax, jax.numpy as jnp
        import numpy as np
        IMG = (96, 96)
        PATCH = (16, 16)
        CH = 3
        LEN = 192
        B = 64
        NPATCH = IMG[0] // PATCH[0] * (IMG[1] // PATCH[1])

        def _pos_encoding(n_patch, length, dtype):
            i = jnp.arange(n_patch, dtype=dtype)[:, None]
            j = jnp.arange(length)
            expo = (2 * (j // 2)).astype(dtype) / length
            angle = i / jnp.power(jnp.asarray(10000.0, dtype), expo)
            angle = angle + jnp.where(j % 2 == 1, jnp.asarray(math.pi / 2, dtype), 0.0)
            return jnp.sin(angle)
        key = jax.random.key(seed)
        k1, k2, k3 = jax.random.split(key, 3)
        x = jax.random.normal(k1, (B, CH, IMG[0], IMG[1]), dtype=jnp.float32)
        fan_in = CH * PATCH[0] * PATCH[1]
        std = math.sqrt(2.0 / fan_in)
        W = jax.random.normal(k2, (LEN, CH, PATCH[0], PATCH[1]), dtype=jnp.float32) * std
        b = jax.random.normal(k3, (LEN,), dtype=jnp.float32) * 0.01
        return {'x': x, 'W': W, 'b': b}
    _L0_tok_all = _L0_tok_setup()
    _L0_tok_in = {k: v for k, v in _L0_tok_all.items() if k in ('W', 'b')}
    del _L0_tok_all

    def _L0_attn_setup():
        import jax, jax.numpy as jnp
        import numpy as np
        B, S, D, H = (8, 256, 192, 12)
        HS = D // H
        key = jax.random.key(seed)
        k1, k2, k3 = jax.random.split(key, 3)
        x = jax.random.normal(k1, (B, S, D), dtype=jnp.float32)
        W_attn = jax.random.normal(k2, (D, 3 * H * HS), dtype=jnp.float32) * 0.02
        b_attn = jnp.zeros((3 * H * HS,), dtype=jnp.float32)
        W_proj = jax.random.normal(k3, (H * HS, D), dtype=jnp.float32) * 0.02
        b_proj = jnp.zeros((D,), dtype=jnp.float32)
        return {'x': x, 'W_attn': W_attn, 'b_attn': b_attn, 'W_proj': W_proj, 'b_proj': b_proj}
    _L0_attn_all = _L0_attn_setup()
    _L0_attn_in = {k: v for k, v in _L0_attn_all.items() if k in ('W_attn', 'b_attn', 'W_proj', 'b_proj')}
    del _L0_attn_all

    def _L0_ffn_setup():
        import jax, jax.numpy as jnp
        import numpy as np
        HID = 192
        NQ = 12
        NKV = 3
        HD = 64
        REP = NQ // NKV
        E = 16
        TOPK = 2
        FF = 384
        EPS = 1e-06
        THETA = 10000.0

        def rms_norm(x, w):
            return x / jnp.sqrt(jnp.mean(x * x, axis=-1, keepdims=True) + EPS) * w

        def rope_tables(seq_len):
            inv = 1.0 / THETA ** (jnp.arange(0, HD, 2, dtype=jnp.float32) / HD)
            f = jnp.arange(seq_len, dtype=jnp.float32)[:, None] * inv[None, :]
            return (jnp.cos(f), jnp.sin(f))

        def apply_rope(t, cos, sin):
            B, S, H, _ = t.shape
            tr = t.reshape(B, S, H, HD // 2, 2)
            c = cos[None, :, None, :]
            s = sin[None, :, None, :]
            r0 = tr[..., 0] * c - tr[..., 1] * s
            r1 = tr[..., 0] * s + tr[..., 1] * c
            return jnp.stack([r0, r1], axis=-1).reshape(B, S, H, HD)

        def attention(x, w_qkv, w_out):
            B, S, _ = x.shape
            qkv = x @ w_qkv
            q, k, v = jnp.split(qkv, [NQ * HD, (NQ + NKV) * HD], axis=-1)
            q = q.reshape(B, S, NQ, HD)
            k = k.reshape(B, S, NKV, HD)
            v = v.reshape(B, S, NKV, HD)
            cos, sin = rope_tables(S)
            q = apply_rope(q, cos, sin)
            k = apply_rope(k, cos, sin)
            k = jnp.repeat(k, REP, axis=2)
            v = jnp.repeat(v, REP, axis=2)
            q = q.transpose(0, 2, 1, 3)
            k = k.transpose(0, 2, 1, 3)
            v = v.transpose(0, 2, 1, 3)
            scores = jnp.einsum('bhqd,bhkd->bhqk', q, k) / jnp.sqrt(jnp.float32(HD))
            causal = jnp.tril(jnp.ones((S, S), dtype=bool))
            scores = jnp.where(causal[None, None], scores, jnp.finfo(scores.dtype).min)
            attn = jax.nn.softmax(scores, axis=-1)
            out = jnp.einsum('bhqk,bhkd->bhqd', attn, v)
            out = out.transpose(0, 2, 1, 3).reshape(B, S, NQ * HD)
            return out @ w_out

        def moe_ffn(x2d, w_router, w_gate_up, w_down):
            logits = x2d @ w_router
            probs = jax.nn.softmax(logits, axis=-1)
            vals, idx = jax.lax.top_k(probs, TOPK)
            vals = vals / jnp.sum(vals, axis=-1, keepdims=True)
            combine = jnp.sum(jax.nn.one_hot(idx, E, dtype=x2d.dtype) * vals[..., None], axis=1)
            out = jnp.zeros_like(x2d)
            for e in range(E):
                gu = x2d @ w_gate_up[e]
                gate, up = jnp.split(gu, 2, axis=-1)
                h = jax.nn.silu(gate) * up
                out = out + combine[:, e:e + 1] * (h @ w_down[e])
            return out
        key = jax.random.key(seed)
        ks = jax.random.split(key, 6)
        B, S = (1, 512)
        return {'x': jax.random.normal(ks[0], (B, S, HID), dtype=jnp.float32), 'norm1_w': jnp.ones((HID,), dtype=jnp.float32), 'w_qkv': jax.random.normal(ks[1], (HID, (NQ + 2 * NKV) * HD), dtype=jnp.float32) * 0.02, 'w_out': jax.random.normal(ks[2], (NQ * HD, HID), dtype=jnp.float32) * 0.02, 'norm2_w': jnp.ones((HID,), dtype=jnp.float32), 'w_router': jax.random.normal(ks[3], (HID, E), dtype=jnp.float32) * 0.02, 'w_gate_up': jax.random.normal(ks[4], (E, HID, 2 * FF), dtype=jnp.float32) * 0.02, 'w_down': jax.random.normal(ks[5], (E, FF, HID), dtype=jnp.float32) * 0.02}
    _L0_ffn_all = _L0_ffn_setup()
    _L0_ffn_in = {k: v for k, v in _L0_ffn_all.items() if k in ('norm1_w', 'w_qkv', 'w_out', 'norm2_w', 'w_router', 'w_gate_up', 'w_down')}
    del _L0_ffn_all
    return {'x': x, 'cls_tok': cls_tok, 'L0_tok_W': _L0_tok_in['W'], 'L0_tok_b': _L0_tok_in['b'], 'L0_attn_W_attn': _L0_attn_in['W_attn'], 'L0_attn_b_attn': _L0_attn_in['b_attn'], 'L0_attn_W_proj': _L0_attn_in['W_proj'], 'L0_attn_b_proj': _L0_attn_in['b_proj'], 'L0_ffn_norm1_w': _L0_ffn_in['norm1_w'], 'L0_ffn_w_qkv': _L0_ffn_in['w_qkv'], 'L0_ffn_w_out': _L0_ffn_in['w_out'], 'L0_ffn_norm2_w': _L0_ffn_in['norm2_w'], 'L0_ffn_w_router': _L0_ffn_in['w_router'], 'L0_ffn_w_gate_up': _L0_ffn_in['w_gate_up'], 'L0_ffn_w_down': _L0_ffn_in['w_down']}

def reference(x, cls_tok, L0_tok_W, L0_tok_b, L0_attn_W_attn, L0_attn_b_attn, L0_attn_W_proj, L0_attn_b_proj, L0_ffn_norm1_w, L0_ffn_w_qkv, L0_ffn_w_out, L0_ffn_norm2_w, L0_ffn_w_router, L0_ffn_w_gate_up, L0_ffn_w_down):
    import jax
    import jax.numpy as jnp

    def _L0_tok_ref(x, W, b):
        import math
        import jax, jax.numpy as jnp
        import numpy as np
        IMG = (96, 96)
        PATCH = (16, 16)
        CH = 3
        LEN = 192
        B = 64
        NPATCH = IMG[0] // PATCH[0] * (IMG[1] // PATCH[1])

        def _pos_encoding(n_patch, length, dtype):
            i = jnp.arange(n_patch, dtype=dtype)[:, None]
            j = jnp.arange(length)
            expo = (2 * (j // 2)).astype(dtype) / length
            angle = i / jnp.power(jnp.asarray(10000.0, dtype), expo)
            angle = angle + jnp.where(j % 2 == 1, jnp.asarray(math.pi / 2, dtype), 0.0)
            return jnp.sin(angle)
        y = jax.lax.conv_general_dilated(x, W, window_strides=PATCH, padding='VALID', dimension_numbers=('NCHW', 'OIHW', 'NCHW'))
        y = y + b[None, :, None, None]
        Bn, L, Hp, Wp = y.shape
        y = y.reshape(Bn, L, Hp * Wp).transpose(0, 2, 1)
        pos = _pos_encoding(Hp * Wp, L, y.dtype)
        return y + pos[None, :, :]

    def _L0_attn_ref(x, W_attn, b_attn, W_proj, b_proj):
        import jax, jax.numpy as jnp
        import numpy as np
        B, S, D, H = (8, 256, 192, 12)
        HS = D // H
        b, s, d = x.shape
        qkv = (x @ W_attn + b_attn).reshape(b, s, 3, H, HS)
        q, k, v = (qkv[:, :, 0], qkv[:, :, 1], qkv[:, :, 2])
        scale = jnp.sqrt(jnp.asarray(HS, dtype=x.dtype))
        scores = jnp.einsum('bqhd,bkhd->bhqk', q, k) / scale
        causal = jnp.tril(jnp.ones((s, s), dtype=bool))
        scores = jnp.where(causal, scores, -jnp.inf)
        attn = jax.nn.softmax(scores, axis=-1)
        out = jnp.einsum('bhqk,bkhd->bqhd', attn, v).reshape(b, s, H * HS)
        return out @ W_proj + b_proj

    def _L0_ffn_ref(x, norm1_w, w_qkv, w_out, norm2_w, w_router, w_gate_up, w_down):
        import jax, jax.numpy as jnp
        import numpy as np
        HID = 192
        NQ = 12
        NKV = 3
        HD = 64
        REP = NQ // NKV
        E = 16
        TOPK = 2
        FF = 384
        EPS = 1e-06
        THETA = 10000.0

        def rms_norm(x, w):
            return x / jnp.sqrt(jnp.mean(x * x, axis=-1, keepdims=True) + EPS) * w

        def rope_tables(seq_len):
            inv = 1.0 / THETA ** (jnp.arange(0, HD, 2, dtype=jnp.float32) / HD)
            f = jnp.arange(seq_len, dtype=jnp.float32)[:, None] * inv[None, :]
            return (jnp.cos(f), jnp.sin(f))

        def apply_rope(t, cos, sin):
            B, S, H, _ = t.shape
            tr = t.reshape(B, S, H, HD // 2, 2)
            c = cos[None, :, None, :]
            s = sin[None, :, None, :]
            r0 = tr[..., 0] * c - tr[..., 1] * s
            r1 = tr[..., 0] * s + tr[..., 1] * c
            return jnp.stack([r0, r1], axis=-1).reshape(B, S, H, HD)

        def attention(x, w_qkv, w_out):
            B, S, _ = x.shape
            qkv = x @ w_qkv
            q, k, v = jnp.split(qkv, [NQ * HD, (NQ + NKV) * HD], axis=-1)
            q = q.reshape(B, S, NQ, HD)
            k = k.reshape(B, S, NKV, HD)
            v = v.reshape(B, S, NKV, HD)
            cos, sin = rope_tables(S)
            q = apply_rope(q, cos, sin)
            k = apply_rope(k, cos, sin)
            k = jnp.repeat(k, REP, axis=2)
            v = jnp.repeat(v, REP, axis=2)
            q = q.transpose(0, 2, 1, 3)
            k = k.transpose(0, 2, 1, 3)
            v = v.transpose(0, 2, 1, 3)
            scores = jnp.einsum('bhqd,bhkd->bhqk', q, k) / jnp.sqrt(jnp.float32(HD))
            causal = jnp.tril(jnp.ones((S, S), dtype=bool))
            scores = jnp.where(causal[None, None], scores, jnp.finfo(scores.dtype).min)
            attn = jax.nn.softmax(scores, axis=-1)
            out = jnp.einsum('bhqk,bhkd->bhqd', attn, v)
            out = out.transpose(0, 2, 1, 3).reshape(B, S, NQ * HD)
            return out @ w_out

        def moe_ffn(x2d, w_router, w_gate_up, w_down):
            logits = x2d @ w_router
            probs = jax.nn.softmax(logits, axis=-1)
            vals, idx = jax.lax.top_k(probs, TOPK)
            vals = vals / jnp.sum(vals, axis=-1, keepdims=True)
            combine = jnp.sum(jax.nn.one_hot(idx, E, dtype=x2d.dtype) * vals[..., None], axis=1)
            out = jnp.zeros_like(x2d)
            for e in range(E):
                gu = x2d @ w_gate_up[e]
                gate, up = jnp.split(gu, 2, axis=-1)
                h = jax.nn.silu(gate) * up
                out = out + combine[:, e:e + 1] * (h @ w_down[e])
            return out
        B, S, _ = x.shape
        h = x + attention(rms_norm(x, norm1_w), w_qkv, w_out)
        moe_in = rms_norm(h, norm2_w).reshape(B * S, HID)
        out = h + moe_ffn(moe_in, w_router, w_gate_up, w_down).reshape(B, S, HID)
        return out
    h = _L0_tok_ref(x, L0_tok_W, L0_tok_b)
    h = jnp.concatenate([jnp.broadcast_to(cls_tok, (h.shape[0], 1, h.shape[2])), h], axis=1)
    h = h + _L0_attn_ref(_layernorm(h, axis=-1), L0_attn_W_attn, L0_attn_b_attn, L0_attn_W_proj, L0_attn_b_proj)
    h = h + _L0_ffn_ref(_layernorm(h, axis=-1), L0_ffn_norm1_w, L0_ffn_w_qkv, L0_ffn_w_out, L0_ffn_norm2_w, L0_ffn_w_router, L0_ffn_w_gate_up, L0_ffn_w_down)
    return h

_drawn_inputs = setup_inputs


def setup_inputs(seed=0):
    import zlib

    import numpy as np

    out = dict(_drawn_inputs(seed))
    spreads = {'L0_attn_b_attn': (0.0, 0.29),
     'L0_attn_b_proj': (0.0, 0.1),
     'L0_ffn_norm1_w': (1.0, 0.6),
     'L0_ffn_norm2_w': (1.0, 0.6)}
    factors = {'L0_tok_b': 8.0, 'L0_ffn_w_router': 8.0, 'L0_ffn_w_gate_up': 8.0, 'L0_ffn_w_down': 8.0}
    for name, (base, spread) in spreads.items():
        noise = np.random.default_rng([zlib.crc32(name.encode()), seed]).standard_normal(out[name].shape)
        drawn = base * np.exp(spread * noise) if base else spread * noise
        out[name] = jnp.asarray(drawn.astype(out[name].dtype))
    for name, factor in factors.items():
        out[name] = (out[name] * factor).astype(out[name].dtype)
    return out
```

```python
from contextlib import ExitStack

import numpy as np

import concourse.bass as bass
from concourse import mybir

F32 = mybir.dt.float32
I32 = mybir.dt.int32
U32 = mybir.dt.uint32
ALU = mybir.AluOpType
ACT = mybir.ActivationFunctionType
AX = mybir.AxisListType

IMAGES, CH, SIDE, PATCH = 32, 3, 84, 16
GRID = SIDE // PATCH
S = GRID * GRID + 1
D = 192
C = 96
PK = CH * PATCH * PATCH // 128
IPT = 4
TILES = IMAGES // IPT
HT = 4
HALVES = TILES // HT
HI = HT * IPT
CT = HI * S
H1, HD1 = 12, 16
HC = C // HD1
G, R, HD2 = 3, 4, 64
J = HD2 // 2
E, FF, TOPK = 16, 384, 2
TOKENS = IMAGES * S
SLOT_TILES = (TOPK * TOKENS + E * 127) // 128
SLOTS = SLOT_TILES * 128
PADS = (32 - S) * IPT * TILES
XS_TILES = SLOT_TILES + (TOPK * PADS + 127) // 128
MOST = (TOKENS + 127) // 128
LN_EPS, RMS_EPS, MASKED = 1e-5, 1e-6, -1e30

_C = {}
_n = 0
for _name, _w in (("pos", D), ("mask1", S), ("mask2", S), ("head_of_row", HC), ("head_of_key", 4),
                  ("group_of_row", G), ("cos", S), ("sin", S), ("eye", 128), ("before", 128), ("ones", 128),
                  ("unrouted", 1), ("trash1", TILES), ("trash2", TILES), ("steps", MOST), ("less", E * E),
                  ("iota", E), ("slot_iota", SLOT_TILES), ("neghalf", HT), ("who", 128)):
    _C[_name] = (_n, _w)
    _n += _w
NCONST = _n

_F = {}
_n = 0
for _name, _w in (("wpatch", PK * D), ("wqkv1", 2 * 3 * D), ("wproj", 2 * D), ("wqk2", 2 * 5 * 2 * C),
                  ("wv2", 2 * D), ("wout", 6 * D), ("wr", 2 * E), ("w2row", D), ("small", 16), ("rows", 2 * D)):
    _F[_name] = (_n, _w)
    _n += _w
NFRONT = _n
GU0 = E * 3 * D


def build_tower(nc, xp, fw, cst, wgu, wdn, xs, ys, out):
    ctx = ExitStack()
    with ctx:
        def sb(name, shape, dt=F32):
            return ctx.enter_context(nc.sbuf_tensor(name, shape, dt))

        def sem(name):
            return ctx.enter_context(nc.semaphore(name))

        big = sb("experts", [128, E * (3 * D + 4 * FF)])
        front = sb("front", [128, NFRONT])
        ct = sb("constants", [128, NCONST])
        xt = sb("patches", [128, 2, PK * 128])
        p2 = sb("probs2", [104, HT, G, IPT, 32])
        ot2 = sb("attended2", [128, 6, HT * 128])
        hsum = sb("residual", [128, TILES, D])
        mall = sb("moe_in", [128, TILES, D])
        lg = sb("logits", [128, TILES * E])
        mv = sb("moments", [128, 4, HT])
        mean = sb("mean", [128, HT])
        st6 = sb("stats", [128, HT, 6])
        ve = sb("variance", [128, HT])
        rs = sb("rstd", [128, HT])
        ms = sb("meansq", [128, HT])
        mx = sb("rowmax", [128, 48])
        sm = sb("rowsum", [128, 48])
        rc = sb("rowrecip", [128, 48])
        ps = [ctx.enter_context(nc.psum_tensor(f"bank{i}", [128, 512], F32)) for i in range(8)]

        def const(name, rows=128):
            a, w = _C[name]
            return ct[0:rows, a:a + w]

        def fview(name, rows=128):
            a, w = _F[name]
            return front[0:rows, a:a + w]

        eye = const("eye")
        wpatch = fview("wpatch").rearrange("p (k n) -> p k n", k=PK)
        wqkv1 = fview("wqkv1", C).rearrange("p (c n) -> p c n", c=2)
        wproj = fview("wproj", C).rearrange("p (c n) -> p c n", c=2)
        wqk2 = fview("wqk2", C).rearrange("p (c s e n) -> p c s e n", c=2, s=5, e=2)
        wv2 = fview("wv2", C).rearrange("p (c n) -> p c n", c=2)
        wout = fview("wout").rearrange("p (k n) -> p k n", k=6)
        wr = fview("wr", C).rearrange("p (c n) -> p c n", c=2)
        w2row = fview("w2row")
        small = fview("small", C)
        bcls = front[0:2, _F["rows"][0]:_F["rows"][0] + D]
        bproj = front[0:1, _F["rows"][0] + D:_F["rows"][0] + 2 * D]

        arena0 = (E // 2) * 3 * D
        at = [arena0]

        def carve(n, rows=128):
            a = at[0]
            at[0] += n
            assert at[0] <= GU0 + (E // 2) * 4 * FF
            return big[0:rows, a:a + n]

        z = carve(HT * D).rearrange("p (t n) -> p t n", t=HT)
        fT = carve(2 * HT * 128, C).rearrange("p (c n) -> p c n", c=2)
        sc = carve(48 * S)
        both = at[0]
        h = carve(HT * D).rearrange("p (t n) -> p t n", t=HT)
        q1 = carve(2 * HT * 128, C).rearrange("p (c n) -> p c n", c=2)
        k1 = carve(2 * CT, C).rearrange("p (c i k) -> p c i k", c=2, k=S)
        kbd = carve(2 * HI * HC * S, C).rearrange("p (c i h k) -> p c i h k", c=2, i=HI, h=HC)
        v1 = carve(HT * D).rearrange("p (t n) -> p t n", t=HT)
        vbd = carve(HI * D, 104).rearrange("p (t i n) -> p t i n", t=HT, i=IPT)
        pT = carve(G * HT * 128, 104).rearrange("p (g n) -> p g n", g=G)
        o1 = carve(HT * D).rearrange("p (t n) -> p t n", t=HT)
        at[0] = both + HT * D
        u = carve(HT * D).rearrange("p (t n) -> p t n", t=HT)
        qr = carve(2 * R * CT, C).rearrange("p (e i r q) -> p e i r q", e=2, i=HI, r=R)
        tmp = carve(2 * 4 * CT, C).rearrange("p (b m i q) -> p b m i q", b=2, m=4, q=S)
        kr = carve(2 * CT, C).rearrange("p (e i k) -> p e i k", e=2, k=S)
        kbd2 = carve(2 * HI * G * S, C).rearrange("p (e i g k) -> p e i g k", e=2, i=HI, g=G)
        v2 = carve(HT * D).rearrange("p (t n) -> p t n", t=HT)
        pT2 = carve(G * HT * 104).rearrange("p (g t n) -> p g t n", g=G, t=HT)

        at = [0]

        def over(n, rows=128):
            a = at[0]
            at[0] += n
            assert at[0] <= NFRONT
            return front[0:rows, a:a + n]

        xin = over(2 * D).rearrange("p (b n) -> p b n", b=2)
        xT = over(2 * 2 * 128, C).rearrange("p (b n) -> p b n", b=2)
        sg = over(2 * FF).rearrange("p (b n) -> p b n", b=2)
        hh = over(2 * FF).rearrange("p (b n) -> p b n", b=2)
        hT = over(2 * FF).rearrange("p (b n) -> p b n", b=2)
        yo = over(2 * D).rearrange("p (b n) -> p b n", b=2)
        y1 = ot2[:, 0:3, :].rearrange("p a n -> p (a n)").rearrange("p (t n) -> p t n", t=TILES)
        y2 = ot2[:, 3:6, :].rearrange("p a n -> p (a n)").rearrange("p (t n) -> p t n", t=TILES)

        top = sb("top", [128, TILES, 8])
        topi = sb("topi", [128, TILES, 8], U32)
        topf = sb("topf", [128, TILES, 2])
        gap = sb("gap", [128, TILES])
        eg = sb("expgap", [128, TILES])
        den = sb("den", [128, TILES])
        g1 = sb("gate1", [128, TILES])
        g2 = sb("gate2", [128, TILES])
        rt = xt[:, :, :].rearrange("p b n -> p (b n)")

        def table(i, n, rows=128):
            return rt[0:rows, i:i + n]

        W8 = TILES * E
        oh = [table(0, W8).rearrange("p (t e) -> p t e", e=E), table(W8, W8).rearrange("p (t e) -> p t e", e=E)]
        ohs = table(2 * W8, W8).rearrange("p (t e) -> p t e", e=E)
        cum = table(3 * W8, W8).rearrange("p (t e) -> p t e", e=E)
        rank = table(4 * W8, W8).rearrange("p (t e) -> p t e", e=E)
        pick = [table(5 * W8, W8).rearrange("p (t e) -> p t e", e=E),
                table(6 * W8, W8).rearrange("p (t e) -> p t e", e=E)]
        over_step = sb("over_step", [128, E, MOST])
        lessed = sb("lessed", [128, E, E])
        cnt = sb("count", [128, E])
        etl = sb("expert_tiles", [128, E])
        est = sb("expert_start", [128, E])
        een = sb("expert_end", [128, E])
        le = sb("ended", [1, SLOT_TILES, E])
        ef = sb("expert_f", [1, 2, SLOT_TILES])
        ei = sb("expert_of_slot_tile", [1, 2, SLOT_TILES], I32)
        slot = [sb("slot1", [128, TILES]), sb("slot2", [128, TILES])]
        sidx = [sb("scatter1", [128, TILES], I32), sb("scatter2", [128, TILES], I32)]
        gidx = [sb("gather1", [128, TILES], I32), sb("gather2", [128, TILES], I32)]
        zero = sb("zeros", [128, D])

        consts_in, front_in, late_in, early_in = sem("consts_in"), sem("front_in"), sem("late_in"), sem("early_in")
        x_in = [sem("x_in0"), sem("x_in1")]
        pads_set, zero_set, zeros_out = sem("pads_set"), sem("zero_set"), sem("zeros_out")
        patch_done = sem("patch_done")
        h_ready = sem("h_ready")
        st_ready = [sem("st_ready_a"), sem("st_ready_b")]
        mv_ready = [sem("mv_ready_a"), sem("mv_ready_b")]
        ve_ready = [sem("ve_ready_a"), sem("ve_ready_b"), sem("ve_ready_c"), sem("ve_ready_d")]
        rs_ready = [sem("rs_ready_a"), sem("rs_ready_b"), sem("rs_ready_c"), sem("rs_ready_d")]
        z_ready = [sem("z_ready_a"), sem("z_ready_b")]
        zt_done, zt_ready = sem("zt_done"), sem("zt_ready")
        qk_done, q_ready, k_ready = sem("qk_done"), sem("q_ready"), sem("k_ready")
        v_done, v1_ready, vrep_in, vbd_ready = sem("v_done"), sem("v1_ready"), sem("vrep_in"), sem("vbd_ready")
        kbd_ready = sem("kbd_ready")
        s_done = [sem("s_done_a"), sem("s_done_b")]
        sm_ready = [sem("sm_ready_a"), sem("sm_ready_b")]
        max_ready = [sem("max_ready_a"), sem("max_ready_b")]
        sub_ready = [sem("sub_ready_a"), sem("sub_ready_b")]
        exp_ready = [sem("exp_ready_a"), sem("exp_ready_b")]
        sum_ready = [sem("sum_ready_a"), sem("sum_ready_b")]
        rc_ready = [sem("rc_ready_a"), sem("rc_ready_b")]
        pt_done, pt_ready = sem("pt_done"), sem("pt_ready")
        o_done, o_ready = sem("o_done"), sem("o_ready")
        ot_done, ot_ready = sem("ot_done"), sem("ot_ready")
        proj_done, h1_ready = sem("proj_done"), sem("h1_ready")
        sq_ready = [sem("sq_ready_a"), sem("sq_ready_b")]
        u_ready = [sem("u_ready_a"), sem("u_ready_b")]
        ut_done, ut_ready = sem("ut_done"), sem("ut_ready")
        v2_done, v2_ready = sem("v2_done"), sem("v2_ready")
        eo_done = sem("eo_done")
        rope_mul, rope_add = sem("rope_mul"), sem("rope_add")
        kbd2_ready = sem("kbd2_ready")
        p2_ready, pt2_done, pt2_ready = sem("p2_ready"), sem("pt2_done"), sem("pt2_ready")
        pv2_done, ot2_a, ot2_d = sem("pv2_done"), sem("ot2_a"), sem("ot2_d")
        wo_done, x2_ready = sem("wo_done"), sem("x2_ready")
        hsum_ready, mcopy_ready = sem("hsum_ready"), sem("mcopy_ready")
        mt_done, mt_ready = sem("mt_done"), sem("mt_ready")
        lg_done, lg_ready = sem("lg_done"), sem("lg_ready")
        r_dve, gap_ready, eg_ready = sem("r_dve"), sem("gap_ready"), sem("eg_ready")
        ohs_ready, ranks_done = sem("ohs_ready"), sem("ranks_done")
        idx_ready, eid_ready, scattered = sem("idx_ready"), sem("eid_ready"), sem("scattered")
        xs_in = [sem("xs_in0"), sem("xs_in1")]
        xtr_done, xT_ready = sem("xtr_done"), sem("xT_ready")
        gate_done, up_done, sg_ready, hh_ready = sem("gate_done"), sem("up_done"), sem("sg_ready"), sem("hh_ready")
        htr_done, hT_ready, y_done, y_ready = sem("htr_done"), sem("hT_ready"), sem("y_done"), sem("y_ready")
        ys_out = [sem("ys_out0"), sem("ys_out1")]
        gathered = [sem(f"gathered{t}") for t in range(TILES)]
        mix_ready, out_done = sem("mix_ready"), sem("out_done")

        def attended(g, i, odd):
            to = ot2[64 * odd:64 * odd + 64, 2 * g:2 * g + 2, :].rearrange("p r (t i q) -> p r t i q", t=HT, i=IPT)
            of = ps[4 * (g % 2) + i][0:64, 0:HT * 104].rearrange("p (t r o q) -> p r t o q", t=HT, r=2, o=2)
            return to[:, :, :, i, 0:S], of[:, :, :, odd, :]

        block = ctx.enter_context(nc.Block())

        @block.sync
        def _(sp):
            def load_x(n):
                if n >= 2:
                    sp.wait_ge(patch_done, n - 1)
                sp.dma_start(xt[:, n % 2, :], xp[n]).then_inc(x_in[n % 2], 16)

            load_x(0)
            sp.dma_start(front[:, :], fw).then_inc(front_in, 16)
            load_x(1)
            sp.dma_start(big[:, 0:arena0], wdn[:, 0:arena0]).then_inc(early_in, 16)
            lo = (E // 2) * 4 * FF
            for part in range(4):
                a, w = lo + part * (lo // 4), lo // 4
                sp.dma_start(big[0:C, GU0 + a:GU0 + a + w], wgu[:, a:a + w]).then_inc(early_in, 16)
            sp.wait_ge(zero_set, 1)
            sp.dma_start(xs.rearrange("(a p) n -> p a n", p=128),
                         zero[:, :].unsqueeze(1).to_broadcast([128, XS_TILES, D])).then_inc(zeros_out, 16)
            for hf in range(HALVES):
                for n in range(HT * hf, HT * hf + HT):
                    if n >= 2:
                        load_x(n)
                sp.wait_ge(v1_ready, 2 * hf + 2)
                for i in range(IPT):
                    for r in range(4):
                        sp.dma_start(vbd[S * r:S * r + S, :, i, :], v1[32 * i:32 * i + S, :, :]).then_inc(vrep_in, 16)
            sp.wait_ge(lg_done, HALVES)
            sp.wait_ge(hsum_ready, HALVES)
            sp.wait_ge(mcopy_ready, HALVES)
            sp.dma_start(big[:, arena0:GU0], wdn[:, arena0:GU0]).then_inc(late_in, 16)
            for part in range(4):
                a, w = part * (lo // 4), lo // 4
                sp.dma_start(big[0:C, GU0 + a:GU0 + a + w], wgu[:, a:a + w]).then_inc(late_in, 16)
            sp.wait_ge(scattered, 16 * TOPK * TILES)
            sp.dma_start(xin[:, 0, :], xs[0:128, :]).then_inc(xs_in[0], 16)

            def step(j, b):
                sp.wait_ge(xtr_done, j)
                sp.dma_start(xin[:, 1 - b, :], xs[bass.ds(j * 128 + 128, 128), :]).then_inc(xs_in[1 - b], 16)
                sp.wait_ge(y_ready, j)
                sp.dma_start(ys[bass.ds(j * 128 - 128, 128), :], yo[:, 1 - b, :]).then_inc(ys_out[1 - b], 16)

            sp.dma_start(xin[:, 1, :], xs[128:256, :]).then_inc(xs_in[1], 16)
            with sp.Fori(0, (SLOT_TILES - 2) // 2) as jj:
                step(jj * 2 + 1, 1)
                step(jj * 2 + 2, 0)
            step(SLOT_TILES - 1, 1)
            sp.wait_ge(y_ready, SLOT_TILES)
            sp.dma_start(ys[SLOTS - 128:SLOTS, :], yo[:, 1, :]).then_inc(ys_out[1], 16)
            sp.wait_ge(mix_ready, TOPK * TILES)
            dst = out.rearrange("(t i) q n -> i q t n", i=IPT)
            for i in range(IPT):
                sp.dma_start(dst[i], hsum[32 * i:32 * i + S, :, :]).then_inc(out_done, 16)
            sp.wait_ge(out_done, 16 * IPT)

        @block.gpsimd
        def _(pool):
            pool.memset(zero[:, :], 0.0).then_inc(zero_set, 1)
            pool.memset(p2[:, :, :, :, :], 0.0).then_inc(pads_set, 1)
            pool.memset(ot2[:, :, :], 0.0).then_inc(pads_set, 1)
            pool.wait_ge(consts_in, 16)

            def rstd(hf, n):
                pool.wait_ge(ve_ready[n], hf + 1)
                pool.tensor_tensor(rs[:, :], ve[:, :], const("neghalf"), ALU.pow).then_inc(rs_ready[n], 1)

            with pool.Fori(0, HALVES) as hf:
                rstd(hf, 0)
                pool.wait_ge(vrep_in, hf * (16 * 16) + 16 * 16)
                vv = vbd.rearrange("p t i (g r d) -> p (t i g) r d", g=G, r=4)
                pool.tensor_tensor(vv, vv, const("head_of_key", 104).unsqueeze(1).unsqueeze(3)
                                   .to_broadcast([104, HI * G, 4, HD1]), ALU.mult).then_inc(vbd_ready, 1)
                rstd(hf, 1)
                rstd(hf, 2)
                for n in range(5):
                    pool.wait_ge(rope_mul, hf * 5 + (n + 1))
                    t4 = tmp[:, n % 2]
                    to = kr if n == 0 else qr[:, :, :, n - 1, :]
                    pool.tensor_tensor(to[:, 0], t4[:, 0], t4[:, 1], ALU.subtract)
                    pool.tensor_tensor(to[:, 1], t4[:, 2], t4[:, 3], ALU.add).then_inc(rope_add, 1)
                    if n == 0:
                        pool.wait_ge(rope_add, hf * 5 + 1)
                        for e in range(2):
                            last = pool.tensor_tensor(
                                kbd2[:, e], kr[:, e].unsqueeze(2).to_broadcast([C, HI, G, S]),
                                const("group_of_row", C).unsqueeze(1).unsqueeze(3).to_broadcast([C, HI, G, S]),
                                ALU.mult)
                        last.then_inc(kbd2_ready, 1)
                pool.wait_ge(x2_ready, hf * 2 + 2)
                pool.tensor_tensor(hsum[:, bass.ds(hf * HT, HT), :], h, z, ALU.add).then_inc(hsum_ready, 1)
                rstd(hf, 3)
                pool.wait_ge(u_ready[1], hf * HT + HT)
                pool.tensor_copy(mall[:, bass.ds(hf * HT, HT), :], u).then_inc(mcopy_ready, 1)
            pool.wait_ge(zeros_out, 16)
            pool.wait_ge(mcopy_ready, HALVES)
            for k in range(TOPK):
                pool.wait_ge(idx_ready, 2 * k + 1)
                for t in range(TILES):
                    pool.indirect_dma_start(xs, bass.IndirectOffsetOnAxis(sidx[k][:, t:t + 1], 0),
                                            mall[:, t, :], None).then_inc(scattered, 16)
            pool.wait_ge(ys_out[0], 16 * (SLOT_TILES // 2))
            pool.wait_ge(ys_out[1], 16 * (SLOT_TILES // 2))
            pool.wait_ge(idx_ready, 4)
            for t in range(TILES):
                for k, y in enumerate((y1, y2)):
                    pool.indirect_dma_start(y[:, t, :], None, ys,
                                            bass.IndirectOffsetOnAxis(gidx[k][:, t:t + 1], 0)).then_inc(gathered[t], 16)

        @block.scalar
        def _(act):
            act.dma_start(ct[:, :], cst).then_inc(consts_in, 16)
            act.wait_ge(front_in, 16)
            with act.Fori(0, HALVES) as hf:
                act.wait_ge(zt_done, hf * HT + HT)
                for c in range(2):
                    act.activation(fT[:, c, :], ps[2 + c][0:C, :], ACT.Copy).then_inc(zt_ready, 1)
                for c in range(2):
                    act.wait_ge(qk_done, hf * 4 + (c + 1))
                    act.activation(k1[:, c].rearrange("p i k -> p (i k)"), ps[6 + c][0:C, 0:CT], ACT.Identity,
                                   bias=small[:, 2 + c:3 + c]).then_inc(k_ready, 1)
                for c in range(2):
                    act.wait_ge(qk_done, hf * 4 + (c + 3))
                    act.activation(q1[:, c, :], ps[4 + c][0:C, :], ACT.Identity,
                                   bias=small[:, c:c + 1]).then_inc(q_ready, 1)
                act.wait_ge(sub_ready[0], hf + 1)
                act.activation(sc, sc, ACT.Exp, scale=HD1 ** -0.5).then_inc(exp_ready[0], 1)
                for g in range(G):
                    act.wait_ge(pt_done, hf * G + (g + 1))
                    act.activation(pT[:, g, :], ps[(6, 7, 0)[g]][0:104, :], ACT.Copy).then_inc(pt_ready, 1)
                act.wait_ge(ot_done, hf + 1)
                for c in range(2):
                    act.activation(fT[:, c, :], ps[3 + c][0:C, :], ACT.Identity,
                                   bias=small[:, 4 + c:5 + c]).then_inc(ot_ready, 1)
                for t in range(HT):
                    act.wait_ge(z_ready[1], hf * HT + (t + 1))
                    act.activation(u[:, t, :], z[:, t, :], ACT.Square, accum_out=ms[:, t:t + 1]).then_inc(sq_ready[0], 1)
                act.wait_ge(ut_done, hf + 1)
                for c in range(2):
                    act.activation(fT[:, c, :], ps[(7, 0)[c]][0:C, :], ACT.Identity,
                                   scale=small[:, 6 + c:7 + c]).then_inc(ut_ready, 1)
                for p in range(2):
                    act.wait_ge(v2_done, hf * 2 + (p + 1))
                    act.activation(v2[:, 2 * p:2 * p + 2, :].rearrange("p t n -> p (t n)"), ps[1 + p][:, 0:2 * D],
                                   ACT.Copy).then_inc(v2_ready, 1)
                act.wait_ge(sub_ready[1], hf + 1)
                act.activation(sc[0:104, :], sc[0:104, :], ACT.Exp, scale=HD2 ** -0.5).then_inc(exp_ready[1], 1)
                for g in range(G):
                    act.wait_ge(pt2_done, hf * G + (g + 1))
                    act.activation(pT2[:, g], ps[5 + g][:, :].rearrange("p (t n) -> p t n", t=HT)[:, :, 0:104],
                                   ACT.Copy).then_inc(pt2_ready, 1)
                for g in range(G):
                    act.wait_ge(pv2_done, hf * G + (g + 1))
                    for i in range(0, IPT, 2):
                        for odd in range(2):
                            last = act.activation(*attended(g, i, odd), ACT.Copy)
                        last.then_inc(ot2_a, 1)
                for t in range(HT):
                    act.wait_ge(x2_ready, hf * 2 + (t // 2 + 1))
                    act.activation(u[:, t, :], z[:, t, :], ACT.Square, accum_out=ms[:, t:t + 1]).then_inc(sq_ready[1], 1)
                act.wait_ge(mt_done, hf + 1)
                for c in range(2):
                    act.activation(fT[:, c, :], ps[6 + c][0:C, :], ACT.Copy).then_inc(mt_ready, 1)
            act.wait_ge(gap_ready, 1)
            act.activation(eg[:, :], gap[:, :], ACT.Exp).then_inc(eg_ready, 1)

            def copy_x(j, b):
                act.wait_ge(xtr_done, j + 1)
                act.activation(xT[:, b, :], ps[6][0:C, 0:256], ACT.Copy).then_inc(xT_ready, 1)

            def silu(j, b):
                act.wait_ge(gate_done, j + 1)
                act.activation(sg[:, b, :], ps[b][:, 0:FF], ACT.Silu).then_inc(sg_ready, 1)

            def copy_h(j, b):
                act.wait_ge(htr_done, j + 1)
                act.activation(hT[:, b, :], ps[4][:, 0:FF], ACT.Copy).then_inc(hT_ready, 1)

            copy_x(0, 0)
            silu(0, 0)
            copy_x(1, 1)

            def step(j, b):
                copy_h(j - 1, 1 - b)
                silu(j, b)
                copy_x(j + 1, 1 - b)

            with act.Fori(0, (SLOT_TILES - 2) // 2) as jj:
                step(jj * 2 + 1, 1)
                step(jj * 2 + 2, 0)
            step(SLOT_TILES - 1, 1)
            copy_h(SLOT_TILES - 1, 1)

        @block.vector
        def _(dve):
            def stats(hf, n, ready):
                for t in range(HT):
                    ready(t)
                    dve.bn_stats(st6[:, t, :], h[:, t, :]).then_inc(st_ready[n], 1)
                dve.wait_ge(st_ready[n], hf * HT + HT)
                dve.tensor_tensor(mv[:, 0, :], st6[:, :, 1], st6[:, :, 4], ALU.add)
                dve.tensor_tensor(mv[:, 1, :], st6[:, :, 1], st6[:, :, 4], ALU.subtract)
                dve.tensor_tensor(mv[:, 2, :], st6[:, :, 2], st6[:, :, 5], ALU.add).then_inc(mv_ready[n], 1)
                dve.wait_ge(mv_ready[n], hf * 2 + 1)
                dve.tensor_scalar(mean[:, :], mv[:, 0, :], 0.5, None, ALU.mult)
                dve.tensor_scalar(mv[:, 2, :], mv[:, 2, :], 1.0 / D, LN_EPS, ALU.mult, ALU.add)
                dve.scalar_tensor_tensor(mv[:, 3, :], mv[:, 1, :], 0.25, mv[:, 1, :],
                                         ALU.mult, ALU.mult).then_inc(mv_ready[n], 1)
                dve.wait_ge(mv_ready[n], hf * 2 + 2)
                dve.tensor_tensor(ve[:, :], mv[:, 2, :], mv[:, 3, :], ALU.add).then_inc(ve_ready[n], 1)

            def meansq(hf, n):
                dve.wait_ge(sq_ready[n - 2], hf * HT + HT)
                dve.tensor_scalar(ve[:, :], ms[:, :], 1.0 / D, RMS_EPS, ALU.mult, ALU.add).then_inc(ve_ready[n], 1)
                dve.wait_ge(rs_ready[n], hf + 1)

            def normalise(hf, n):
                dve.wait_ge(rs_ready[n], hf + 1)
                for t in range(HT):
                    dve.tensor_scalar(z[:, t, :], h[:, t, :], mean[:, t:t + 1], rs[:, t:t + 1],
                                      ALU.subtract, ALU.mult).then_inc(z_ready[n], 1)

            def masked_max(hf, n, rows):
                mask = const("mask1" if n == 0 else "mask2", rows)
                for t in range(HT):
                    dve.wait_ge(s_done[n], hf * HT + (t + 1))
                    bank = ps[(2 if n == 0 else 1) + t]
                    dve.tensor_tensor(sc[0:rows, t * 12 * S:(t + 1) * 12 * S].rearrange("p (h k) -> p h k", h=12),
                                      bank[0:rows, 0:12 * S].rearrange("p (h k) -> p h k", h=12),
                                      mask.unsqueeze(1).to_broadcast([rows, 12, S]), ALU.add).then_inc(sm_ready[n], 1)
                s3 = sc[0:rows, :].rearrange("p (h k) -> p h k", k=S)
                dve.wait_ge(sm_ready[n], hf * HT + HT)
                dve.tensor_reduce(mx[0:rows, :], s3, AX.X, ALU.max).then_inc(max_ready[n], 1)
                dve.wait_ge(max_ready[n], hf + 1)
                dve.tensor_tensor(s3, s3, mx[0:rows, :].unsqueeze(2).to_broadcast([rows, 48, S]),
                                  ALU.subtract).then_inc(sub_ready[n], 1)

            def row_sums(hf, n, rows):
                s3 = sc[0:rows, :].rearrange("p (h k) -> p h k", k=S)
                dve.wait_ge(exp_ready[n], hf + 1)
                dve.tensor_reduce(sm[0:rows, :], s3, AX.X, ALU.add).then_inc(sum_ready[n], 1)
                dve.wait_ge(sum_ready[n], hf + 1)
                dve.reciprocal(rc[0:rows, :], sm[0:rows, :]).then_inc(rc_ready[n], 1)
                dve.wait_ge(rc_ready[n], hf + 1)

            dve.wait_ge(consts_in, 16)
            with dve.Fori(0, HALVES) as hf:
                for p in range(2):
                    dve.wait_ge(patch_done, hf * HT + (2 * p + 2))
                    dve.tensor_tensor(h[:, 2 * p:2 * p + 2, :], ps[p][:, 0:2 * D].rearrange("p (t n) -> p t n", t=2),
                                      const("pos").unsqueeze(1).to_broadcast([128, 2, D]), ALU.add).then_inc(h_ready, 1)
                stats(hf, 0, lambda t: dve.wait_ge(h_ready, hf * 2 + (t // 2 + 1)))
                normalise(hf, 0)
                for p in range(2):
                    dve.wait_ge(v_done, hf * 2 + (p + 1))
                    dve.tensor_copy(v1[:, 2 * p:2 * p + 2, :].rearrange("p t n -> p (t n)"),
                                    ps[p][:, 0:2 * D]).then_inc(v1_ready, 1)
                for c in range(2):
                    dve.wait_ge(k_ready, hf * 2 + (c + 1))
                    dve.tensor_tensor(kbd[:, c], k1[:, c].unsqueeze(2).to_broadcast([C, HI, HC, S]),
                                      const("head_of_row", C).unsqueeze(1).unsqueeze(3).to_broadcast([C, HI, HC, S]),
                                      ALU.mult).then_inc(kbd_ready, 1)
                masked_max(hf, 0, 128)
                row_sums(hf, 0, 128)
                for p in range(2):
                    dve.wait_ge(o_done, hf * 2 + (p + 1))
                    dve.tensor_tensor(o1[:, 2 * p:2 * p + 2, :].rearrange("p t (h d) -> p (t h) d", h=H1),
                                      ps[1 + p][:, 0:2 * D].rearrange("p (h d) -> p h d", d=HD1),
                                      rc[:, 24 * p:24 * p + 24].unsqueeze(2).to_broadcast([128, 24, HD1]),
                                      ALU.mult).then_inc(o_ready, 1)
                for p in range(2):
                    dve.wait_ge(proj_done, hf * 2 + (p + 1))
                    hp = h[:, 2 * p:2 * p + 2, :].rearrange("p t n -> p (t n)")
                    dve.tensor_tensor(hp, ps[5 + p][:, 0:2 * D], hp, ALU.add).then_inc(h1_ready, 1)
                stats(hf, 1, lambda t: dve.wait_ge(h1_ready, hf * 2 + (t // 2 + 1)))
                normalise(hf, 1)
                meansq(hf, 2)
                for t in range(HT):
                    dve.tensor_scalar(u[:, t, :], z[:, t, :], rs[:, t:t + 1], None, ALU.mult).then_inc(u_ready[0], 1)
                for n in range(5):
                    dve.wait_ge(eo_done, hf * 5 + (n + 1))
                    if n >= 2:
                        dve.wait_ge(rope_add, hf * 5 + (n - 1))
                    b0, b1 = ((3, 4), (5, 6), (7, 0))[n % 3]
                    for m, (b, w) in enumerate(((b0, "cos"), (b1, "sin"), (b0, "sin"), (b1, "cos"))):
                        last = dve.tensor_tensor(tmp[:, n % 2, m], ps[b][0:C, 0:CT].rearrange("p (i q) -> p i q", i=HI),
                                                 const(w, C).unsqueeze(1).to_broadcast([C, HI, S]), ALU.mult)
                    last.then_inc(rope_mul, 1)
                masked_max(hf, 1, 104)
                row_sums(hf, 1, 104)
                if True:
                    dve.wait_ge(pads_set, 2)
                    for t in range(HT):
                        dve.tensor_tensor(
                            p2[:, t, :, :, 0:S],
                            sc[0:104, t * 12 * S:(t + 1) * 12 * S].rearrange("p (i g k) -> p g i k", i=IPT, g=G),
                            rc[0:104, 12 * t:12 * t + 12].rearrange("p (i g) -> p g i", i=IPT).unsqueeze(3)
                            .to_broadcast([104, G, IPT, S]), ALU.mult).then_inc(p2_ready, 1)
                for g in range(G):
                    dve.wait_ge(pv2_done, hf * G + (g + 1))
                    for i in range(1, IPT, 2):
                        for odd in range(2):
                            last = dve.tensor_copy(*attended(g, i, odd))
                        last.then_inc(ot2_d, 1)
                for p in range(2):
                    dve.wait_ge(wo_done, hf * 2 + (p + 1))
                    zp = z[:, 2 * p:2 * p + 2, :].rearrange("p t n -> p (t n)")
                    dve.tensor_tensor(zp, ps[4 + p][:, 0:2 * D], zp, ALU.add).then_inc(x2_ready, 1)
                meansq(hf, 3)
                for t in range(HT):
                    dve.scalar_tensor_tensor(u[:, t, :], z[:, t, :], rs[:, t:t + 1], w2row,
                                             ALU.mult, ALU.mult).then_inc(u_ready[1], 1)
                dve.wait_ge(lg_done, hf + 1)
                dve.tensor_copy(lg[:, bass.ds(hf * (HT * E), HT * E)], ps[0][:, 0:HT * E]).then_inc(lg_ready, 1)
                dve.wait_ge(hsum_ready, hf + 1)
                dve.wait_ge(mcopy_ready, hf + 1)

            done = [0]

            def then(ins):
                done[0] += 1
                ins.then_inc(r_dve, 1)
                dve.wait_ge(r_dve, done[0])

            dve.wait_ge(lg_ready, HALVES)
            for t in range(TILES):
                last = dve.max(top[:, t, :], lg[:, t * E:(t + 1) * E])
            then(last)
            for t in range(TILES):
                last = dve.max_index(topi[:, t, :], top[:, t, :], lg[:, t * E:(t + 1) * E])
            dve.tensor_tensor(gap[:, :], top[:, :, 1], top[:, :, 0], ALU.subtract).then_inc(gap_ready, 1)
            then(last)
            then(dve.tensor_scalar(topf[:, :, :], topi[:, :, 0:2], const("unrouted"), None, ALU.add))
            for k in range(TOPK):
                last = dve.tensor_tensor(oh[k], const("iota").unsqueeze(1).to_broadcast([128, TILES, E]),
                                         topf[:, :, k].unsqueeze(2).to_broadcast([128, TILES, E]), ALU.is_equal)
            then(last)
            dve.tensor_tensor(ohs, oh[0], oh[1], ALU.add).then_inc(ohs_ready, 1)
            then(dve.memset(cum[:, 0, :], 0.0))
            dve.wait_ge(ranks_done, 1)
            tot = ps[1][:, 0:W8].rearrange("p (t e) -> p t e", e=E)
            for t in range(1, TILES):
                then(dve.tensor_tensor(cum[:, t, :], tot[:, t - 1, :], cum[:, t - 1, :], ALU.add))
            then(dve.tensor_tensor(cnt[:, :], tot[:, TILES - 1, :], cum[:, TILES - 1, :], ALU.add))
            then(dve.tensor_tensor(over_step[:, :, :], cnt[:, :].unsqueeze(2).to_broadcast([128, E, MOST]),
                                   const("steps").unsqueeze(1).to_broadcast([128, E, MOST]), ALU.is_gt))
            then(dve.tensor_reduce(etl[:, :], over_step[:, :, :], AX.X, ALU.add))
            then(dve.tensor_tensor(lessed[:, :, :], etl[:, :].unsqueeze(1).to_broadcast([128, E, E]),
                                   const("less").rearrange("p (a b) -> p a b", a=E), ALU.mult))
            then(dve.tensor_reduce(est[:, :], lessed[:, :, :], AX.X, ALU.add))
            then(dve.tensor_tensor(rank, ps[0][:, 0:W8].rearrange("p (t e) -> p t e", e=E), cum, ALU.add))
            then(dve.scalar_tensor_tensor(rank, est[:, :].unsqueeze(1).to_broadcast([128, TILES, E]), 128.0, rank,
                                          ALU.mult, ALU.add))
            for k in range(TOPK):
                then(dve.tensor_tensor(pick[k], oh[k], rank, ALU.mult))
                then(dve.tensor_reduce(slot[k][:, :], pick[k], AX.X, ALU.add))
                dve.tensor_tensor(sidx[k][:, :], slot[k][:, :], const("trash1" if k == 0 else "trash2"),
                                  ALU.add).then_inc(idx_ready, 1)
                dve.tensor_scalar(gidx[k][:, :], slot[k][:, :], float(SLOTS - 1), None, ALU.min).then_inc(idx_ready, 1)
            then(dve.tensor_tensor(een[:, :], est[:, :], etl[:, :], ALU.add))
            then(dve.tensor_tensor(le[:, :, :], een[0:1, :].unsqueeze(1).to_broadcast([1, SLOT_TILES, E]),
                                   const("slot_iota", 1).unsqueeze(2).to_broadcast([1, SLOT_TILES, E]), ALU.is_le))
            then(dve.tensor_reduce(ef[:, 0, :], le[:, :, :], AX.X, ALU.add))
            then(dve.tensor_scalar(ef[:, 0, :], ef[:, 0, :], float(E - 1), None, ALU.min))
            then(dve.tensor_scalar(ef[:, 1, :], ef[:, 0, :], -1.0, float(E - 1), ALU.mult, ALU.add))
            dve.tensor_copy(ei[:, :, :], ef[:, :, :]).then_inc(eid_ready, 1)
            dve.wait_ge(eg_ready, 1)
            then(dve.tensor_scalar(den[:, :], eg[:, :], 1.0, None, ALU.add))
            then(dve.reciprocal(g1[:, :], den[:, :]))
            then(dve.tensor_tensor(g2[:, :], eg[:, :], g1[:, :], ALU.mult))

            def gated(j, b):
                dve.wait_ge(up_done, j + 1)
                dve.wait_ge(sg_ready, j + 1)
                dve.tensor_tensor(hh[:, b, :], ps[2 + b][:, 0:FF], sg[:, b, :], ALU.mult).then_inc(hh_ready, 1)

            def copy_y(j, b, used=None):
                dve.wait_ge(y_done, j + 1)
                if used is not None:
                    dve.wait_ge(ys_out[b], used)
                dve.tensor_copy(yo[:, b, :], ps[5][:, 0:D]).then_inc(y_ready, 1)

            gated(0, 0)
            gated(1, 1)
            copy_y(0, 0)
            gated(2, 0)
            copy_y(1, 1)
            with dve.Fori(0, (SLOT_TILES - 4) // 2) as jj:
                gated(jj * 2 + 3, 1)
                copy_y(jj * 2 + 2, 0, jj * 16 + 16)
                gated(jj * 2 + 4, 0)
                copy_y(jj * 2 + 3, 1, jj * 16 + 16)
            gated(SLOT_TILES - 1, 1)
            copy_y(SLOT_TILES - 2, 0, 16 * (SLOT_TILES // 2 - 1))
            copy_y(SLOT_TILES - 1, 1, 16 * (SLOT_TILES // 2 - 1))
            for t in range(TILES):
                dve.wait_ge(gathered[t], 16 * TOPK)
                for k, (y, g) in enumerate(((y1, g1), (y2, g2))):
                    if k == 1:
                        dve.wait_ge(mix_ready, 2 * t + 1)
                    dve.scalar_tensor_tensor(hsum[:, t, :], y[:, t, :], g[:, t:t + 1], hsum[:, t, :],
                                             ALU.mult, ALU.add).then_inc(mix_ready, 1)

        @block.tensor
        def _(pe):
            mm = pe.matmul
            pe.wait_ge(consts_in, 16)
            pe.wait_ge(front_in, 16)

            def transposed(banks, src, ready, hf, n, done, each):
                for t in range(HT):
                    pe.wait_ge(ready, hf * n + ((t + 1) if n == HT else (t // 2 + 1)))
                    for c in range(2):
                        last = pe.transpose(ps[banks[c]][0:C, 128 * t:128 * t + 128], src[:, t, C * c:C * c + C], eye)
                    if each or t == HT - 1:
                        last.then_inc(done, 1)

            with pe.Fori(0, HALVES) as hf:
                for t in range(HT):
                    pe.wait_ge(x_in[t % 2], hf * 32 + 16 * (t // 2 + 1))
                    o = ps[t // 2][:, D * (t % 2):D * (t % 2) + D]
                    mm(o, const("who", 2), bcls, start=True, stop=False)
                    for k in range(PK):
                        last = mm(o, xt[:, t % 2, 128 * k:128 * k + 128], wpatch[:, k, :],
                                  start=False, stop=(k == PK - 1))
                    last.then_inc(patch_done, 1)
                transposed((2, 3), z, z_ready[0], hf, HT, zt_done, True)
                pe.wait_ge(zt_ready, hf * 2 + 2)
                for c in range(2):
                    for k in range(2):
                        last = mm(ps[6 + c][0:C, 0:CT], wqkv1[:, k, D + C * c:D + C * c + C],
                                  fT[:, k, :].rearrange("p (i q) -> p i q", q=32)[:, :, 0:S], start=(k == 0), stop=(k == 1))
                    last.then_inc(qk_done, 1)
                for c in range(2):
                    for k in range(2):
                        last = mm(ps[4 + c][0:C, :], wqkv1[:, k, C * c:C * c + C], fT[:, k, :],
                                  start=(k == 0), stop=(k == 1))
                    last.then_inc(qk_done, 1)
                for t in range(HT):
                    for k in range(2):
                        last = mm(ps[t // 2][:, D * (t % 2):D * (t % 2) + D], fT[:, k, 128 * t:128 * t + 128],
                                  wqkv1[:, k, 2 * D:3 * D], start=(k == 0), stop=(k == 1))
                    if t % 2:
                        last.then_inc(v_done, 1)
                pe.wait_ge(q_ready, hf * 2 + 2)
                pe.wait_ge(kbd_ready, hf * 2 + 2)
                for t in range(HT):
                    for i in range(IPT):
                        for c in range(2):
                            last = mm(ps[2 + t][32 * i:32 * i + 32, HC * S * c:HC * S * (c + 1)],
                                      q1[:, c, 128 * t + 32 * i:128 * t + 32 * i + 32],
                                      kbd[:, c, IPT * t + i].rearrange("p h k -> p (h k)"), start=True, stop=True,
                                      tile_position=(0, 32 * i))
                    last.then_inc(s_done[0], 1)
                pe.wait_ge(exp_ready[0], hf + 1)
                pe.wait_ge(v1_ready, hf * 2 + 2)
                for g in range(G):
                    for t in range(HT):
                        a = (12 * t + 4 * g) * S
                        last = pe.transpose(ps[(6, 7, 0)[g]][0:104, 128 * t:128 * t + 128], sc[:, a:a + 4 * S], eye)
                    last.then_inc(pt_done, 1)
                pe.wait_ge(pt_ready, hf * G + G)
                pe.wait_ge(vbd_ready, hf + 1)
                for t in range(HT):
                    for i in range(IPT):
                        for g in range(G):
                            last = mm(ps[1 + t // 2][32 * i:32 * i + 32, D * (t % 2) + 64 * g:D * (t % 2) + 64 * g + 64],
                                      pT[:, g, 128 * t + 32 * i:128 * t + 32 * i + 32],
                                      vbd[:, t, i, 64 * g:64 * g + 64], start=True, stop=True,
                                      tile_position=(0, 32 * i))
                    if t % 2:
                        last.then_inc(o_done, 1)
                transposed((3, 4), o1, o_ready, hf, 2, ot_done, False)
                pe.wait_ge(ot_ready, hf * 2 + 2)
                for t in range(HT):
                    o = ps[5 + t // 2][:, D * (t % 2):D * (t % 2) + D]
                    mm(o, const("ones", 1), bproj, start=True, stop=False)
                    for k in range(2):
                        last = mm(o, fT[:, k, 128 * t:128 * t + 128], wproj[:, k, :], start=False, stop=(k == 1))
                    if t % 2:
                        last.then_inc(proj_done, 1)
                transposed((7, 0), u, u_ready[0], hf, HT, ut_done, False)
                pe.wait_ge(ut_ready, hf * 2 + 2)
                for t in range(HT):
                    for k in range(2):
                        last = mm(ps[1 + t // 2][:, D * (t % 2):D * (t % 2) + D], fT[:, k, 128 * t:128 * t + 128],
                                  wv2[:, k, :], start=(k == 0), stop=(k == 1))
                    if t % 2:
                        last.then_inc(v2_done, 1)
                for n in range(5):
                    if n >= 3:
                        pe.wait_ge(rope_mul, hf * 5 + (n - 2))
                    for e in range(2):
                        for k in range(2):
                            last = mm(ps[((3, 4), (5, 6), (7, 0))[n % 3][e]][0:C, 0:CT], wqk2[:, k, (n + 4) % 5, e, :],
                                      fT[:, k, :].rearrange("p (i q) -> p i q", q=32)[:, :, 0:S],
                                      start=(k == 0), stop=(k == 1))
                    last.then_inc(eo_done, 1)
                pe.wait_ge(rope_add, hf * 5 + 5)
                pe.wait_ge(kbd2_ready, hf + 1)
                pe.wait_ge(v2_ready, hf * 2 + 2)
                for t in range(HT):
                    for i in range(IPT):
                        for e in range(2):
                            last = mm(ps[1 + t][0:104, G * S * i:G * S * (i + 1)],
                                      qr[:, e, IPT * t + i].rearrange("p r q -> p (r q)"),
                                      kbd2[:, e, IPT * t + i].rearrange("p g k -> p (g k)"),
                                      start=(e == 0), stop=(e == 1))
                    last.then_inc(s_done[1], 1)
                pe.wait_ge(p2_ready, hf * HT + HT)
                for g in range(G):
                    for t in range(HT):
                        last = pe.transpose(ps[5 + g][:, 128 * t:128 * t + 104],
                                            p2[:, t, g].rearrange("p i k -> p (i k)"), eye[0:104, 0:104])
                    last.then_inc(pt2_done, 1)
                for g in range(G):
                    pe.wait_ge(pt2_ready, hf * G + (1 if g == 0 else G))
                    for i in range(IPT):
                        if g == 2:
                            pe.wait_ge((ot2_a, ot2_d)[i % 2], hf * (2 * G) + (i // 2 + 1))
                        for t in range(HT):
                            last = mm(ps[4 * (g % 2) + i][0:64, 104 * t:104 * t + 104],
                                      v2[32 * i:32 * i + S, t, 64 * g:64 * g + 64],
                                      pT2[32 * i:32 * i + S, g, t, :], start=True, stop=True, tile_position=(32 * i, 0))
                    last.then_inc(pv2_done, 1)
                pe.wait_ge(ot2_a, hf * (2 * G) + 2 * G)
                pe.wait_ge(ot2_d, hf * (2 * G) + 2 * G)
                for t in range(HT):
                    for k in range(6):
                        last = mm(ps[4 + t // 2][:, D * (t % 2):D * (t % 2) + D], ot2[:, k, 128 * t:128 * t + 128],
                                  wout[:, k, :], start=(k == 0), stop=(k == 5))
                    if t % 2:
                        last.then_inc(wo_done, 1)
                transposed((6, 7), u, u_ready[1], hf, HT, mt_done, False)
                pe.wait_ge(mt_ready, hf * 2 + 2)
                for t in range(HT):
                    for k in range(2):
                        last = mm(ps[0][:, E * t:E * t + E], fT[:, k, 128 * t:128 * t + 128], wr[:, k, :],
                                  start=(k == 0), stop=(k == 1))
                last.then_inc(lg_done, 1)
                pe.wait_ge(lg_ready, hf + 1)

            pe.wait_ge(ohs_ready, 1)
            flat = rt[:, 2 * W8:3 * W8]
            mm(ps[0][:, 0:W8], const("before"), flat, start=True, stop=True)
            mm(ps[1][:, 0:W8], const("ones"), flat, start=True, stop=True).then_inc(ranks_done, 1)

            def x_turn(j, b, loads):
                pe.wait_ge(xs_in[b], loads)
                for c in range(2):
                    last = pe.transpose(ps[6][0:C, 128 * c:128 * c + 128], xin[:, b, C * c:C * c + C], eye)
                last.then_inc(xtr_done, 1)

            def gate_up(j, b):
                e = pe.value_load(ei[0:1, 1, bass.ds(j, 1)], min_val=0, max_val=E - 1)
                pe.wait_ge(xT_ready, j + 1)
                for half, done in ((0, gate_done), (1, up_done)):
                    for k in range(2):
                        last = mm(ps[2 * half + b][:, 0:FF], xT[:, b, 128 * k:128 * k + 128],
                                  big[0:C, bass.ds(e * (4 * FF) + (GU0 + 2 * FF * k + FF * half), FF)],
                                  start=(k == 0), stop=(k == 1))
                    last.then_inc(done, 1)

            def h_turn(j, b):
                pe.wait_ge(hh_ready, j + 1)
                for k in range(3):
                    last = pe.transpose(ps[4][:, 128 * k:128 * k + 128], hh[:, b, 128 * k:128 * k + 128], eye)
                last.then_inc(htr_done, 1)

            def down(j, b, first=False):
                e = pe.value_load(ei[0:1, 0, bass.ds(j, 1)], min_val=0, max_val=E - 1)
                pe.wait_ge(hT_ready, j + 1)
                if not first:
                    pe.wait_ge(y_ready, j)
                for k in range(3):
                    last = mm(ps[5][:, 0:D], hT[:, b, 128 * k:128 * k + 128],
                              big[:, bass.ds(e * (3 * D) + D * k, D)], start=(k == 0), stop=(k == 2))
                last.then_inc(y_done, 1)

            pe.wait_ge(eid_ready, 1)
            x_turn(0, 0, 16)
            pe.wait_ge(early_in, 16 * 5)
            pe.wait_ge(late_in, 16 * 5)
            gate_up(0, 0)
            x_turn(1, 1, 16)

            def step(j, b, loads, first=False):
                h_turn(j - 1, 1 - b)
                gate_up(j, b)
                down(j - 1, 1 - b, first)
                x_turn(j + 1, 1 - b, loads)

            step(1, 1, 32, True)
            step(2, 0, 32)
            with pe.Fori(0, (SLOT_TILES - 4) // 2) as jj:
                step(jj * 2 + 3, 1, jj * 16 + 48)
                step(jj * 2 + 4, 0, jj * 16 + 48)
            step(SLOT_TILES - 1, 1, 16 * (SLOT_TILES // 2 + 1))
            h_turn(SLOT_TILES - 1, 1)
            down(SLOT_TILES - 1, 1)


def table_of_constants():
    t = np.zeros((128, NCONST), np.float32)

    def put(name, a):
        a = np.asarray(a, np.float32)
        at, w = _C[name]
        t[:a.shape[0], at:at + w] = a.reshape(a.shape[0], w)

    row = np.arange(128)
    q = row % 32
    j = np.arange(D)
    i = np.arange(S - 1, dtype=np.float32)[:, None]
    angle = i / np.power(np.float32(10000.0), ((2 * (j // 2)).astype(np.float32) / np.float32(D)))
    pos = np.sin(angle + np.where(j % 2 == 1, np.float32(np.pi / 2), np.float32(0.0)).astype(np.float32))
    full = np.zeros((128, D), np.float32)
    for b in range(IPT):
        full[32 * b + 1:32 * b + S] = pos
    put("pos", full)
    key = np.arange(S)[None, :]
    put("mask1", np.where(key <= q[:, None], 0.0, MASKED))
    put("mask2", np.where(key <= (row[:104] % S)[:, None], 0.0, MASKED))
    put("head_of_row", row[:C, None] // HD1 == np.arange(HC))
    put("head_of_key", row[:104, None] // S == np.arange(4))
    put("group_of_row", row[:C, None] // J == np.arange(G))
    inv = (1.0 / np.power(np.float32(10000.0), np.arange(0, HD2, 2, dtype=np.float32) / np.float32(HD2))).astype(np.float32)
    f = np.arange(S, dtype=np.float32)[None, :] * inv[row[:C] % J][:, None]
    put("cos", np.cos(f))
    put("sin", np.sin(f))
    put("eye", np.eye(128))
    put("before", row[:, None] < row[None, :])
    put("ones", np.ones((128, 128)))
    put("unrouted", (99.0 * (q >= S))[:, None])
    trash = np.zeros((128, TILES))
    pads = np.flatnonzero(q >= S)
    trash[pads, :] = SLOTS + np.arange(len(pads) * TILES).reshape(len(pads), TILES)
    put("trash1", trash)
    put("trash2", np.where(trash > 0, trash + PADS, 0))
    put("steps", np.broadcast_to(128.0 * np.arange(MOST), (128, MOST)))
    less = (np.arange(E)[None, :] < np.arange(E)[:, None]).reshape(1, -1)
    put("less", np.broadcast_to(less, (128, E * E)))
    put("iota", np.broadcast_to(np.arange(E), (128, E)))
    put("slot_iota", np.broadcast_to(np.arange(SLOT_TILES), (128, SLOT_TILES)))
    put("neghalf", np.full((128, HT), -0.5))
    put("who", np.stack([(q >= 1) & (q < S), q == 0]))
    return t


def kernel(x, cls_tok, L0_tok_W, L0_tok_b, L0_attn_W_attn, L0_attn_b_attn, L0_attn_W_proj, L0_attn_b_proj,
           L0_ffn_norm1_w, L0_ffn_w_qkv, L0_ffn_w_out, L0_ffn_norm2_w, L0_ffn_w_router, L0_ffn_w_gate_up,
           L0_ffn_w_down):
    import concourse.bacc as bacc
    from concourse.bass_utils import run_bass_kernel_spmd

    f = lambda a: np.asarray(a, np.float32)
    edge = GRID * PATCH
    p = f(x)[:, :, :edge, :edge].reshape(IMAGES, CH, GRID, PATCH, GRID, PATCH).transpose(1, 3, 5, 0, 2, 4)
    padded = np.zeros((PK * 128, IMAGES, 32), np.float32)
    padded[:, :, 1:S] = p.reshape(PK * 128, IMAGES, S - 1)
    xp = padded.reshape(PK, 128, TILES, 128).transpose(2, 1, 0, 3).reshape(TILES, 128, PK * 128)

    fw = np.zeros((128, NFRONT), np.float32)

    def put(name, a):
        at, w = _F[name]
        fw[:a.shape[0], at:at + w] = a.reshape(a.shape[0], w)

    def chunks(a, n):
        return a.reshape(n, a.shape[0] // n, -1).transpose(1, 0, 2)

    put("wpatch", chunks(f(L0_tok_W).reshape(D, -1).T, PK))
    put("wqkv1", chunks(f(L0_attn_W_attn), 2))
    put("wproj", chunks(f(L0_attn_W_proj), 2))
    wq = f(L0_ffn_w_qkv)
    q = wq[:, :G * R * HD2].reshape(D, G, R, J, 2).transpose(0, 2, 4, 1, 3)
    k = wq[:, G * R * HD2:G * (R + 1) * HD2].reshape(D, G, J, 2).transpose(0, 3, 1, 2)[:, None]
    put("wqk2", chunks(np.concatenate([q, k], 1).reshape(D, -1), 2))
    put("wv2", chunks(wq[:, G * (R + 1) * HD2:], 2))
    put("wout", chunks(f(L0_ffn_w_out), 6))
    put("wr", chunks(f(L0_ffn_w_router), 2))
    put("w2row", np.broadcast_to(f(L0_ffn_norm2_w)[None], (128, D)))
    cols = np.concatenate([f(L0_attn_b_attn).reshape(6, C), f(L0_ffn_norm1_w).reshape(2, C)]).T
    at = _F["small"][0]
    fw[:C, at:at + 8] = cols
    at = _F["rows"][0]
    fw[0, at:at + D] = f(L0_tok_b)
    fw[1, at:at + D] = f(cls_tok).reshape(D)
    fw[0, at + D:at + 2 * D] = f(L0_attn_b_proj)

    wgu = f(L0_ffn_w_gate_up).reshape(E, 2, C, 2 * FF)[::-1].transpose(2, 0, 1, 3).reshape(C, -1)
    wdn = f(L0_ffn_w_down).reshape(E, 3, 128, D).transpose(2, 0, 1, 3).reshape(128, -1)
    arrays = {"xp": xp, "fw": fw, "cst": table_of_constants(), "wgu": wgu, "wdn": wdn}
    arrays = {n: np.ascontiguousarray(a) for n, a in arrays.items()}

    nc = bacc.Bacc("TRN2", target_bir_lowering=False, num_devices=1)
    args = [nc.dram_tensor(n, a.shape, F32, kind="ExternalInput").ap() for n, a in arrays.items()]
    xs = nc.dram_tensor("slot_inputs", (XS_TILES * 128, D), F32, kind="Internal").ap()
    ys = nc.dram_tensor("slot_outputs", (SLOTS, D), F32, kind="Internal").ap()
    out = nc.dram_tensor("out", (IMAGES, S, D), F32, kind="ExternalOutput").ap()
    build_tower(nc, *args, xs, ys, out)
    r = run_bass_kernel_spmd(nc, [arrays], core_ids=[0])
    return r.results[0]["out"]
```

```python
from contextlib import ExitStack

import numpy as np

import concourse.bass as bass
from concourse import mybir

F32 = mybir.dt.float32
I32 = mybir.dt.int32
U32 = mybir.dt.uint32
ALU = mybir.AluOpType
ACT = mybir.ActivationFunctionType
AX = mybir.AxisListType

IMAGES, CH, SIDE, PATCH = 32, 3, 84, 16
GRID = SIDE // PATCH
S = GRID * GRID + 1
D = 192
C = 96
PK = CH * PATCH * PATCH // 128
IPT = 4
TILES = IMAGES // IPT
GT = 2
GROUPS = TILES // GT
GI = GT * IPT
CT = GI * S
H1, HD1 = 12, 16
HC = C // HD1
G, R, HD2 = 3, 4, 64
J = HD2 // 2
E, FF, TOPK = 16, 384, 2
TOKENS = IMAGES * S
SLOT_TILES = (TOPK * TOKENS + E * 127) // 128
SLOTS = SLOT_TILES * 128
PADS = (32 - S) * IPT * TILES
XS_TILES = SLOT_TILES + (TOPK * PADS + 127) // 128
MOST = (TOKENS + 127) // 128
W = D + 2
LN_EPS, RMS_EPS, MASKED = 1e-5, 1e-6, -1e30

_C = {}
_n = 0
for _name, _w in (("pos", D), ("who", 128), ("eye", 128), ("neghalf", GT), ("number", TILES), ("spare", 1),
                  ("mask1", S), ("mask2", S), ("head_of_row", HC), ("head_of_key", 4),
                  ("group_of_row", G), ("turn", 4 * S), ("before", 128), ("ones", 128),
                  ("unrouted", 1), ("trash1", TILES), ("trash2", TILES), ("steps", MOST), ("less", E * E),
                  ("iota", E), ("slot_iota", SLOT_TILES)):
    _C[_name] = (_n, _w)
    _n += _w
NCONST = _n
NFIRST = _C["mask1"][0]

_F = {}
_n = 0
for _name, _w in (("bcls", D), ("wpatch", PK * D), ("wqkv1", 2 * 3 * D), ("wproj", 2 * D), ("small", 16),
                  ("bprow", D), ("wqk2", 2 * 5 * 2 * C), ("wv2", 2 * D), ("wout", 6 * D), ("wr", 2 * E),
                  ("w2row", D)):
    _F[_name] = (_n, _w)
    _n += _w
NFRONT = _n
GU0 = E * 3 * D


def build_tower(nc, xp, fw, cst, wgu, wdn, xs, out):
    ctx = ExitStack()
    with ctx:
        def sb(name, shape, dt=F32):
            return ctx.enter_context(nc.sbuf_tensor(name, shape, dt))

        def sem(name):
            return ctx.enter_context(nc.semaphore(name))

        big = sb("experts", [128, E * (3 * D + 4 * FF)])
        front = sb("front", [128, NFRONT])
        ct = sb("constants", [128, NCONST])
        xt = sb("patches", [128, 2, PK * 128])
        base = sb("embedding_base", [128, D])
        p2 = sb("probs2", [104, GT, G, IPT, 32])
        pbd = sb("probs2_by_key", [128, G, GT, IPT, R * S])
        ot2a = sb("attended2_groups01", [128, R, GT, 128])
        ot2b = sb("attended2_group2", [128, 2, GT, 128])
        hsum = sb("residual", [128, TILES, D])
        mall = sb("moe_in", [128, TILES, W])
        lg = sb("logits", [128, TILES * E])
        fill = sb("empty_slot", [128, W])
        st6 = sb("stats", [128, GT, 6])
        mom = sb("moments", [128, 4, GT])
        mean = sb("mean", [128, GT])
        ve = [sb("variance_a", [128, GT]), sb("variance_b", [128, GT])]
        rs = [sb("rstd_a", [128, GT]), sb("rstd_b", [128, GT])]
        ms = [sb("meansq_a", [128, GT]), sb("meansq_b", [128, GT])]
        NR = 12 * GT
        mx = [sb("rowmax_a", [128, NR]), sb("rowmax_b", [128, NR])]
        sm = [sb("rowsum_a", [128, NR]), sb("rowsum_b", [128, NR])]
        rc = [sb("rowrecip_a", [128, NR]), sb("rowrecip_b", [128, NR])]
        ps = [ctx.enter_context(nc.psum_tensor(f"bank{i}", [128, 512], F32)) for i in range(8)]

        def const(name, rows=128):
            a, w = _C[name]
            return ct[0:rows, a:a + w]

        def fview(name, rows=128):
            a, w = _F[name]
            return front[0:rows, a:a + w]

        eye = const("eye")
        wpatch = fview("wpatch").rearrange("p (k n) -> p k n", k=PK)
        wqkv1 = fview("wqkv1", C).rearrange("p (c n) -> p c n", c=2)
        wproj = fview("wproj", C).rearrange("p (c n) -> p c n", c=2)
        wqk2 = fview("wqk2", C).rearrange("p (c s e n) -> p c s e n", c=2, s=5, e=2)
        wv2 = fview("wv2", C).rearrange("p (c n) -> p c n", c=2)
        wout = fview("wout").rearrange("p (k n) -> p k n", k=6)
        wr = fview("wr", C).rearrange("p (c n) -> p c n", c=2)
        w2row = fview("w2row")
        bprow = fview("bprow")
        small = fview("small", C)
        bcls = fview("bcls", 2)

        arena0 = (E // 2) * 3 * D
        at = [arena0]

        def carve(n, rows=128):
            a = at[0]
            at[0] += n
            assert at[0] <= GU0 + (E // 2) * 4 * FF
            return big[0:rows, a:a + n]

        h = carve(GT * D).rearrange("p (t n) -> p t n", t=GT)
        z = carve(GT * D).rearrange("p (t n) -> p t n", t=GT)
        fTa = carve(2 * GT * 128, C)
        q1 = carve(2 * GT * 128, C).rearrange("p (c n) -> p c n", c=2)
        k1 = carve(2 * CT, C).rearrange("p (c i k) -> p c i k", c=2, k=S)
        kbd = carve(2 * GI * HC * S, C).rearrange("p (c i h k) -> p c i h k", c=2, i=GI, h=HC)
        v1 = carve(GT * D).rearrange("p (t n) -> p t n", t=GT)
        vbd = carve(GI * D, 104).rearrange("p (t i n) -> p t i n", t=GT, i=IPT)
        sca = carve(NR * S)
        pT = carve(G * GT * 128, 104)
        o1 = carve(GT * D).rearrange("p (t n) -> p t n", t=GT)
        hB = carve(GT * D).rearrange("p (t n) -> p t n", t=GT)
        zB = carve(GT * D).rearrange("p (t n) -> p t n", t=GT)
        u = carve(GT * D).rearrange("p (t n) -> p t n", t=GT)
        fTb = carve(2 * GT * 128, C)
        qr = carve(2 * R * CT, C).rearrange("p (e i r q) -> p e i r q", e=2, i=GI, r=R)
        tmp = carve(2 * 4 * CT, C).rearrange("p (b m e i q) -> p b m e i q", b=2, m=2, e=2, q=S)
        kr = carve(2 * CT, C).rearrange("p (e i k) -> p e i k", e=2, k=S)
        kbd2 = carve(2 * GI * G * S, C).rearrange("p (e i g k) -> p e i g k", e=2, i=GI, g=G)
        v2 = carve(GT * D).rearrange("p (t n) -> p t n", t=GT)
        scb = carve(NR * S)
        sc = [sca, scb]

        at = [0]

        def over(n, rows=128):
            a = at[0]
            at[0] += n
            assert at[0] <= NFRONT
            return front[0:rows, a:a + n]

        xin = over(2 * W).rearrange("p (b n) -> p b n", b=2)
        xT = over(2 * 2 * 128, C).rearrange("p (b n) -> p b n", b=2)
        sg = over(2 * FF).rearrange("p (b n) -> p b n", b=2)
        hh = over(2 * FF).rearrange("p (b n) -> p b n", b=2)
        hT = over(2 * FF).rearrange("p (b n) -> p b n", b=2)
        yo = over(2 * D).rearrange("p (b n) -> p b n", b=2)
        mall2 = pbd[:, :, :, :, :].rearrange("p g t i n -> p (g t i n)")[:, 0:TILES * W]\
            .rearrange("p (t n) -> p t n", t=TILES)

        top = sb("top", [128, TILES, 8])
        topi = sb("topi", [128, TILES, 8], U32)
        topf = sb("topf", [128, TILES, 2])
        gap = sb("gap", [128, TILES])
        eg = sb("expgap", [128, TILES])
        den = sb("den", [128, TILES])
        rt = xt[:, :, :].rearrange("p b n -> p (b n)")
        W8 = TILES * E

        def table(i):
            return rt[:, W8 * i:W8 * (i + 1)].rearrange("p (t e) -> p t e", e=E)

        oh, ohs, cum, rank, pick = [table(0), table(1)], table(2), table(3), table(4), [table(5), table(6)]
        a = 7 * W8
        over_step = rt[:, a:a + E * MOST].rearrange("p (e m) -> p e m", e=E)
        a += E * MOST
        lessed = rt[:, a:a + E * E].rearrange("p (e f) -> p e f", e=E)
        assert a + E * E <= 2 * PK * 128
        cnt = sb("count", [128, E])
        etl = sb("expert_tiles", [128, E])
        est = sb("expert_start", [128, E])
        een = sb("expert_end", [128, E])
        held_gate = sb("held_gate", [128, 2])
        held_row = sb("held_row", [128, 2], I32)
        gate = sb("gate", [128, 2])
        row = sb("row", [128, 2], I32)
        le = sb("ended", [1, SLOT_TILES, E])
        ef = sb("expert_f", [1, 2 * SLOT_TILES + 1])
        ei = sb("expert_of_slot_tile", [1, 2 * SLOT_TILES + 3], I32)
        slot = [sb("slot1", [128, TILES]), sb("slot2", [128, TILES])]
        sidx = [sb("scatter1", [128, TILES], I32), sb("scatter2", [128, TILES], I32)]

        first_in, consts_in, late_in, early_in = sem("first_in"), sem("consts_in"), sem("late_in"), sem("early_in")
        patch_w_in, attn_w_in, rest_w_in = sem("patch_w_in"), sem("attn_w_in"), sem("rest_w_in")
        x_in = [sem("x_in0"), sem("x_in1")]
        pads_set, fill_set, filled = sem("pads_set"), sem("fill_set"), sem("filled")
        base_done, base_ready, number_set = sem("base_done"), sem("base_ready"), sem("number_set")
        patch_done = sem("patch_done")
        h_ready, hb_ready = sem("h_ready"), sem("hb_ready")
        st_ready = [sem("st_ready_a"), sem("st_ready_b")]
        mom_ready = [sem("mom_ready_a"), sem("mom_ready_b")]
        ve_ready = [sem(f"ve_ready_{n}") for n in range(4)]
        rs_ready = [sem(f"rs_ready_{n}") for n in range(4)]
        z_ready = [sem("z_ready_a"), sem("z_ready_b")]
        zt_done, zt_ready = sem("zt_done"), sem("zt_ready")
        k_done, q_done, k_ready, q_ready = sem("k_done"), sem("q_done"), sem("k_ready"), sem("q_ready")
        v_done, v1_ready = sem("v_done"), sem("v1_ready")
        vrep_in, vbd_ready = sem("vrep_in"), sem("vbd_ready")
        kbd_ready = sem("kbd_ready")
        s_done = [sem("s_done_a"), sem("s_done_b")]
        sm_ready = [sem("sm_ready_a"), sem("sm_ready_b")]
        max_ready = [sem("max_ready_a"), sem("max_ready_b")]
        sub_ready = [sem("sub_ready_a"), sem("sub_ready_b")]
        exp_ready = [sem("exp_ready_a"), sem("exp_ready_b")]
        sum_ready = [sem("sum_ready_a"), sem("sum_ready_b")]
        rc_ready = [sem("rc_ready_a"), sem("rc_ready_b")]
        pt_done, pt_ready = sem("pt_done"), sem("pt_ready")
        o_done, o_ready = sem("o_done"), sem("o_ready")
        ot_done, ot_ready = sem("ot_done"), sem("ot_ready")
        proj_done, h1_ready = sem("proj_done"), sem("h1_ready")
        sq_ready = [sem("sq_ready_a"), sem("sq_ready_b")]
        u_ready = [sem("u_ready_a"), sem("u_ready_b")]
        ut_done, ut_ready = sem("ut_done"), sem("ut_ready")
        v2_done, v2_ready = sem("v2_done"), sem("v2_ready")
        eo_done = sem("eo_done")
        rope_mul, rope_add = sem("rope_mul"), sem("rope_add")
        kbd2_ready = sem("kbd2_ready")
        p2_ready = sem("p2_ready")
        pt2_done, pbd_a, pbd_d = sem("pt2_done"), sem("pbd_a"), sem("pbd_d")
        pv2_done = sem("pv2_done")
        ot2_a, ot2_d = sem("ot2_a"), sem("ot2_d")
        wo_done, x2_ready = sem("wo_done"), sem("x2_ready")
        hsum_ready, mcopy_ready = sem("hsum_ready"), sem("mcopy_ready")
        mt_done, mt_ready = sem("mt_done"), sem("mt_ready")
        lg_done, lg_ready = sem("lg_done"), sem("lg_ready")
        r_dve, gap_ready, eg_ready, twice = sem("r_dve"), sem("gap_ready"), sem("eg_ready"), sem("twice")
        ohs_ready, ranks_done = sem("ohs_ready"), sem("ranks_done")
        gates_set, idx_ready, eid_ready = sem("gates_set"), sem("idx_ready"), sem("eid_ready")
        scattered, res_out = sem("scattered"), sem("res_out")
        xs_in = [sem("xs_in0"), sem("xs_in1")]
        xtr_done, xT_ready = sem("xtr_done"), sem("xT_ready")
        gate_done, up_done, sg_ready, hh_ready = sem("gate_done"), sem("up_done"), sem("sg_ready"), sem("hh_ready")
        htr_done, hT_ready, y_done, y_ready = sem("htr_done"), sem("hT_ready"), sem("y_done"), sem("y_ready")
        kept, taken = sem("kept"), sem("taken")
        adding, added = sem("adding"), sem("added")

        block = ctx.enter_context(nc.Block())

        def further_pairs(eng):
            return eng.value_load(ei[0:1, 2 * SLOT_TILES:2 * SLOT_TILES + 1], min_val=0, max_val=SLOT_TILES // 2 - 1)

        def stages(eng, a_phases, b_phases):
            for a in a_phases:
                a(0)
            with eng.Fori(0, GROUPS - 1) as g:
                for a, b in zip(a_phases, b_phases):
                    a(g + 1)
                    b(g)
            for b in b_phases:
                b(GROUPS - 1)

        def later(g):
            return not isinstance(g, int) or g > 0

        def nothing(g):
            pass

        @block.sync
        def _(sp):
            def load_x(n):
                if n >= 2:
                    sp.wait_ge(patch_done, n - 1)
                sp.dma_start(xt[:, n % 2, :], xp[n]).then_inc(x_in[n % 2], 16)

            def load_front(name, last, done):
                a, b = _F[name][0], sum(_F[last])
                sp.dma_start(front[:, a:b], fw[:, a:b]).then_inc(done, 16)

            load_x(0)
            load_front("bcls", "wpatch", patch_w_in)
            load_x(1)
            load_front("wqkv1", "small", attn_w_in)
            load_front("bprow", "w2row", rest_w_in)
            sp.wait_ge(fill_set, 3)
            sp.dma_start(xs.rearrange("(a p) n -> p a n", p=128),
                         fill[:, :].unsqueeze(1).to_broadcast([128, XS_TILES, W])).then_inc(filled, 16)
            sp.dma_start(out[TOKENS:TOKENS + 128, :], fill[:, 0:D]).then_inc(res_out, 16)
            lo = (E // 2) * 4 * FF
            for g in range(GROUPS):
                for n in range(GT * g + 2, GT * g + 4):
                    if n < TILES:
                        load_x(n)
                sp.wait_ge(v1_ready, g + 1)
                for i in range(IPT):
                    for r in range(4):
                        sp.dma_start(vbd[S * r:S * r + S, :, i, :], v1[32 * i:32 * i + S, :, :]).then_inc(vrep_in, 16)
                if g == 0:
                    sp.dma_start(big[:, 0:arena0], wdn[:, 0:arena0]).then_inc(early_in, 16)
                else:
                    for part in (2 * g - 2, 2 * g - 1):
                        a, w = lo + part * (lo // 6), lo // 6
                        sp.dma_start(big[0:C, GU0 + a:GU0 + a + w], wgu[:, a:a + w]).then_inc(early_in, 16)
            sp.wait_ge(lg_ready, GROUPS)
            sp.wait_ge(hsum_ready, GROUPS)
            sp.wait_ge(mcopy_ready, GROUPS)
            sp.dma_start(big[:, arena0:GU0], wdn[:, arena0:GU0]).then_inc(late_in, 16)
            for part in range(4):
                a, w = part * (lo // 4), lo // 4
                sp.dma_start(big[0:C, GU0 + a:GU0 + a + w], wgu[:, a:a + w]).then_inc(late_in, 16)
            dst = out[0:TOKENS, :].rearrange("(t i q) n -> i q t n", i=IPT, q=S)
            for i in range(IPT):
                sp.dma_start(dst[i], hsum[32 * i:32 * i + S, :, :]).then_inc(res_out, 16)
            sp.wait_ge(scattered, 16 * TOPK * TILES)

            def load(j, b):
                sp.dma_start(xin[:, b, :], xs[bass.ds(j * 128, 128), :]).then_inc(xs_in[b], 16)

            def reload(j, b):
                sp.wait_ge(xtr_done, j - 1)
                sp.wait_ge(kept, j - 1)
                load(j, b)

            load(0, 0)
            load(1, 1)
            reload(2, 0)
            sp.wait_ge(eid_ready, 1)
            further = further_pairs(sp)
            with sp.Fori(1, SLOT_TILES // 2) as jj:
                with sp.If(jj <= further):
                    reload(jj * 2 + 1, 1)
                    reload(jj * 2 + 2, 0)

        @block.gpsimd
        def _(pool):
            pool.memset(fill[:, 0:D + 1], 0.0).then_inc(fill_set, 1)
            pool.memset(p2[:, :, :, :, :], 0.0).then_inc(pads_set, 1)
            pool.memset(pbd[:, :, :, :, :], 0.0).then_inc(pads_set, 1)
            pool.wait_ge(first_in, 16)
            pool.tensor_copy(fill[:, D + 1:W].bitcast(I32), const("spare")).then_inc(fill_set, 1)
            pool.tensor_copy(mall[:, :, D + 1].bitcast(I32), const("number")).then_inc(fill_set, 1)
            pool.memset(ot2a[:, :, :, :], 0.0).then_inc(pads_set, 1)
            pool.memset(ot2b[:, :, :, :], 0.0).then_inc(pads_set, 1)

            def rstd(g, n):
                s = (0, 0, 0, 1)[n]
                pool.wait_ge(ve_ready[n], g + 1)
                pool.tensor_tensor(rs[s][:, :], ve[s][:, :], const("neghalf"), ALU.pow).then_inc(rs_ready[n], 1)

            def a1(g):
                rstd(g, 0)

            def a2(g):
                if not later(g):
                    pool.wait_ge(rest_w_in, 16)
                pool.wait_ge(z_ready[0], g + 1)
                pool.tensor_tensor(h, h, bprow.unsqueeze(1).to_broadcast([128, GT, D]), ALU.add).then_inc(hb_ready, 1)

            def a4(g):
                if not later(g):
                    pool.wait_ge(consts_in, 16)
                pool.wait_ge(vrep_in, g * (16 * 16) + 16 * 16)
                vv = vbd.rearrange("p t i (g r d) -> p (t i g) r d", g=G, r=4)
                pool.tensor_tensor(vv, vv, const("head_of_key", 104).unsqueeze(1).unsqueeze(3)
                                   .to_broadcast([104, GI * G, 4, HD1]), ALU.mult).then_inc(vbd_ready, 1)

            def a8(g):
                rstd(g, 1)
                rstd(g, 2)

            def b2(g):
                for n in range(5):
                    pool.wait_ge(rope_mul, g * 5 + (n + 1))
                    to = kr if n == 0 else qr[:, :, :, n - 1, :]
                    pool.tensor_tensor(to, tmp[:, n % 2, :, 0], tmp[:, n % 2, :, 1], ALU.add).then_inc(rope_add, 1)
                    if n == 0:
                        pool.wait_ge(rope_add, g * 5 + 1)
                        for e in range(2):
                            last = pool.tensor_tensor(
                                kbd2[:, e], kr[:, e].unsqueeze(2).to_broadcast([C, GI, G, S]),
                                const("group_of_row", C).unsqueeze(1).unsqueeze(3).to_broadcast([C, GI, G, S]),
                                ALU.mult)
                        last.then_inc(kbd2_ready, 1)

            def b6(g):
                rstd(g, 3)
                pool.wait_ge(x2_ready, g * 2 + 2)
                pool.tensor_tensor(hsum[:, bass.ds(g * GT, GT), :], hB, zB, ALU.add).then_inc(hsum_ready, 1)
                pool.wait_ge(u_ready[1], g + 1)
                pool.tensor_copy(mall[:, bass.ds(g * GT, GT), 0:D], u).then_inc(mcopy_ready, 1)

            stages(pool, [a1, a2, nothing, a4, nothing, nothing, nothing, a8],
                   [nothing, b2, nothing, nothing, nothing, b6, nothing, nothing])
            pool.wait_ge(filled, 16)
            pool.wait_ge(mcopy_ready, GROUPS)
            pool.wait_ge(fill_set, 3)
            for k in range(TOPK):
                pool.wait_ge(gates_set, k + 1)
                pool.wait_ge(idx_ready, k + 1)
                if k == 1:
                    pool.wait_ge(twice, 1)
                for t in range(TILES):
                    pool.indirect_dma_start(xs, bass.IndirectOffsetOnAxis(sidx[k][:, t:t + 1], 0),
                                            (mall, mall2)[k][:, t, :], None).then_inc(scattered, 16)
            pool.wait_ge(res_out, 16 * (IPT + 1))
            pool.wait_ge(eid_ready, 1)
            further = further_pairs(pool)

            def add(j, b):
                if later(j):
                    pool.wait_ge(added, j * 16)
                pool.wait_ge(y_ready, j + 1)
                pool.sem_inc(adding, 1)
                pool.indirect_dma_start(out, bass.IndirectOffsetOnAxis(row[:, b:b + 1], 0),
                                        yo[:, b, :], None, compute_op=ALU.add).then_inc(added, 16)

            add(0, 0)
            add(1, 1)
            with pool.Fori(1, SLOT_TILES // 2) as jj:
                with pool.If(jj <= further):
                    add(jj * 2, 0)
                    add(jj * 2 + 1, 1)
            pool.wait_ge(added, further * 32 + 32)

        @block.scalar
        def _(act):
            act.dma_start(ct[:, 0:NFIRST], cst[:, 0:NFIRST]).then_inc(first_in, 16)
            act.dma_start(ct[:, NFIRST:], cst[:, NFIRST:]).then_inc(consts_in, 16)

            def a2(g):
                act.wait_ge(zt_done, g + 1)
                act.activation(fTa, ps[1][0:C, :], ACT.Copy).then_inc(zt_ready, 1)

            def a3(g):
                if not later(g):
                    act.wait_ge(attn_w_in, 16)
                act.wait_ge(k_done, g + 1)
                for c in range(2):
                    act.activation(k1[:, c].rearrange("p i k -> p (i k)"), ps[2][0:C, CT * c:CT * c + CT],
                                   ACT.Identity, bias=small[:, 2 + c:3 + c]).then_inc(k_ready, 1)
                act.wait_ge(q_done, g + 1)
                for c in range(2):
                    act.activation(q1[:, c, :], ps[3][0:C, 256 * c:256 * c + 256], ACT.Identity,
                                   bias=small[:, c:c + 1]).then_inc(q_ready, 1)

            def a4(g):
                act.wait_ge(sub_ready[0], g + 1)
                act.activation(sca, sca, ACT.Exp, scale=HD1 ** -0.5).then_inc(exp_ready[0], 1)

            def a5(g):
                act.wait_ge(pt_done, g * 2 + 1)
                act.activation(pT[:, 0:512], ps[3][0:104, :], ACT.Copy).then_inc(pt_ready, 1)
                act.wait_ge(pt_done, g * 2 + 2)
                act.activation(pT[:, 512:768], ps[0][0:104, 0:256], ACT.Copy).then_inc(pt_ready, 1)

            def a7(g):
                act.wait_ge(ot_done, g + 1)
                for c in range(2):
                    act.activation(fTa[:, 256 * c:256 * c + 256], ps[2][0:C, 256 * c:256 * c + 256], ACT.Identity,
                                   bias=small[:, 4 + c:5 + c]).then_inc(ot_ready, 1)

            def squares(g, s, ready):
                for t in range(GT):
                    act.wait_ge(*ready(t))
                    act.activation(u[:, t, :], zB[:, t, :], ACT.Square,
                                   accum_out=ms[s][:, t:t + 1]).then_inc(sq_ready[s], 1)

            def a8(g):
                if later(g):
                    act.wait_ge(mcopy_ready, g)
                    act.wait_ge(mt_done, g)
                squares(g, 0, lambda t: (z_ready[1], g + 1))

            def b1(g):
                act.wait_ge(ut_done, g + 1)
                for c in range(2):
                    act.activation(fTb[:, 256 * c:256 * c + 256], ps[4][0:C, 256 * c:256 * c + 256], ACT.Identity,
                                   scale=small[:, 6 + c:7 + c]).then_inc(ut_ready, 1)

            def b2(g):
                act.wait_ge(v2_done, g + 1)
                act.activation(v2.rearrange("p t n -> p (t n)"), ps[5][:, 0:GT * D], ACT.Copy).then_inc(v2_ready, 1)

            def b3(g):
                act.wait_ge(sub_ready[1], g + 1)
                act.activation(scb[0:104, :], scb[0:104, :], ACT.Exp, scale=HD2 ** -0.5).then_inc(exp_ready[1], 1)

            def b4(g):
                act.wait_ge(pads_set, 4)
                act.wait_ge(pt2_done, g * 2 + 1)
                for i in range(IPT):
                    rows = slice(32 * i, 32 * i + 32)
                    last = act.activation(pbd[rows, 0:2, :, i, :].rearrange("p g t n -> p (g t) n"),
                                          ps[6][rows, 0:4 * 104].rearrange("p (a n) -> p a n", a=4), ACT.Copy)
                last.then_inc(pbd_a, 1)

            def b5(g):
                act.wait_ge(pv2_done, g * 3 + 1)
                act.activation(ot2a[:, :, 0, :].rearrange("p r (i q) -> p r i q", i=IPT)[:, :, :, 0:S],
                               ps[4][:, 0:IPT * R * S].rearrange("p (i r q) -> p r i q", i=IPT, r=R),
                               ACT.Copy).then_inc(ot2_a, 1)
                act.wait_ge(pv2_done, g * 3 + 3)
                for t in range(GT):
                    last = act.activation(ot2b[:, :, t, :].rearrange("p r (i q) -> p r i q", i=IPT)[:, :, :, 0:S],
                                          ps[6][:, CT * t:CT * t + CT].rearrange("p (i r q) -> p r i q", i=IPT, r=2),
                                          ACT.Copy)
                last.then_inc(ot2_a, 1)

            def b6(g):
                squares(g, 1, lambda t: (x2_ready, g * 2 + (t + 1)))

            def b7(g):
                act.wait_ge(mt_done, g + 1)
                act.activation(fTb, ps[5][0:C, :], ACT.Copy).then_inc(mt_ready, 1)

            stages(act, [nothing, a2, a3, a4, a5, nothing, a7, a8], [b1, b2, b3, b4, b5, b6, b7, nothing])
            act.wait_ge(mcopy_ready, GROUPS)
            act.wait_ge(fill_set, 3)
            act.wait_ge(mt_done, GROUPS)
            act.activation(mall2[:, :, 0:D], mall[:, :, 0:D], ACT.Copy)
            act.activation(mall2[:, :, D + 1].bitcast(I32), const("number"), ACT.Copy).then_inc(twice, 1)
            act.wait_ge(gap_ready, 1)
            act.activation(eg[:, :], gap[:, :], ACT.Exp).then_inc(eg_ready, 1)

            def copy_x(j, b):
                act.wait_ge(xtr_done, j + 1)
                act.activation(xT[:, b, :], ps[6][0:C, 0:256], ACT.Copy).then_inc(xT_ready, 1)

            def silu(j, b):
                act.wait_ge(gate_done, j + 1)
                act.activation(sg[:, b, :], ps[b][:, 0:FF], ACT.Silu).then_inc(sg_ready, 1)

            def copy_h(j, b):
                act.wait_ge(htr_done, j + 1)
                act.activation(hT[:, b, :], ps[4][:, 0:FF], ACT.Copy).then_inc(hT_ready, 1)

            def step(j, b, prior=True):
                if prior:
                    copy_h(j - 1, 1 - b)
                silu(j, b)
                copy_x(j + 1, 1 - b)

            copy_x(0, 0)
            step(0, 0, prior=False)
            step(1, 1)
            act.wait_ge(eid_ready, 1)
            further = further_pairs(act)
            with act.Fori(1, SLOT_TILES // 2 + 1) as jj:
                with act.If(jj <= further):
                    step(jj * 2, 0)
                    step(jj * 2 + 1, 1)
                with act.If(jj == further + 1):
                    copy_h(jj * 2 - 1, 1)

        @block.vector
        def _(dve):
            def layer_stats(g, n, src, ready):
                for t in range(GT):
                    dve.wait_ge(ready, g + 1)
                    dve.bn_stats(st6[:, t, :], src[:, t, :]).then_inc(st_ready[n], 1)
                dve.wait_ge(st_ready[n], g * GT + GT)
                dve.tensor_tensor(mom[:, 0, :], st6[:, :, 1], st6[:, :, 4], ALU.add)
                dve.tensor_tensor(mom[:, 1, :], st6[:, :, 1], st6[:, :, 4], ALU.subtract)
                dve.tensor_tensor(mom[:, 2, :], st6[:, :, 2], st6[:, :, 5], ALU.add).then_inc(mom_ready[n], 1)
                dve.wait_ge(mom_ready[n], g * 2 + 1)
                dve.tensor_scalar(mean[:, :], mom[:, 0, :], 0.5, None, ALU.mult)
                dve.tensor_scalar(mom[:, 2, :], mom[:, 2, :], 1.0 / D, LN_EPS, ALU.mult, ALU.add)
                dve.scalar_tensor_tensor(mom[:, 3, :], mom[:, 1, :], 0.25, mom[:, 1, :],
                                         ALU.mult, ALU.mult).then_inc(mom_ready[n], 1)
                dve.wait_ge(mom_ready[n], g * 2 + 2)
                dve.tensor_tensor(ve[0][:, :], mom[:, 2, :], mom[:, 3, :], ALU.add).then_inc(ve_ready[n], 1)

            def normalise(g, n, src, to):
                dve.wait_ge(rs_ready[n], g + 1)
                for t in range(GT):
                    last = dve.tensor_scalar(to[:, t, :], src[:, t, :], mean[:, t:t + 1], rs[0][:, t:t + 1],
                                             ALU.subtract, ALU.mult)
                last.then_inc(z_ready[n], 1)

            def mean_square(g, n):
                s = n - 2
                dve.wait_ge(sq_ready[s], g * GT + GT)
                dve.tensor_scalar(ve[s][:, :], ms[s][:, :], 1.0 / D, RMS_EPS, ALU.mult, ALU.add)\
                   .then_inc(ve_ready[n], 1)
                dve.wait_ge(rs_ready[n], g + 1)

            def softmax(g, n, rows):
                mask = const("mask1" if n == 0 else "mask2", rows)
                s3 = sc[n][0:rows, :].rearrange("p (h k) -> p h k", k=S)
                for t in range(GT):
                    dve.wait_ge(s_done[n], g * GT + (t + 1))
                    bank = ps[(1 if n == 0 else 4) + t]
                    dve.tensor_tensor(s3[:, 12 * t:12 * t + 12, :],
                                      bank[0:rows, 0:12 * S].rearrange("p (h k) -> p h k", h=12),
                                      mask.unsqueeze(1).to_broadcast([rows, 12, S]), ALU.add).then_inc(sm_ready[n], 1)
                dve.wait_ge(sm_ready[n], g * GT + GT)
                dve.tensor_reduce(mx[n][0:rows, :], s3, AX.X, ALU.max).then_inc(max_ready[n], 1)
                dve.wait_ge(max_ready[n], g + 1)
                dve.tensor_tensor(s3, s3, mx[n][0:rows, :].unsqueeze(2).to_broadcast([rows, NR, S]),
                                  ALU.subtract).then_inc(sub_ready[n], 1)
                dve.wait_ge(exp_ready[n], g + 1)
                dve.tensor_reduce(sm[n][0:rows, :], s3, AX.X, ALU.add).then_inc(sum_ready[n], 1)
                dve.wait_ge(sum_ready[n], g + 1)
                dve.reciprocal(rc[n][0:rows, :], sm[n][0:rows, :]).then_inc(rc_ready[n], 1)
                dve.wait_ge(rc_ready[n], g + 1)

            dve.wait_ge(first_in, 16)
            dve.wait_ge(base_done, 1)
            dve.tensor_tensor(base[:, :], ps[0][:, 0:D], const("pos"), ALU.add).then_inc(base_ready, 1)
            dve.wait_ge(base_ready, 1)

            def a1(g):
                dve.wait_ge(patch_done, g * GT + GT)
                if later(g):
                    dve.wait_ge(h1_ready, g)
                dve.tensor_tensor(h, ps[0][:, 0:GT * D].rearrange("p (t n) -> p t n", t=GT),
                                  base[:, :].unsqueeze(1).to_broadcast([128, GT, D]), ALU.add).then_inc(h_ready, 1)
                layer_stats(g, 0, h, h_ready)
                normalise(g, 0, h, z)

            def a3(g):
                if not later(g):
                    dve.wait_ge(consts_in, 16)
                dve.wait_ge(v_done, g + 1)
                dve.tensor_copy(v1.rearrange("p t n -> p (t n)"), ps[0][:, 0:GT * D]).then_inc(v1_ready, 1)
                for c in range(2):
                    dve.wait_ge(k_ready, g * 2 + (c + 1))
                    last = dve.tensor_tensor(
                        kbd[:, c], k1[:, c].unsqueeze(2).to_broadcast([C, GI, HC, S]),
                        const("head_of_row", C).unsqueeze(1).unsqueeze(3).to_broadcast([C, GI, HC, S]), ALU.mult)
                last.then_inc(kbd_ready, 1)

            def a4(g):
                softmax(g, 0, 128)

            def a6(g):
                dve.wait_ge(o_done, g + 1)
                dve.tensor_tensor(o1.rearrange("p t (h d) -> p (t h) d", h=H1),
                                  ps[1][:, 0:GT * D].rearrange("p (h d) -> p h d", d=HD1),
                                  rc[0][:, :].unsqueeze(2).to_broadcast([128, NR, HD1]), ALU.mult).then_inc(o_ready, 1)

            def a8(g):
                if later(g):
                    dve.wait_ge(hsum_ready, g)
                dve.wait_ge(hb_ready, g + 1)
                dve.wait_ge(proj_done, g + 1)
                dve.tensor_tensor(hB, ps[3][:, 0:GT * D].rearrange("p (t n) -> p t n", t=GT), h,
                                  ALU.add).then_inc(h1_ready, 1)
                layer_stats(g, 1, hB, h1_ready)
                normalise(g, 1, hB, zB)
                mean_square(g, 2)
                for t in range(GT):
                    last = dve.tensor_scalar(u[:, t, :], zB[:, t, :], rs[0][:, t:t + 1], None, ALU.mult)
                last.then_inc(u_ready[0], 1)

            def b2(g):
                for n in range(5):
                    dve.wait_ge(eo_done, g * 5 + (n + 1))
                    if n >= 2:
                        dve.wait_ge(rope_add, g * 5 + (n - 1))
                    eo = ps[(6, 7, 4)[n % 3]][0:C, 0:2 * CT].rearrange("p (e i q) -> p e i q", e=2, i=GI)
                    turn = const("turn", C).rearrange("p (m e q) -> p m e q", m=2, e=2)
                    for m in range(2):
                        last = dve.tensor_tensor(tmp[:, n % 2, m], eo,
                                                 turn[:, m].unsqueeze(2).to_broadcast([C, 2, GI, S]), ALU.mult)
                    last.then_inc(rope_mul, 1)

            def b3(g):
                softmax(g, 1, 104)
                dve.wait_ge(pads_set, 4)
                for t in range(GT):
                    last = dve.tensor_tensor(
                        p2[:, t, :, :, 0:S],
                        scb[0:104, t * 12 * S:(t + 1) * 12 * S].rearrange("p (i g k) -> p g i k", i=IPT, g=G),
                        rc[1][0:104, 12 * t:12 * t + 12].rearrange("p (i g) -> p g i", i=IPT).unsqueeze(3)
                        .to_broadcast([104, G, IPT, S]), ALU.mult)
                last.then_inc(p2_ready, 1)

            def b4(g):
                dve.wait_ge(pt2_done, g * 2 + 2)
                for i in range(IPT):
                    rows = slice(32 * i, 32 * i + 32)
                    last = dve.tensor_copy(pbd[rows, 2, :, i, :], ps[7][rows, 0:2 * 104].rearrange("p (a n) -> p a n", a=2))
                last.then_inc(pbd_d, 1)

            def b5(g):
                dve.wait_ge(pv2_done, g * 3 + 2)
                dve.tensor_copy(ot2a[:, :, 1, :].rearrange("p r (i q) -> p r i q", i=IPT)[:, :, :, 0:S],
                                ps[5][:, 0:IPT * R * S].rearrange("p (i r q) -> p r i q", i=IPT, r=R)).then_inc(ot2_d, 1)

            def b6(g):
                for t in range(GT):
                    dve.wait_ge(wo_done, g * GT + (t + 1))
                    dve.tensor_tensor(zB[:, t, :], ps[(7, 4)[t]][:, 0:D], zB[:, t, :], ALU.add).then_inc(x2_ready, 1)
                mean_square(g, 3)
                for t in range(GT):
                    last = dve.scalar_tensor_tensor(u[:, t, :], zB[:, t, :], rs[1][:, t:t + 1], w2row,
                                                    ALU.mult, ALU.mult)
                last.then_inc(u_ready[1], 1)

            def b8(g):
                dve.wait_ge(lg_done, g + 1)
                dve.tensor_copy(lg[:, bass.ds(g * (GT * E), GT * E)], ps[6][:, 0:GT * E]).then_inc(lg_ready, 1)

            stages(dve, [a1, nothing, a3, a4, nothing, a6, nothing, a8], [nothing, b2, b3, b4, b5, b6, nothing, b8])

            done = [0]

            def then(ins):
                done[0] += 1
                ins.then_inc(r_dve, 1)
                dve.wait_ge(r_dve, done[0])

            dve.wait_ge(lg_ready, GROUPS)
            for t in range(TILES):
                last = dve.max(top[:, t, :], lg[:, t * E:(t + 1) * E])
            then(last)
            dve.tensor_tensor(gap[:, :], top[:, :, 1], top[:, :, 0], ALU.subtract).then_inc(gap_ready, 1)
            for t in range(TILES):
                last = dve.max_index(topi[:, t, :], top[:, t, :], lg[:, t * E:(t + 1) * E])
            then(last)
            then(dve.tensor_scalar(topf[:, :, :], topi[:, :, 0:2], const("unrouted"), None, ALU.add))
            for k in range(TOPK):
                last = dve.tensor_tensor(oh[k], const("iota").unsqueeze(1).to_broadcast([128, TILES, E]),
                                         topf[:, :, k].unsqueeze(2).to_broadcast([128, TILES, E]), ALU.is_equal)
            then(last)
            dve.tensor_tensor(ohs, oh[0], oh[1], ALU.add).then_inc(ohs_ready, 1)
            dve.wait_ge(eg_ready, 1)
            dve.wait_ge(mcopy_ready, GROUPS)
            then(dve.tensor_scalar(den[:, :], eg[:, :], 1.0, None, ALU.add))
            dve.reciprocal(mall[:, :, D], den[:, :]).then_inc(gates_set, 1)
            dve.wait_ge(gates_set, 1)
            dve.wait_ge(twice, 1)
            dve.tensor_tensor(mall2[:, :, D], eg[:, :], mall[:, :, D], ALU.mult).then_inc(gates_set, 1)
            then(dve.memset(cum[:, 0, :], 0.0))
            dve.wait_ge(ranks_done, 1)
            tot = ps[1][:, 0:W8].rearrange("p (t e) -> p t e", e=E)
            for t in range(1, TILES):
                then(dve.tensor_tensor(cum[:, t, :], tot[:, t - 1, :], cum[:, t - 1, :], ALU.add))
            then(dve.tensor_tensor(cnt[:, :], tot[:, TILES - 1, :], cum[:, TILES - 1, :], ALU.add))
            then(dve.tensor_tensor(over_step, cnt[:, :].unsqueeze(2).to_broadcast([128, E, MOST]),
                                   const("steps").unsqueeze(1).to_broadcast([128, E, MOST]), ALU.is_gt))
            then(dve.tensor_reduce(etl[:, :], over_step, AX.X, ALU.add))
            dve.tensor_tensor(rank, ps[0][:, 0:W8].rearrange("p (t e) -> p t e", e=E), cum, ALU.add)
            then(dve.tensor_tensor(lessed, etl[:, :].unsqueeze(1).to_broadcast([128, E, E]),
                                   const("less").rearrange("p (a b) -> p a b", a=E), ALU.mult))
            then(dve.tensor_reduce(est[:, :], lessed, AX.X, ALU.add))
            then(dve.scalar_tensor_tensor(rank, est[:, :].unsqueeze(1).to_broadcast([128, TILES, E]), 128.0, rank,
                                          ALU.mult, ALU.add))
            for k in range(TOPK):
                then(dve.tensor_tensor(pick[k], oh[k], rank, ALU.mult))
                then(dve.tensor_reduce(slot[k][:, :], pick[k], AX.X, ALU.add))
                dve.tensor_tensor(sidx[k][:, :], slot[k][:, :], const("trash1" if k == 0 else "trash2"),
                                  ALU.add).then_inc(idx_ready, 1)
            then(dve.tensor_tensor(een[:, :], est[:, :], etl[:, :], ALU.add))
            then(dve.tensor_tensor(le[:, :, :], een[0:1, :].unsqueeze(1).to_broadcast([1, SLOT_TILES, E]),
                                   const("slot_iota", 1).unsqueeze(2).to_broadcast([1, SLOT_TILES, E]), ALU.is_le))
            e0, e1 = ef[:, 0:SLOT_TILES], ef[:, SLOT_TILES:2 * SLOT_TILES]
            then(dve.tensor_reduce(e0, le[:, :, :], AX.X, ALU.add))
            then(dve.tensor_scalar(e0, e0, float(E - 1), None, ALU.min))
            then(dve.tensor_scalar(e1, e0, -1.0, float(E - 1), ALU.mult, ALU.add))
            then(dve.tensor_scalar(le[:, 0:SLOT_TILES // 2 - 1, 0], const("slot_iota", 1)[:, 1:SLOT_TILES // 2],
                                   2.0, None, ALU.mult))
            then(dve.tensor_scalar(le[:, 0:SLOT_TILES // 2 - 1, 1], le[:, 0:SLOT_TILES // 2 - 1, 0], een[0:1, E - 1:E], None,
                                   ALU.is_lt))
            then(dve.tensor_reduce(ef[:, 2 * SLOT_TILES:], le[:, 0:SLOT_TILES // 2 - 1, 1], AX.X, ALU.add))
            dve.tensor_copy(ei[:, 0:2 * SLOT_TILES + 1], ef[:, :]).then_inc(eid_ready, 1)
            dve.wait_ge(eid_ready, 1)
            further = further_pairs(dve)

            def keep(b, loads):
                dve.wait_ge(xs_in[b], loads)
                dve.tensor_copy(held_gate[:, b:b + 1], xin[:, b, D:D + 1])
                dve.tensor_copy(held_row[:, b:b + 1], xin[:, b, D + 1:W].bitcast(I32)).then_inc(kept, 1)

            def gated(j, b):
                dve.wait_ge(up_done, j + 1)
                dve.wait_ge(sg_ready, j + 1)
                dve.tensor_tensor(hh[:, b, :], ps[2 + b][:, 0:FF], sg[:, b, :], ALU.mult).then_inc(hh_ready, 1)

            def take(j, b):
                dve.wait_ge(kept, j + 1)
                if not isinstance(j, int):
                    dve.wait_ge(added, j * 16 - 16)
                dve.tensor_copy(gate[:, b:b + 1], held_gate[:, b:b + 1])
                dve.tensor_copy(row[:, b:b + 1], held_row[:, b:b + 1]).then_inc(taken, 1)

            def scaled_y(j, b):
                dve.wait_ge(y_done, j + 1)
                dve.wait_ge(taken, j + 1)
                dve.tensor_scalar(yo[:, b, :], ps[5][:, 0:D], gate[:, b:b + 1], None, ALU.mult).then_inc(y_ready, 1)

            keep(0, 16)
            keep(1, 16)
            gated(0, 0)
            take(0, 0)
            dve.wait_ge(taken, 1)
            keep(0, 32)
            gated(1, 1)
            scaled_y(0, 0)
            take(1, 1)
            with dve.Fori(1, SLOT_TILES // 2 + 1) as jj:
                with dve.If(jj <= further):
                    dve.wait_ge(taken, jj * 2)
                    keep(1, jj * 16 + 16)
                    gated(jj * 2, 0)
                    scaled_y(jj * 2 - 1, 1)
                    take(jj * 2, 0)
                    dve.wait_ge(taken, jj * 2 + 1)
                    keep(0, jj * 16 + 32)
                    gated(jj * 2 + 1, 1)
                    scaled_y(jj * 2, 0)
                    take(jj * 2 + 1, 1)
                with dve.If(jj == further + 1):
                    scaled_y(jj * 2 - 1, 1)

        @block.tensor
        def _(pe):
            mm = pe.matmul

            def turned(bank, src):
                for t in range(GT):
                    for c in range(2):
                        last = pe.transpose(ps[bank][0:C, 256 * c + 128 * t:256 * c + 128 * t + 128],
                                            src[:, t, C * c:C * c + C], eye)
                return last

            def real(fT, c):
                return fT[:, 256 * c:256 * c + 256].rearrange("p (i q) -> p i q", q=32)[:, :, 0:S]

            def a1(g):
                if later(g):
                    pe.wait_ge(pt_ready, g * 2)
                for t in range(GT):
                    pe.wait_ge(x_in[t], g * 16 + 16)
                    for k in range(PK):
                        last = mm(ps[0][:, D * t:D * t + D], xt[:, t, 128 * k:128 * k + 128], wpatch[:, k, :],
                                  start=(k == 0), stop=(k == PK - 1))
                    last.then_inc(patch_done, 1)

            def a2(g):
                pe.wait_ge(z_ready[0], g + 1)
                turned(1, z).then_inc(zt_done, 1)

            def a3(g):
                if not later(g):
                    pe.wait_ge(attn_w_in, 16)
                pe.wait_ge(zt_ready, g + 1)
                for c in range(2):
                    for k in range(2):
                        last = mm(ps[2][0:C, CT * c:CT * c + CT], wqkv1[:, k, D + C * c:D + C * c + C], real(fTa, k),
                                  start=(k == 0), stop=(k == 1))
                last.then_inc(k_done, 1)
                for t in range(GT):
                    for k in range(2):
                        last = mm(ps[0][:, D * t:D * t + D], fTa[:, 256 * k + 128 * t:256 * k + 128 * t + 128],
                                  wqkv1[:, k, 2 * D:3 * D], start=(k == 0), stop=(k == 1))
                last.then_inc(v_done, 1)
                if later(g):
                    pe.wait_ge(h1_ready, g)
                for c in range(2):
                    for k in range(2):
                        last = mm(ps[3][0:C, 256 * c:256 * c + 256], wqkv1[:, k, C * c:C * c + C],
                                  fTa[:, 256 * k:256 * k + 256], start=(k == 0), stop=(k == 1))
                last.then_inc(q_done, 1)

            def a4(g):
                pe.wait_ge(q_ready, g * 2 + 2)
                pe.wait_ge(kbd_ready, g + 1)
                for t in range(GT):
                    for i in range(IPT):
                        for c in range(2):
                            last = mm(ps[1 + t][32 * i:32 * i + 32, HC * S * c:HC * S * (c + 1)],
                                      q1[:, c, 128 * t + 32 * i:128 * t + 32 * i + 32],
                                      kbd[:, c, IPT * t + i].rearrange("p h k -> p (h k)"), start=True, stop=True,
                                      tile_position=(0, 32 * i))
                    last.then_inc(s_done[0], 1)

            def a5(g):
                pe.wait_ge(exp_ready[0], g + 1)
                pe.wait_ge(v1_ready, g + 1)
                for n in range(G):
                    for t in range(GT):
                        a = (12 * t + 4 * n) * S
                        last = pe.transpose(ps[(3, 3, 0)[n]][0:104, 256 * (n % 2) + 128 * t:256 * (n % 2) + 128 * t + 128],
                                            sca[:, a:a + 4 * S], eye)
                    if n:
                        last.then_inc(pt_done, 1)

            def a6(g):
                pe.wait_ge(pt_ready, g * 2 + 2)
                pe.wait_ge(vbd_ready, g + 1)
                for t in range(GT):
                    for i in range(IPT):
                        for n in range(G):
                            a = 256 * n + 128 * t + 32 * i
                            last = mm(ps[1][32 * i:32 * i + 32, D * t + 64 * n:D * t + 64 * n + 64], pT[:, a:a + 32],
                                      vbd[:, t, i, 64 * n:64 * n + 64], start=True, stop=True,
                                      tile_position=(0, 32 * i))
                last.then_inc(o_done, 1)

            def a7(g):
                pe.wait_ge(o_ready, g + 1)
                turned(2, o1).then_inc(ot_done, 1)

            def a8(g):
                pe.wait_ge(ot_ready, g * 2 + 2)
                for t in range(GT):
                    for k in range(2):
                        last = mm(ps[3][:, D * t:D * t + D], fTa[:, 256 * k + 128 * t:256 * k + 128 * t + 128],
                                  wproj[:, k, :], start=(k == 0), stop=(k == 1))
                last.then_inc(proj_done, 1)

            def b1(g):
                pe.wait_ge(u_ready[0], g + 1)
                turned(4, u).then_inc(ut_done, 1)

            def b2(g):
                pe.wait_ge(rest_w_in, 16)
                pe.wait_ge(ut_ready, g * 2 + 2)
                for t in range(GT):
                    for k in range(2):
                        last = mm(ps[5][:, D * t:D * t + D], fTb[:, 256 * k + 128 * t:256 * k + 128 * t + 128],
                                  wv2[:, k, :], start=(k == 0), stop=(k == 1))
                last.then_inc(v2_done, 1)
                if isinstance(g, int):
                    pe.wait_ge(lg_ready, g)
                for n in range(5):
                    if n >= 3:
                        pe.wait_ge(rope_mul, g * 5 + (n - 2))
                    for e in range(2):
                        for k in range(2):
                            last = mm(ps[(6, 7, 4)[n % 3]][0:C, CT * e:CT * e + CT], wqk2[:, k, (n + 4) % 5, e, :],
                                      real(fTb, k), start=(k == 0), stop=(k == 1))
                    last.then_inc(eo_done, 1)

            def b3(g):
                pe.wait_ge(rope_add, g * 5 + 5)
                pe.wait_ge(kbd2_ready, g + 1)
                pe.wait_ge(v2_ready, g + 1)
                for t in range(GT):
                    for i in range(IPT):
                        for e in range(2):
                            last = mm(ps[4 + t][0:104, G * S * i:G * S * (i + 1)],
                                      qr[:, e, IPT * t + i].rearrange("p r q -> p (r q)"),
                                      kbd2[:, e, IPT * t + i].rearrange("p g k -> p (g k)"),
                                      start=(e == 0), stop=(e == 1))
                    last.then_inc(s_done[1], 1)

            def b4(g):
                pe.wait_ge(p2_ready, g + 1)
                for n in range(G):
                    for t in range(GT):
                        a = (n % 2) * GT * 104 + 104 * t
                        last = pe.transpose(ps[(6, 6, 7)[n]][:, a:a + 104], p2[:, t, n].rearrange("p i k -> p (i k)"),
                                            eye[0:104, 0:104])
                    if n:
                        last.then_inc(pt2_done, 1)

            def b5(g):
                pe.wait_ge(pbd_a, g + 1)
                pe.wait_ge(pbd_d, g + 1)
                for t in range(GT):
                    for n in range(2):
                        last = mm(ps[4 + t][64 * n:64 * n + 64, 0:IPT * R * S], v2[:, t, 64 * n:64 * n + 64],
                                  pbd[:, n, t].rearrange("p i n -> p (i n)"), start=True, stop=True,
                                  tile_position=(0, 64 * n))
                    last.then_inc(pv2_done, 1)
                for t in range(GT):
                    for odd in range(2):
                        last = mm(ps[6][64 * odd:64 * odd + 64, CT * t:CT * t + CT], v2[:, t, 128:192],
                                  pbd[:, 2, t].rearrange("p i (r o q) -> p i r o q", r=2, o=2)[:, :, :, odd, :],
                                  start=True, stop=True, tile_position=(0, 64 * odd))
                last.then_inc(pv2_done, 1)

            def b6(g):
                pe.wait_ge(ot2_a, g * 2 + 2)
                pe.wait_ge(ot2_d, g + 1)
                for t in range(GT):
                    for k in range(6):
                        last = mm(ps[(7, 4)[t]][:, 0:D], ot2a[:, k, t, :] if k < R else ot2b[:, k - R, t, :],
                                  wout[:, k, :], start=(k == 0), stop=(k == 5))
                    last.then_inc(wo_done, 1)

            def b7(g):
                pe.wait_ge(u_ready[1], g + 1)
                turned(5, u).then_inc(mt_done, 1)

            def b8(g):
                pe.wait_ge(mt_ready, g + 1)
                for t in range(GT):
                    for k in range(2):
                        last = mm(ps[6][:, E * t:E * t + E], fTb[:, 256 * k + 128 * t:256 * k + 128 * t + 128],
                                  wr[:, k, :], start=(k == 0), stop=(k == 1))
                last.then_inc(lg_done, 1)

            pe.wait_ge(first_in, 16)
            pe.wait_ge(patch_w_in, 16)
            mm(ps[0][:, 0:D], const("who", 2), bcls, start=True, stop=True).then_inc(base_done, 1)
            pe.wait_ge(base_ready, 1)
            stages(pe, [a1, a2, a3, a4, a5, a6, a7, a8], [b1, b2, b3, b4, b5, b6, b7, b8])

            pe.wait_ge(ohs_ready, 1)
            flat = rt[:, 2 * W8:3 * W8]
            mm(ps[0][:, 0:W8], const("before"), flat, start=True, stop=True)
            mm(ps[1][:, 0:W8], const("ones"), flat, start=True, stop=True).then_inc(ranks_done, 1)

            def x_turn(b, loads):
                pe.wait_ge(xs_in[b], loads)
                for c in range(2):
                    last = pe.transpose(ps[6][0:C, 128 * c:128 * c + 128], xin[:, b, C * c:C * c + C], eye)
                last.then_inc(xtr_done, 1)

            def gate_or_up(j, b, e, half, done):
                for k in range(2):
                    last = mm(ps[2 * half + b][:, 0:FF], xT[:, b, 128 * k:128 * k + 128],
                              big[0:C, bass.ds(e * (4 * FF) + (GU0 + 2 * FF * k + FF * half), FF)],
                              start=(k == 0), stop=(k == 1))
                last.then_inc(done, 1)

            def h_turn(j, b):
                pe.wait_ge(hh_ready, j + 1)
                for k in range(3):
                    last = pe.transpose(ps[4][:, 128 * k:128 * k + 128], hh[:, b, 128 * k:128 * k + 128], eye)
                last.then_inc(htr_done, 1)

            def down(j, b, first=False):
                e = pe.value_load(ei[0:1, bass.ds(j, 1)], min_val=0, max_val=E - 1)
                pe.wait_ge(hT_ready, j + 1)
                if not first:
                    pe.wait_ge(y_ready, j)
                for k in range(3):
                    last = mm(ps[5][:, 0:D], hT[:, b, 128 * k:128 * k + 128],
                              big[:, bass.ds(e * (3 * D) + D * k, D)], start=(k == 0), stop=(k == 2))
                last.then_inc(y_done, 1)

            def step(j, b, loads, prior=True, first=False):
                e = pe.value_load(ei[0:1, bass.ds(j + SLOT_TILES, 1)], min_val=0, max_val=E - 1)
                if prior:
                    h_turn(j - 1, 1 - b)
                pe.wait_ge(xT_ready, j + 1)
                gate_or_up(j, b, e, 0, gate_done)
                x_turn(1 - b, loads)
                gate_or_up(j, b, e, 1, up_done)
                if prior:
                    down(j - 1, 1 - b, first)

            pe.wait_ge(eid_ready, 1)
            further = further_pairs(pe)
            x_turn(0, 16)
            pe.wait_ge(early_in, 16 * 7)
            pe.wait_ge(late_in, 16 * 5)
            step(0, 0, 16, prior=False)
            step(1, 1, 32, first=True)
            with pe.Fori(1, SLOT_TILES // 2 + 1) as jj:
                with pe.If(jj <= further):
                    step(jj * 2, 0, jj * 16 + 16)
                    step(jj * 2 + 1, 1, jj * 16 + 32)
                with pe.If(jj == further + 1):
                    h_turn(jj * 2 - 1, 1)
                    down(jj * 2 - 1, 1)


def table_of_constants():
    t = np.zeros((128, NCONST), np.float32)

    def put(name, a):
        a = np.asarray(a, np.float32)
        at, w = _C[name]
        t[:a.shape[0], at:at + w] = a.reshape(a.shape[0], w)

    row = np.arange(128)
    q = row % 32
    j = np.arange(D)
    i = np.arange(S - 1, dtype=np.float32)[:, None]
    angle = i / np.power(np.float32(10000.0), ((2 * (j // 2)).astype(np.float32) / np.float32(D)))
    pos = np.sin(angle + np.where(j % 2 == 1, np.float32(np.pi / 2), np.float32(0.0)).astype(np.float32))
    full = np.zeros((128, D), np.float32)
    for b in range(IPT):
        full[32 * b + 1:32 * b + S] = pos
    put("pos", full)
    key = np.arange(S)[None, :]
    put("mask1", np.where(key <= q[:, None], 0.0, MASKED))
    put("mask2", np.where(key <= (row[:104] % S)[:, None], 0.0, MASKED))
    put("head_of_row", row[:C, None] // HD1 == np.arange(HC))
    put("head_of_key", row[:104, None] // S == np.arange(4))
    put("group_of_row", row[:C, None] // J == np.arange(G))
    inv = (1.0 / np.power(np.float32(10000.0), np.arange(0, HD2, 2, dtype=np.float32) / np.float32(HD2))).astype(np.float32)
    f = np.arange(S, dtype=np.float32)[None, :] * inv[row[:C] % J][:, None]
    put("turn", np.stack([np.cos(f), -np.sin(f), np.sin(f), np.cos(f)], 1))
    put("eye", np.eye(128))
    put("before", row[:, None] < row[None, :])
    put("ones", np.ones((128, 128)))
    put("unrouted", (99.0 * (q >= S))[:, None])
    trash = np.zeros((128, TILES))
    pads = np.flatnonzero(q >= S)
    trash[pads, :] = SLOTS + np.arange(len(pads) * TILES).reshape(len(pads), TILES)
    put("trash1", trash)
    put("trash2", np.where(trash > 0, trash + PADS, 0))
    put("steps", np.broadcast_to(128.0 * np.arange(MOST), (128, MOST)))
    less = (np.arange(E)[None, :] < np.arange(E)[:, None]).reshape(1, -1)
    put("less", np.broadcast_to(less, (128, E * E)))
    put("iota", np.broadcast_to(np.arange(E), (128, E)))
    put("slot_iota", np.broadcast_to(np.arange(SLOT_TILES), (128, SLOT_TILES)))
    put("neghalf", np.full((128, GT), -0.5))
    put("who", np.stack([(q >= 1) & (q < S), q == 0]))
    put("number", np.arange(TILES)[None, :] * IPT * S + ((row // 32) * S + np.minimum(q, S - 1))[:, None])
    put("spare", (TOKENS + row)[:, None])
    return t


def kernel(x, cls_tok, L0_tok_W, L0_tok_b, L0_attn_W_attn, L0_attn_b_attn, L0_attn_W_proj, L0_attn_b_proj,
           L0_ffn_norm1_w, L0_ffn_w_qkv, L0_ffn_w_out, L0_ffn_norm2_w, L0_ffn_w_router, L0_ffn_w_gate_up,
           L0_ffn_w_down):
    import concourse.bacc as bacc
    from concourse.bass_utils import run_bass_kernel_spmd

    f = lambda a: np.asarray(a, np.float32)
    edge = GRID * PATCH
    p = f(x)[:, :, :edge, :edge].reshape(IMAGES, CH, GRID, PATCH, GRID, PATCH).transpose(1, 3, 5, 0, 2, 4)
    padded = np.zeros((PK * 128, IMAGES, 32), np.float32)
    padded[:, :, 1:S] = p.reshape(PK * 128, IMAGES, S - 1)
    xp = padded.reshape(PK, 128, TILES, 128).transpose(2, 1, 0, 3).reshape(TILES, 128, PK * 128)

    fw = np.zeros((128, NFRONT), np.float32)

    def put(name, a):
        at, w = _F[name]
        fw[:a.shape[0], at:at + w] = a.reshape(a.shape[0], w)

    def chunks(a, n):
        return a.reshape(n, a.shape[0] // n, -1).transpose(1, 0, 2)

    put("wpatch", chunks(f(L0_tok_W).reshape(D, -1).T, PK))
    put("wqkv1", chunks(f(L0_attn_W_attn), 2))
    put("wproj", chunks(f(L0_attn_W_proj), 2))
    wq = f(L0_ffn_w_qkv)
    q = wq[:, :G * R * HD2].reshape(D, G, R, J, 2).transpose(0, 2, 4, 1, 3)
    k = wq[:, G * R * HD2:G * (R + 1) * HD2].reshape(D, G, J, 2).transpose(0, 3, 1, 2)[:, None]
    put("wqk2", chunks(np.concatenate([q, k], 1).reshape(D, -1), 2))
    put("wv2", chunks(wq[:, G * (R + 1) * HD2:], 2))
    wo = f(L0_ffn_w_out).reshape(G * R, HD2, D)
    put("wout", np.stack([wo[[r, R + r]].reshape(128, D) for r in range(R)]
                         + [wo[8 + 2 * r:10 + 2 * r].reshape(128, D) for r in range(2)], 1))
    put("wr", chunks(f(L0_ffn_w_router), 2))
    put("w2row", np.broadcast_to(f(L0_ffn_norm2_w)[None], (128, D)))
    cols = np.concatenate([f(L0_attn_b_attn).reshape(6, C), f(L0_ffn_norm1_w).reshape(2, C)]).T
    at = _F["small"][0]
    fw[:C, at:at + 8] = cols
    at = _F["bcls"][0]
    fw[0, at:at + D] = f(L0_tok_b)
    fw[1, at:at + D] = f(cls_tok).reshape(D)
    put("bprow", np.broadcast_to(f(L0_attn_b_proj)[None], (128, D)))

    wgu = f(L0_ffn_w_gate_up).reshape(E, 2, C, 2 * FF)[::-1].transpose(2, 0, 1, 3).reshape(C, -1)
    wdn = f(L0_ffn_w_down).reshape(E, 3, 128, D).transpose(2, 0, 1, 3).reshape(128, -1)
    arrays = {"xp": xp, "fw": fw, "cst": table_of_constants(), "wgu": wgu, "wdn": wdn}
    arrays = {n: np.ascontiguousarray(a) for n, a in arrays.items()}

    nc = bacc.Bacc("TRN2", target_bir_lowering=False, num_devices=1)
    args = [nc.dram_tensor(n, a.shape, F32, kind="ExternalInput").ap() for n, a in arrays.items()]
    xs = nc.dram_tensor("slot_inputs", (XS_TILES * 128, W), F32, kind="Internal").ap()
    out = nc.dram_tensor("out", (TOKENS + 128, D), F32, kind="ExternalOutput").ap()
    build_tower(nc, *args, xs, out)
    r = run_bass_kernel_spmd(nc, [arrays], core_ids=[0])
    return r.results[0]["out"][:TOKENS].reshape(IMAGES, S, D)
```

```python
from contextlib import ExitStack

import numpy as np

import concourse.bass as bass
from concourse import mybir

F32 = mybir.dt.float32
I32 = mybir.dt.int32
U32 = mybir.dt.uint32
ALU = mybir.AluOpType
ACT = mybir.ActivationFunctionType
AX = mybir.AxisListType

IMAGES, CH, SIDE, PATCH = 32, 3, 84, 16
GRID = SIDE // PATCH
S = GRID * GRID + 1
D = 192
C = 96
PK = CH * PATCH * PATCH // 128
IPT = 4
TILES = IMAGES // IPT
GT = 2
GROUPS = TILES // GT
GI = GT * IPT
CT = GI * S
H1, HD1 = 12, 16
HC = C // HD1
G, R, HD2 = 3, 4, 64
J = HD2 // 2
E, FF, TOPK = 16, 384, 2
TOKENS = IMAGES * S
SLOT_TILES = (TOPK * TOKENS + E * 127) // 128
PADS = (32 - S) * IPT * TILES
MOST = (TOKENS + 127) // 128
TABLE_TILES = E * MOST + 1 + (TOPK * PADS + 127) // 128
LISTED = SLOT_TILES + 5
RT = TILES // 2
RANKS = 512 - 2 * RT * E
LATE_PARTS = 8
LATE_CUTS = (0, 12, 18, 24)
LN_EPS, RMS_EPS, MASKED = 1e-5, 1e-6, -1e30

PHASES, A_FIRST = 8, 3
LEAD = (("A", 0), ("B", 0), ("B", 1), ("B", 2))
FOLLOW = (("A", 1), ("A", 2), ("A", 3), ("B", 3))

_C = {}
_n = 0
for _name, _w in (("pos", D), ("who", 128), ("eye", 128), ("neghalf", GT), ("number", TILES), ("spare", TABLE_TILES),
                  ("mask1", S), ("mask2", S), ("head_of_row", HC), 
                  ("group_of_row", G), ("turn", 4 * S), ("before", 128), ("ones", 128),
                  ("unrouted", 1), ("trash", TOPK * TILES), ("expert_slots", E), ("steps", MOST), ("less", E * E),
                  ("iota", E), ("tile_iota", LISTED),
                  ("even_tiles", SLOT_TILES // 2 - 1)):
    _C[_name] = (_n, _w)
    _n += _w
NCONST = _n
NFIRST = _C["mask1"][0]

_F = {}
_n = 0
for _name, _w in (("bcls", D), ("wpatch", PK * D), ("wqkv1", 2 * 3 * D), ("wproj", 2 * D), ("small", 16),
                  ("bprow", D), ("wqk2", 2 * 5 * 2 * C), ("wv2", 2 * D), ("wout", 6 * D), ("wr", 2 * E),
                  ("w2row", D)):
    _F[_name] = (_n, _w)
    _n += _w
NFRONT = _n
GU0 = E * 3 * D


class Buffers:
    pass


def build_tower(nc, xp, fw, cst, wgu, wdn, moe_in, slots, out):
    ctx = ExitStack()
    with ctx:
        def sb(name, shape, dt=F32):
            return ctx.enter_context(nc.sbuf_tensor(name, shape, dt))

        def sem(name):
            return ctx.enter_context(nc.semaphore(name))

        big = sb("experts", [128, E * (3 * D + 4 * FF)])
        front = sb("front", [128, NFRONT])
        ct = sb("constants", [128, NCONST])
        xt = sb("patches", [128, 2, PK * 128])
        base = sb("embedding_base", [128, D])
        probs2 = sb("probs2", [104, GT * G * IPT * 32])
        by_key = sb("probs2_by_key", [128, G * GT * IPT * R * S])
        attended2 = sb("attended2", [128, (R + 2) * GT * 128])
        hsum = sb("residual", [128, TILES, D])
        lg = sb("logits", [128, TILES * E])
        zeros = sb("zeros", [128, D])
        empty = sb("empty_slots", [128, TABLE_TILES, 2])
        st6 = sb("stats", [128, GT, 6])
        mom = sb("moments", [128, 4, GT])
        mean = sb("mean", [128, GT])
        ve = [sb("variance_a", [128, GT]), sb("variance_b", [128, GT])]
        rs = [sb("rstd_a", [128, GT]), sb("rstd_b", [128, GT])]
        ms = [sb("meansq_a", [128, GT]), sb("meansq_b", [128, GT])]
        NR = 12 * GT
        mx = [sb("rowmax_a", [128, NR]), sb("rowmax_b", [128, NR])]
        sm = [sb("rowsum_a", [128, NR]), sb("rowsum_b", [128, NR])]
        rc = [sb("rowrecip_a", [128, NR]), sb("rowrecip_b", [128, NR])]
        ps = [ctx.enter_context(nc.psum_tensor(f"bank{i}", [128, 512], F32)) for i in range(8)]

        def const(name, rows=128):
            a, w = _C[name]
            return ct[0:rows, a:a + w]

        def fview(name, rows=128):
            a, w = _F[name]
            return front[0:rows, a:a + w]

        eye = const("eye")
        wpatch = fview("wpatch").rearrange("p (k n) -> p k n", k=PK)
        wqkv1 = fview("wqkv1", C).rearrange("p (c n) -> p c n", c=2)
        wproj = fview("wproj", C).rearrange("p (c n) -> p c n", c=2)
        wqk2 = fview("wqk2", C).rearrange("p (c s e n) -> p c s e n", c=2, s=5, e=2)
        wv2 = fview("wv2", C).rearrange("p (c n) -> p c n", c=2)
        wout = fview("wout").rearrange("p (k n) -> p k n", k=6)
        wr = fview("wr", C).rearrange("p (c n) -> p c n", c=2)
        w2row = fview("w2row")
        bprow = fview("bprow")
        small = fview("small", C)
        bcls = fview("bcls", 2)

        arena_end = GU0 + (E // 2) * 4 * FF
        arena0 = (E // 2) * 3 * D
        at = [arena0]

        def carve(n, rows=128):
            a = at[0]
            at[0] += n
            assert at[0] <= arena_end
            return big[0:rows, a:a + n]

        def tokens(n=D):
            return carve(GT * n).rearrange("p (t n) -> p t n", t=GT)

        hand = [(tokens(), tokens(), tokens()) for _ in range(2)]

        def of_group(g, s):
            w = Buffers()
            w.s, w.ps = s, ps[4 * s:4 * s + 4]
            w.hB, w.zB, w.u = hand[g % 2]
            at[0] = (set0, set1)[s]
            return w

        def stage_a(g, s, values):
            w = of_group(g, s)
            w.h, w.z = tokens(), tokens()
            w.o1 = w.z
            w.fTa = carve(2 * GT * 128, C)
            w.q1 = carve(2 * GT * 128, C).rearrange("p (c n) -> p c n", c=2)
            w.k1 = carve(2 * CT, C).rearrange("p (c i k) -> p c i k", c=2, k=S)
            w.kbd = carve(2 * GI * HC * S, C).rearrange("p (c i h k) -> p c i h k", c=2, i=GI, h=HC)
            w.vbd = (carve(GI * D) if values is None else values[:, 0:GI * D])\
                .rearrange("p (t i g r d) -> p t i g r d", t=GT, i=IPT, g=G, r=4)
            w.scp = carve(NR * 32)
            w.s3 = w.scp.rearrange("p (h k) -> p h k", k=32)[:, :, 0:S]
            w.pT = carve(G * GT * 128)
            return w

        def stage_b(g, s, probs, keyed, attended):
            w = of_group(g, s)
            w.fTb = carve(2 * GT * 128, C)
            w.qr = carve(2 * R * CT, C).rearrange("p (e i r q) -> p e i r q", e=2, i=GI, r=R)
            w.tmp = carve(2 * 4 * CT, C).rearrange("p (b m e i q) -> p b m e i q", b=2, m=2, e=2, q=S)
            w.kr = carve(2 * CT, C).rearrange("p (e i k) -> p e i k", e=2, k=S)
            w.kbd2 = carve(2 * GI * G * S, C).rearrange("p (e i g k) -> p e i g k", e=2, i=GI, g=G)
            w.v2 = tokens()
            w.sc = carve(NR * S)
            w.s3 = w.sc[0:104, :].rearrange("p (h k) -> p h k", k=S)
            w.p2 = (carve(GT * G * IPT * 32, 104) if probs is None else probs[0:104, :])\
                .rearrange("p (t g i k) -> p t g i k", t=GT, g=G, i=IPT)
            w.pbd = keyed[:, 0:G * GT * CT * 2].rearrange("p (g t i n) -> p g t i n", g=G, t=GT, i=IPT)
            n = GT * 128
            w.ot2a = attended[:, 0:R * n].rearrange("p (r t n) -> p r t n", r=R, t=GT)
            w.ot2b = attended[:, R * n:(R + 2) * n].rearrange("p (r t n) -> p r t n", r=2, t=GT)
            return w

        xt_flat = xt[:, :, :].rearrange("p b n -> p (b n)")

        def patches(n):
            if n in (2, 3):
                return attended2[:, (n - 2) * PK * 128:(n - 1) * PK * 128]
            return xt[:, n % 2, :]

        set0 = set1 = at[0]
        A = [stage_a(g, 0, None) for g in range(1, GROUPS)]
        set1 = at[0]
        A = [stage_a(0, 1, by_key[:, :])] + A
        B = [stage_b(g, 1, probs2[:, :], by_key[:, :], attended2[:, :]) for g in range(GROUPS - 1)]
        B += [stage_b(3, 0, None, front[:, _F["wpatch"][0]:_F["small"][0]], xt_flat)]
        assert at[0] <= set1

        at = [0]

        def over(n, rows=128):
            a = at[0]
            at[0] += n
            assert at[0] <= NFRONT
            return front[0:rows, a:a + n]

        tb = over(2 * 2).rearrange("p (b n) -> p b n", b=2)
        xin = over(2 * D).rearrange("p (b n) -> p b n", b=2)
        xT = over(2 * 2 * 128, C).rearrange("p (b n) -> p b n", b=2)
        sg = over(2 * FF).rearrange("p (b n) -> p b n", b=2)
        hh = over(2 * FF).rearrange("p (b n) -> p b n", b=2)
        hT = over(2 * FF).rearrange("p (b n) -> p b n", b=2)
        yo = over(2 * D).rearrange("p (b n) -> p b n", b=2)

        top = sb("top", [128, TILES, 8])
        topi = sb("topi", [128, TILES, 8], U32)
        topf = sb("topf", [128, TOPK, RT])
        gap = sb("gap", [128, RT])
        eg = sb("expgap", [128, RT])
        den = sb("den", [128, RT])
        oh = sb("one_hot", [128, TOPK, RT, E])
        ohs = sb("one_hot_sum", [128, RT, E])
        cum = sb("cumulated", [128, TILES + 1, E])
        ranks = sb("ranks_in_tile", [128, 2 * RT * E])
        rank = sb("rank", [128, RT * E])
        pick = sb("picked", [128, TOPK, RT * E])
        slot = sb("slot", [128, TOPK * RT])
        sidx = sb("slot_index", [128, TOPK, TILES], I32)
        pay = sb("slot_contents", [128, TOPK, TILES, 2])
        at = [0]

        def wide(n, rows=128):
            a = at[0]
            at[0] += n
            assert at[0] <= 2 * PK * 128
            return xt_flat[0:rows, a:a + n]

        over_step = wide(E * MOST).rearrange("p (e m) -> p e m", e=E)
        lessed = wide(E * E).rearrange("p (e f) -> p e f", e=E)
        le = wide(LISTED * E, 1).rearrange("p (j e) -> p j e", e=E)
        skip = wide(LISTED * E, 1).rearrange("p (j e) -> p j e", e=E)
        cnt = sb("count", [128, E])
        etl = sb("expert_tiles", [128, E])
        est = sb("expert_start", [128, E])
        een = sb("expert_end", [128, E])
        spare = sb("expert_spare_tiles", [128, E])
        held_gate = sb("held_gate", [128, 2])
        held_row = sb("held_row", [128, 2], I32)
        gate = sb("gate", [128, 2])
        row = sb("row", [128, 2], I32)
        ef = sb("lists_f", [1, 3 * LISTED + 1])
        ei = sb("lists", [1, 3 * LISTED + 1], I32)

        first_in, consts_in, late_in, early_in = sem("first_in"), sem("consts_in"), sem("late_in"), sem("early_in")
        bias_in = sem("bias_in")
        patch_w_in, attn_w_in, rest_w_in = sem("patch_w_in"), sem("attn_w_in"), sem("rest_w_in")
        x_in = [sem(f"x_in{n}") for n in range(4)]
        pads_a = sem("pads_a")
        pads_set, fill_set, filled = sem("pads_set"), sem("fill_set"), sem("filled")
        base_done, base_ready = sem("base_done"), sem("base_ready")
        patch_done = sem("patch_done")
        h_ready, hb_ready = sem("h_ready"), sem("hb_ready")
        st_ready = [sem("st_ready_a"), sem("st_ready_b")]
        mom_ready = [sem("mom_ready_a"), sem("mom_ready_b")]
        ve_ready = [sem(f"ve_ready_{n}") for n in range(4)]
        rs_ready = [sem(f"rs_ready_{n}") for n in range(4)]
        z_ready = [sem("z_ready_a"), sem("z_ready_b")]
        zt_done, zt_ready = sem("zt_done"), sem("zt_ready")
        k_done, q_done, k_ready, q_ready = sem("k_done"), sem("q_done"), sem("k_ready"), sem("q_ready")
        v_done, v_a, v_d = sem("v_done"), sem("v_a"), sem("v_d")
        kbd_ready = sem("kbd_ready")
        s_done = [sem("s_done_a"), sem("s_done_b")]
        sm_ready = [sem("sm_ready_a"), sem("sm_ready_b")]
        max_ready = [sem("max_ready_a"), sem("max_ready_b")]
        sub_ready = [sem("sub_ready_a"), sem("sub_ready_b")]
        exp_ready = [sem("exp_ready_a"), sem("exp_ready_b")]
        sum_ready = [sem("sum_ready_a"), sem("sum_ready_b")]
        rc_ready = [sem("rc_ready_a"), sem("rc_ready_b")]
        pt_done, pt_ready = sem("pt_done"), sem("pt_ready")
        o_done, o_ready = sem("o_done"), sem("o_ready")
        ot_done, ot_ready = sem("ot_done"), sem("ot_ready")
        proj_done, h1_ready = sem("proj_done"), sem("h1_ready")
        sq_ready = [sem("sq_ready_a"), sem("sq_ready_b")]
        u_ready = [sem("u_ready_a"), sem("u_ready_b")]
        ut_done, ut_ready = sem("ut_done"), sem("ut_ready")
        v2_done, v2_ready = sem("v2_done"), sem("v2_ready")
        eo_done = sem("eo_done")
        rope_mul, rope_add = sem("rope_mul"), sem("rope_add")
        kbd2_ready = sem("kbd2_ready")
        p2_ready = sem("p2_ready")
        pt2_done, pbd_a, pbd_d = sem("pt2_done"), sem("pbd_a"), sem("pbd_d")
        pv2_done = sem("pv2_done")
        ot2_a, ot2_d = sem("ot2_a"), sem("ot2_d")
        wo_done, x2_ready = sem("wo_done"), sem("x2_ready")
        hsum_ready = sem("hsum_ready")
        tokens_out = [sem("tokens_out0"), sem("tokens_out1")]
        mt_done, mt_ready = sem("mt_done"), sem("mt_ready")
        lg_done, lg_ready = sem("lg_done"), sem("lg_ready")
        r_dve, gap_ready, eg_ready = sem("r_dve"), sem("gap_ready"), sem("eg_ready")
        ohs_ready, ranks_done, ranks_read = sem("ohs_ready"), sem("ranks_done"), sem("ranks_read")
        gates_set, idx_ready, eid_ready = sem("gates_set"), sem("idx_ready"), sem("eid_ready")
        scattered, res_out = sem("scattered"), sem("res_out")
        tb_in = [sem("tb_in0"), sem("tb_in1")]
        gathered = [sem("gathered0"), sem("gathered1")]
        xtr_done, xT_ready = sem("xtr_done"), sem("xT_ready")
        gate_done, up_done, sg_ready, hh_ready = sem("gate_done"), sem("up_done"), sem("sg_ready"), sem("hh_ready")
        htr_done, hT_ready, y_done, y_ready = sem("htr_done"), sem("hT_ready"), sem("y_done"), sem("y_ready")
        zeros_out = sem("zeros_out")
        kept, taken = sem("kept"), sem("taken")
        moving, added = sem("moving"), sem("added")

        block = ctx.enter_context(nc.Block())

        def further_pairs(eng):
            return eng.value_load(ei[0:1, 3 * LISTED:3 * LISTED + 1], min_val=0, max_val=SLOT_TILES // 2 - 1)

        def spread_values(copy, w, images, done):
            for i in images:
                for r in range(4):
                    last = copy(w.vbd[32 * r:32 * r + 32, :, i, :, r, :],
                                w.ps[0][32 * i:32 * i + 32, 0:GT * D]
                                .rearrange("p (t g r d) -> p t g r d", t=GT, g=G, r=4)[:, :, :, r, :])
            last.then_inc(done, 1)

        def stages(a_phases, b_phases, routing):
            phases = {"A": a_phases, "B": b_phases}
            for (stage, g), (other, other_g) in zip(LEAD, FOLLOW):
                for n in range(1, PHASES + 1):
                    turn = [(stage, g), (other, other_g)]
                    if stage == "B" and other == "A" and n == A_FIRST:
                        turn.reverse()
                    for what, group in turn:
                        phases[what][n - 1](group)
                        if (what, group) == LEAD[-1] and n in routing:
                            routing[n](0)

        def nothing(g):
            pass

        @block.sync
        def _(sp):
            def load_x(n):
                if n >= 4:
                    sp.wait_ge(patch_done, n - 1 if n >= 6 else n - 3)
                sp.dma_start(patches(n), xp[n]).then_inc(x_in[n % 4], 16)

            def load_front(name, last, done):
                a, b = _F[name][0], sum(_F[last])
                sp.dma_start(front[:, a:b], fw[:, a:b]).then_inc(done, 16)

            load_x(0)
            load_front("bcls", "wpatch", patch_w_in)
            load_x(1)
            load_x(2)
            load_x(3)
            load_front("wqkv1", "small", attn_w_in)
            load_front("bprow", "bprow", bias_in)
            lo = (E // 2) * 4 * FF
            real_rows = moe_in[0:TOKENS, :].rearrange("(t i q) n -> i q t n", i=IPT, q=S)

            def tokens_to_dram(g):
                sp.wait_ge(u_ready[1], g + 1)
                for i in range(IPT):
                    sp.dma_start(real_rows[i][:, g * GT:g * GT + GT, :],
                                 B[g].u[32 * i:32 * i + S, :, :]).then_inc(tokens_out[g % 2], 16)

            for g in range(GROUPS):
                sp.wait_ge(v_done, g + 1)
                if g == 0:
                    continue
                if g < 3:
                    load_x(2 * g + 2)
                    load_x(2 * g + 3)
                if g == 1:
                    load_front("wqk2", "w2row", rest_w_in)
                    sp.wait_ge(fill_set, 3)
                    sp.dma_start(slots.rearrange("(p a) n -> p (a n)", p=128),
                                 empty[:, :, :].rearrange("p a n -> p (a n)")).then_inc(filled, 16)
                    sp.dma_start(moe_in[TOKENS:TOKENS + 128, :], zeros[:, :]).then_inc(zeros_out, 16)
                    sp.dma_start(out[TOKENS:TOKENS + 128, :], zeros[:, :]).then_inc(zeros_out, 16)
                if g == 1:
                    sp.dma_start(big[:, 0:arena0], wdn[:, 0:arena0]).then_inc(early_in, 16)
                for part in ((), (0, 1), (2, 3), (4, 5))[g]:
                    a, w = lo + part * (lo // 6), lo // 6
                    sp.dma_start(big[0:C, GU0 + a:GU0 + a + w], wgu[:, a:a + w]).then_inc(early_in, 16)
                if g == 2:
                    tokens_to_dram(0)
            for g in range(1, GROUPS):
                tokens_to_dram(g)
            dst = out[0:TOKENS, :].rearrange("(t i q) n -> i q t n", i=IPT, q=S)
            sp.wait_ge(hsum_ready, GROUPS)
            for i in range(IPT):
                sp.dma_start(dst[i], hsum[32 * i:32 * i + S, :, :]).then_inc(res_out, 16)
            sp.wait_ge(scattered, 16 * TOPK * TILES)
            sp.wait_ge(filled, 16)

            def load(j, b, gathers):
                if gathers is not None:
                    sp.wait_ge(kept, j - 1)
                    sp.wait_ge(gathered[b], gathers)
                place = sp.value_load(ei[0:1, bass.ds(j + 2 * LISTED, 1)], min_val=0, max_val=E * MOST)
                sp.dma_start(tb[:, b, :], slots[bass.ds(place * 128, 128), :]).then_inc(tb_in[b], 16)

            sp.wait_ge(eid_ready, 1)
            load(0, 0, None)
            load(1, 1, None)
            load(2, 0, 16)
            load(3, 1, 16)
            further = further_pairs(sp)
            with sp.Fori(1, SLOT_TILES // 2) as jj:
                with sp.If(jj <= further):
                    load(jj * 2 + 2, 0, jj * 16 + 16)
                    load(jj * 2 + 3, 1, jj * 16 + 16)
            sp.wait_ge(late_in, 16 * 3 * LATE_PARTS)

        @block.gpsimd
        def _(pool):
            pool.memset(zeros[:, :], 0.0).then_inc(fill_set, 1)
            pool.memset(empty[:, :, :], 0.0).then_inc(fill_set, 1)
            for g in range(2):
                pool.memset(A[g].vbd, 0.0).then_inc(pads_a, 1)
                pool.memset(A[g].scp.rearrange("p (h k) -> p h k", k=32)[:, :, S:32], 0.0).then_inc(pads_a, 1)
            pool.wait_ge(first_in, 16)
            pool.wait_ge(fill_set, 2)
            pool.tensor_copy(empty[:, :, 1].bitcast(I32), const("spare")).then_inc(fill_set, 1)
            for k in range(TOPK):
                pool.tensor_copy(pay[:, k, :, 1].bitcast(I32), const("number")).then_inc(fill_set, 1)

            def pads(w):
                pool.memset(w.p2, 0.0)
                pool.memset(w.ot2a, 0.0)
                pool.memset(w.ot2b, 0.0)
                pool.memset(w.pbd, 0.0).then_inc(pads_set, 1)

            def rstd(g, n):
                s = (0, 0, 0, 1)[n]
                pool.wait_ge(ve_ready[n], g + 1)
                pool.tensor_tensor(rs[s][:, :], ve[s][:, :], const("neghalf"), ALU.pow).then_inc(rs_ready[n], 1)

            def a1(g):
                w = A[g]
                rstd(g, 0)

            def a2(g):
                w = A[g]
                if g == 0:
                    pool.wait_ge(bias_in, 16)
                pool.wait_ge(z_ready[0], g + 1)
                pool.tensor_tensor(w.h, w.h, bprow.unsqueeze(1).to_broadcast([128, GT, D]), ALU.add).then_inc(hb_ready, 1)

            def a8(g):
                w = A[g]
                rstd(g, 1)
                rstd(g, 2)

            def b1(g):
                w = B[g]
                if B[g].s == 0:
                    pool.wait_ge(patch_done, TILES)
                    pool.wait_ge(proj_done, GROUPS)
                    pads(B[g])
                elif g == 0:
                    pool.wait_ge(o_done, 1)
                    pool.wait_ge(patch_done, 4)
                    pads(B[g])

            def b2(g):
                w = B[g]
                for n in range(5):
                    pool.wait_ge(rope_mul, g * 5 + (n + 1))
                    to = w.kr if n == 0 else w.qr[:, :, :, n - 1, :]
                    pool.tensor_tensor(to, w.tmp[:, n % 2, :, 0], w.tmp[:, n % 2, :, 1], ALU.add).then_inc(rope_add, 1)
                    if n == 0:
                        pool.wait_ge(rope_add, g * 5 + 1)
                        for e in range(2):
                            last = pool.tensor_tensor(
                                w.kbd2[:, e], w.kr[:, e].unsqueeze(2).to_broadcast([C, GI, G, S]),
                                const("group_of_row", C).unsqueeze(1).unsqueeze(3).to_broadcast([C, GI, G, S]),
                                ALU.mult)
                        last.then_inc(kbd2_ready, 1)

            def b6(g):
                w = B[g]
                rstd(g, 3)
                pool.wait_ge(x2_ready, g * 2 + 2)
                pool.tensor_tensor(hsum[:, bass.ds(g * GT, GT), :], w.hB, w.zB, ALU.add).then_inc(hsum_ready, 1)

            def scatter(q):
                pool.wait_ge(filled, 16)
                pool.wait_ge(fill_set, 3 + TOPK)
                pool.wait_ge(gates_set, TOPK * (q + 1))
                pool.wait_ge(idx_ready, q + 1)
                for t in range(RT * q, RT * q + RT):
                    for k in range(TOPK):
                        pool.indirect_dma_start(slots, bass.IndirectOffsetOnAxis(sidx[:, k, t:t + 1], 0),
                                                pay[:, k, t, :], None).then_inc(scattered, 16)

            stages([a1, a2, nothing, nothing, nothing, nothing, nothing, a8],
                   [b1, b2, nothing, nothing, nothing, b6, nothing, nothing], {4: scatter})
            scatter(1)
            pool.wait_ge(tokens_out[0], 2 * 16 * IPT)
            pool.wait_ge(tokens_out[1], 2 * 16 * IPT)
            pool.wait_ge(zeros_out, 32)
            pool.wait_ge(res_out, 16 * IPT)
            pool.wait_ge(eid_ready, 1)
            further = further_pairs(pool)

            def gather(j, b, loads):
                pool.wait_ge(tb_in[b], loads)
                if not isinstance(j, int) or j >= 2:
                    pool.wait_ge(xtr_done, j - 1)
                pool.sem_inc(moving, 1)
                pool.indirect_dma_start(xin[:, b, :], None, moe_in,
                                        bass.IndirectOffsetOnAxis(tb[:, b, 1:2].bitcast(I32), 0)
                                        ).then_inc(gathered[b], 16)

            def add(j, b):
                pool.wait_ge(y_ready, j + 1)
                pool.sem_inc(moving, 1)
                pool.indirect_dma_start(out, bass.IndirectOffsetOnAxis(row[:, b:b + 1], 0),
                                        yo[:, b, :], None, compute_op=ALU.add).then_inc(added, 16)

            def add_pair(jj, between):
                add(jj * 2 - 2, 0)
                between()
                pool.wait_ge(added, jj * 32 - 16)
                add(jj * 2 - 1, 1)
                pool.wait_ge(added, jj * 32)

            gather(0, 0, 16)
            gather(1, 1, 16)
            gather(2, 0, 32)
            gather(3, 1, 32)
            with pool.Fori(1, SLOT_TILES // 2 + 1) as jj:
                with pool.If(jj <= further + 1):
                    with pool.If(jj <= further):
                        gather(jj * 2 + 2, 0, jj * 16 + 32)
                        add_pair(jj, lambda: gather(jj * 2 + 3, 1, jj * 16 + 32))
                    with pool.If(jj == further + 1):
                        add_pair(jj, lambda: None)

        @block.scalar
        def _(act):
            act.dma_start(ct[:, 0:NFIRST], cst[:, 0:NFIRST]).then_inc(first_in, 16)
            act.dma_start(ct[:, NFIRST:], cst[:, NFIRST:]).then_inc(consts_in, 16)

            def a2(g):
                w = A[g]
                act.wait_ge(zt_done, g + 1)
                act.activation(w.fTa, w.ps[1][0:C, :], ACT.Copy).then_inc(zt_ready, 1)

            def a3(g):
                w = A[g]
                if g == 0:
                    act.wait_ge(attn_w_in, 16)
                act.wait_ge(k_done, g + 1)
                for c in range(2):
                    act.activation(w.k1[:, c].rearrange("p i k -> p (i k)"), w.ps[2][0:C, CT * c:CT * c + CT],
                                   ACT.Identity, bias=small[:, 2 + c:3 + c]).then_inc(k_ready, 1)
                act.wait_ge(pads_a, 4)
                act.wait_ge(v_done, g + 1)
                spread_values(lambda to, src: act.activation(to, src, ACT.Copy), w, (0, 1), v_a)
                act.wait_ge(q_done, g + 1)
                for c in range(2):
                    act.activation(w.q1[:, c, :], w.ps[3][0:C, 256 * c:256 * c + 256], ACT.Identity,
                                   bias=small[:, c:c + 1]).then_inc(q_ready, 1)

            def a4(g):
                w = A[g]
                act.wait_ge(sub_ready[0], g + 1)
                act.activation(w.s3, w.s3, ACT.Exp, scale=HD1 ** -0.5).then_inc(exp_ready[0], 1)

            def a5(g):
                w = A[g]
                act.wait_ge(pt_done, g * 2 + 1)
                act.activation(w.pT[:, 0:512], w.ps[3][:, :], ACT.Copy).then_inc(pt_ready, 1)
                act.wait_ge(pt_done, g * 2 + 2)
                act.activation(w.pT[:, 512:768], w.ps[0][:, 0:256], ACT.Copy).then_inc(pt_ready, 1)

            def a7(g):
                w = A[g]
                act.wait_ge(ot_done, g + 1)
                for c in range(2):
                    act.activation(w.fTa[:, 256 * c:256 * c + 256], w.ps[2][0:C, 256 * c:256 * c + 256], ACT.Identity,
                                   bias=small[:, 4 + c:5 + c]).then_inc(ot_ready, 1)

            def squares(w, s, ready):
                for t in range(GT):
                    act.wait_ge(*ready(t))
                    act.activation(w.u[:, t, :], w.zB[:, t, :], ACT.Square,
                                   accum_out=ms[s][:, t:t + 1]).then_inc(sq_ready[s], 1)

            def a8(g):
                w = A[g]
                if g >= 2:
                    act.wait_ge(tokens_out[g % 2], 16 * IPT)
                    act.wait_ge(mt_done, g - 1)
                squares(w, 0, lambda t: (z_ready[1], g + 1))

            def b1(g):
                w = B[g]
                act.wait_ge(ut_done, g + 1)
                for c in range(2):
                    act.activation(w.fTb[:, 256 * c:256 * c + 256], w.ps[0][0:C, 256 * c:256 * c + 256], ACT.Identity,
                                   scale=small[:, 6 + c:7 + c]).then_inc(ut_ready, 1)

            def b2(g):
                w = B[g]
                act.wait_ge(v2_done, g + 1)
                act.activation(w.v2.rearrange("p t n -> p (t n)"), w.ps[1][:, 0:GT * D], ACT.Copy).then_inc(v2_ready, 1)

            def b3(g):
                w = B[g]
                act.wait_ge(sub_ready[1], g + 1)
                act.activation(w.sc[0:104, :], w.sc[0:104, :], ACT.Exp, scale=HD2 ** -0.5).then_inc(exp_ready[1], 1)

            def b4(g):
                w = B[g]
                act.wait_ge(pads_set, 1 if B[g].s else 2)
                act.wait_ge(pt2_done, g * 2 + 1)
                for i in range(IPT):
                    rows = slice(32 * i, 32 * i + 32)
                    last = act.activation(w.pbd[rows, 0:2, :, i, :].rearrange("p g t n -> p (g t) n"),
                                          w.ps[2][rows, 0:4 * 104].rearrange("p (a n) -> p a n", a=4), ACT.Copy)
                last.then_inc(pbd_a, 1)

            def b5(g):
                w = B[g]
                act.wait_ge(pv2_done, g * 3 + 1)
                act.activation(w.ot2a[:, :, 0, :].rearrange("p r (i q) -> p r i q", i=IPT)[:, :, :, 0:S],
                               w.ps[0][:, 0:IPT * R * S].rearrange("p (i r q) -> p r i q", i=IPT, r=R),
                               ACT.Copy).then_inc(ot2_a, 1)
                act.wait_ge(pv2_done, g * 3 + 3)
                for t in range(GT):
                    last = act.activation(w.ot2b[:, :, t, :].rearrange("p r (i q) -> p r i q", i=IPT)[:, :, :, 0:S],
                                          w.ps[2][:, CT * t:CT * t + CT].rearrange("p (i r q) -> p r i q", i=IPT, r=2),
                                          ACT.Copy)
                last.then_inc(ot2_a, 1)

            def b6(g):
                w = B[g]
                squares(w, 1, lambda t: (x2_ready, g * 2 + (t + 1)))

            def b7(g):
                w = B[g]
                act.wait_ge(mt_done, g + 1)
                act.activation(w.fTb, w.ps[1][0:C, :], ACT.Copy).then_inc(mt_ready, 1)

            def gate_exp(q):
                act.wait_ge(gap_ready, q + 1)
                act.activation(eg[:, :], gap[:, :], ACT.Exp).then_inc(eg_ready, 1)

            def copy_ranks(q):
                act.wait_ge(ranks_done, q + 1)
                act.activation(ranks[:, :], ps[5][:, RANKS:], ACT.Copy).then_inc(ranks_read, 1)

            stages([nothing, a2, a3, a4, a5, nothing, a7, a8], [b1, b2, b3, b4, b5, b6, b7, nothing],
                   {1: gate_exp, 2: copy_ranks})
            gate_exp(1)
            copy_ranks(1)
            def load_late(first, last):
                for n in range(first, last):
                    if n < LATE_PARTS:
                        w = (E // 2) * 3 * D // LATE_PARTS
                        a = arena0 + n * w
                        act.dma_start(big[:, a:a + w], wdn[:, a:a + w]).then_inc(late_in, 16)
                    else:
                        w = (E // 2) * 4 * FF // (2 * LATE_PARTS)
                        a = (n - LATE_PARTS) * w
                        act.dma_start(big[0:C, GU0 + a:GU0 + a + w], wgu[:, a:a + w]).then_inc(late_in, 16)

            act.wait_ge(lg_ready, GROUPS)
            act.wait_ge(hsum_ready, GROUPS)
            act.wait_ge(tokens_out[0], 2 * 16 * IPT)
            act.wait_ge(tokens_out[1], 2 * 16 * IPT)
            load_late(*LATE_CUTS[0:2])

            def copy_x(j, b):
                act.wait_ge(xtr_done, j + 1)
                act.activation(xT[:, b, :], ps[6][0:C, 0:256], ACT.Copy).then_inc(xT_ready, 1)

            def silu(j, b):
                act.wait_ge(gate_done, j + 1)
                act.activation(sg[:, b, :], ps[b][:, 0:FF], ACT.Silu).then_inc(sg_ready, 1)

            def copy_h(j, b):
                act.wait_ge(htr_done, j + 1)
                act.activation(hT[:, b, :], ps[4][:, 0:FF], ACT.Copy).then_inc(hT_ready, 1)

            def step(j, b, prior=True):
                if prior:
                    copy_h(j - 1, 1 - b)
                silu(j, b)
                if not prior:
                    load_late(*LATE_CUTS[2:4])
                copy_x(j + 1, 1 - b)

            copy_x(0, 0)
            load_late(*LATE_CUTS[1:3])
            step(0, 0, prior=False)
            step(1, 1)
            act.wait_ge(eid_ready, 1)
            further = further_pairs(act)
            with act.Fori(1, SLOT_TILES // 2 + 1) as jj:
                with act.If(jj <= further + 1):
                    with act.If(jj <= further):
                        step(jj * 2, 0)
                        step(jj * 2 + 1, 1)
                    with act.If(jj == further + 1):
                        copy_h(jj * 2 - 1, 1)

        @block.vector
        def _(dve):
            def layer_stats(g, n, src, ready):
                for t in range(GT):
                    dve.wait_ge(ready, g + 1)
                    dve.bn_stats(st6[:, t, :], src[:, t, :]).then_inc(st_ready[n], 1)
                dve.wait_ge(st_ready[n], g * GT + GT)
                dve.tensor_tensor(mom[:, 0, :], st6[:, :, 1], st6[:, :, 4], ALU.add)
                dve.tensor_tensor(mom[:, 1, :], st6[:, :, 1], st6[:, :, 4], ALU.subtract)
                dve.tensor_tensor(mom[:, 2, :], st6[:, :, 2], st6[:, :, 5], ALU.add).then_inc(mom_ready[n], 1)
                dve.wait_ge(mom_ready[n], g * 2 + 1)
                dve.tensor_scalar(mean[:, :], mom[:, 0, :], 0.5, None, ALU.mult)
                dve.tensor_scalar(mom[:, 2, :], mom[:, 2, :], 1.0 / D, LN_EPS, ALU.mult, ALU.add)
                dve.scalar_tensor_tensor(mom[:, 3, :], mom[:, 1, :], 0.25, mom[:, 1, :],
                                         ALU.mult, ALU.mult).then_inc(mom_ready[n], 1)
                dve.wait_ge(mom_ready[n], g * 2 + 2)
                dve.tensor_tensor(ve[0][:, :], mom[:, 2, :], mom[:, 3, :], ALU.add).then_inc(ve_ready[n], 1)

            def normalise(g, n, src, to):
                dve.wait_ge(rs_ready[n], g + 1)
                for t in range(GT):
                    last = dve.tensor_scalar(to[:, t, :], src[:, t, :], mean[:, t:t + 1], rs[0][:, t:t + 1],
                                             ALU.subtract, ALU.mult)
                last.then_inc(z_ready[n], 1)

            def mean_square(g, n):
                s = n - 2
                dve.wait_ge(sq_ready[s], g * GT + GT)
                dve.tensor_scalar(ve[s][:, :], ms[s][:, :], 1.0 / D, RMS_EPS, ALU.mult, ALU.add)\
                   .then_inc(ve_ready[n], 1)
                dve.wait_ge(rs_ready[n], g + 1)

            def softmax(g, n, w, rows):
                mask = const("mask1" if n == 0 else "mask2", rows)
                s3 = w.s3
                for t in range(GT):
                    dve.wait_ge(s_done[n], g * GT + (t + 1))
                    bank = w.ps[(1 if n == 0 else 0) + t]
                    dve.tensor_tensor(s3[:, 12 * t:12 * t + 12, :],
                                      bank[0:rows, 0:12 * S].rearrange("p (h k) -> p h k", h=12),
                                      mask.unsqueeze(1).to_broadcast([rows, 12, S]), ALU.add).then_inc(sm_ready[n], 1)
                dve.wait_ge(sm_ready[n], g * GT + GT)
                dve.tensor_reduce(mx[w.s][0:rows, :], s3, AX.X, ALU.max).then_inc(max_ready[n], 1)
                dve.wait_ge(max_ready[n], g + 1)
                dve.tensor_tensor(s3, s3, mx[w.s][0:rows, :].unsqueeze(2).to_broadcast([rows, NR, S]),
                                  ALU.subtract).then_inc(sub_ready[n], 1)
                dve.wait_ge(exp_ready[n], g + 1)
                dve.tensor_reduce(sm[w.s][0:rows, :], s3, AX.X, ALU.add).then_inc(sum_ready[n], 1)
                dve.wait_ge(sum_ready[n], g + 1)
                dve.reciprocal(rc[w.s][0:rows, :], sm[w.s][0:rows, :]).then_inc(rc_ready[n], 1)
                dve.wait_ge(rc_ready[n], g + 1)

            dve.wait_ge(first_in, 16)
            dve.wait_ge(base_done, 1)
            dve.tensor_tensor(base[:, :], ps[0][:, 0:D], const("pos"), ALU.add).then_inc(base_ready, 1)
            dve.wait_ge(base_ready, 1)

            def a1(g):
                w = A[g]
                dve.wait_ge(patch_done, g * GT + GT)
                if g > 0:
                    dve.wait_ge(z_ready[0], g)
                if g >= 2:
                    dve.wait_ge(h1_ready, g)
                dve.tensor_tensor(w.h, w.ps[0][:, 0:GT * D].rearrange("p (t n) -> p t n", t=GT),
                                  base[:, :].unsqueeze(1).to_broadcast([128, GT, D]), ALU.add).then_inc(h_ready, 1)
                layer_stats(g, 0, w.h, h_ready)
                normalise(g, 0, w.h, w.z)

            def a3(g):
                w = A[g]
                if g == 0:
                    dve.wait_ge(consts_in, 16)
                dve.wait_ge(pads_a, 4)
                dve.wait_ge(v_done, g + 1)
                spread_values(dve.tensor_copy, w, (2, 3), v_d)
                for c in range(2):
                    dve.wait_ge(k_ready, g * 2 + (c + 1))
                    last = dve.tensor_tensor(
                        w.kbd[:, c], w.k1[:, c].unsqueeze(2).to_broadcast([C, GI, HC, S]),
                        const("head_of_row", C).unsqueeze(1).unsqueeze(3).to_broadcast([C, GI, HC, S]), ALU.mult)
                last.then_inc(kbd_ready, 1)

            def a4(g):
                w = A[g]
                softmax(g, 0, w, 128)

            def a6(g):
                w = A[g]
                dve.wait_ge(o_done, g + 1)
                dve.tensor_tensor(w.o1.rearrange("p t (h d) -> p (t h) d", h=H1),
                                  w.ps[1][:, 0:GT * D].rearrange("p (h d) -> p h d", d=HD1),
                                  rc[w.s][:, :].unsqueeze(2).to_broadcast([128, NR, HD1]), ALU.mult).then_inc(o_ready, 1)

            def a8(g):
                w = A[g]
                if g >= 2:
                    dve.wait_ge(hsum_ready, g - 1)
                dve.wait_ge(hb_ready, g + 1)
                dve.wait_ge(proj_done, g + 1)
                dve.tensor_tensor(w.hB, w.ps[3][:, 0:GT * D].rearrange("p (t n) -> p t n", t=GT), w.h,
                                  ALU.add).then_inc(h1_ready, 1)
                layer_stats(g, 1, w.hB, h1_ready)
                normalise(g, 1, w.hB, w.zB)
                mean_square(g, 2)
                for t in range(GT):
                    last = dve.tensor_scalar(w.u[:, t, :], w.zB[:, t, :], rs[0][:, t:t + 1], None, ALU.mult)
                last.then_inc(u_ready[0], 1)

            def b2(g):
                w = B[g]
                for n in range(5):
                    dve.wait_ge(eo_done, g * 5 + (n + 1))
                    if n >= 2:
                        dve.wait_ge(rope_add, g * 5 + (n - 1))
                    eo = w.ps[(2, 3, 0)[n % 3]][0:C, 0:2 * CT].rearrange("p (e i q) -> p e i q", e=2, i=GI)
                    turn = const("turn", C).rearrange("p (m e q) -> p m e q", m=2, e=2)
                    for m in range(2):
                        last = dve.tensor_tensor(w.tmp[:, n % 2, m], eo,
                                                 turn[:, m].unsqueeze(2).to_broadcast([C, 2, GI, S]), ALU.mult)
                    last.then_inc(rope_mul, 1)

            def b3(g):
                w = B[g]
                softmax(g, 1, w, 104)
                dve.wait_ge(pads_set, 1 if B[g].s else 2)
                for t in range(GT):
                    last = dve.tensor_tensor(
                        w.p2[:, t, :, :, 0:S],
                        w.sc[0:104, t * 12 * S:(t + 1) * 12 * S].rearrange("p (i g k) -> p g i k", i=IPT, g=G),
                        rc[w.s][0:104, 12 * t:12 * t + 12].rearrange("p (i g) -> p g i", i=IPT).unsqueeze(3)
                        .to_broadcast([104, G, IPT, S]), ALU.mult)
                last.then_inc(p2_ready, 1)

            def b4(g):
                w = B[g]
                dve.wait_ge(pt2_done, g * 2 + 2)
                for i in range(IPT):
                    rows = slice(32 * i, 32 * i + 32)
                    last = dve.tensor_copy(w.pbd[rows, 2, :, i, :], w.ps[3][rows, 0:2 * 104].rearrange("p (a n) -> p a n", a=2))
                last.then_inc(pbd_d, 1)

            def b5(g):
                w = B[g]
                dve.wait_ge(pv2_done, g * 3 + 2)
                dve.tensor_copy(w.ot2a[:, :, 1, :].rearrange("p r (i q) -> p r i q", i=IPT)[:, :, :, 0:S],
                                w.ps[1][:, 0:IPT * R * S].rearrange("p (i r q) -> p r i q", i=IPT, r=R)).then_inc(ot2_d, 1)

            def b6(g):
                w = B[g]
                for t in range(GT):
                    dve.wait_ge(wo_done, g * GT + (t + 1))
                    dve.tensor_tensor(w.zB[:, t, :], w.ps[(3, 0)[t]][:, 0:D], w.zB[:, t, :], ALU.add).then_inc(x2_ready, 1)
                mean_square(g, 3)
                for t in range(GT):
                    last = dve.scalar_tensor_tensor(w.u[:, t, :], w.zB[:, t, :], rs[1][:, t:t + 1], w2row,
                                                    ALU.mult, ALU.mult)
                last.then_inc(u_ready[1], 1)

            def b8(g):
                w = B[g]
                dve.wait_ge(lg_done, g + 1)
                dve.tensor_copy(lg[:, bass.ds(g * (GT * E), GT * E)], w.ps[2][:, 0:GT * E]).then_inc(lg_ready, 1)

            done = [0]

            def then(ins):
                done[0] += 1
                ins.then_inc(r_dve, 1)
                dve.wait_ge(r_dve, done[0])

            def choose(q):
                ts = range(RT * q, RT * q + RT)
                tiles = slice(RT * q, RT * q + RT)
                dve.wait_ge(lg_ready, (q + 1) * RT // GT)
                for t in ts:
                    last = dve.max(top[:, t, :], lg[:, t * E:(t + 1) * E])
                then(last)
                dve.tensor_tensor(gap[:, :], top[:, tiles, 1], top[:, tiles, 0], ALU.subtract).then_inc(gap_ready, 1)
                for t in ts:
                    last = dve.max_index(topi[:, t, :], top[:, t, :], lg[:, t * E:(t + 1) * E])
                then(last)
                then(dve.tensor_scalar(topf[:, :, :], topi[:, tiles, 0:TOPK].rearrange("p t k -> p k t"),
                                       const("unrouted"), None, ALU.add))
                then(dve.tensor_tensor(oh[:, :, :, :].rearrange("p k t e -> p (k t) e"),
                                       const("iota").unsqueeze(1).to_broadcast([128, TOPK * RT, E]),
                                       topf[:, :, :].rearrange("p k t -> p (k t)").unsqueeze(2)
                                       .to_broadcast([128, TOPK * RT, E]), ALU.is_equal))
                dve.tensor_tensor(ohs[:, :, :], oh[:, 0], oh[:, 1], ALU.add).then_inc(ohs_ready, 1)

            def place(q):
                tiles = slice(RT * q, RT * q + RT)
                dve.wait_ge(eg_ready, q + 1)
                then(dve.tensor_scalar(den[:, :], eg[:, :], 1.0, None, ALU.add))
                dve.reciprocal(pay[:, 0, tiles, 0], den[:, :]).then_inc(gates_set, 1)
                dve.wait_ge(gates_set, TOPK * q + 1)
                dve.tensor_tensor(pay[:, 1, tiles, 0], eg[:, :], pay[:, 0, tiles, 0], ALU.mult).then_inc(gates_set, 1)
                if q == 0:
                    then(dve.tensor_copy(cum[:, 0, :], const("expert_slots")))
                dve.wait_ge(ranks_read, q + 1)
                for i in range(RT):
                    then(dve.tensor_tensor(cum[:, RT * q + i + 1, :], ranks[:, (RT + i) * E:(RT + i + 1) * E],
                                           cum[:, RT * q + i, :], ALU.add))
                then(dve.tensor_tensor(rank[:, :], ranks[:, 0:RT * E],
                                       cum[:, tiles, :].rearrange("p t e -> p (t e)"), ALU.add))
                then(dve.tensor_tensor(pick[:, :, :], oh[:, :, :, :].rearrange("p k t e -> p k (t e)"),
                                       rank[:, :].unsqueeze(1).to_broadcast([128, TOPK, RT * E]), ALU.mult))
                then(dve.tensor_reduce(slot[:, :], pick[:, :, :].rearrange("p k (t e) -> p (k t) e", e=E),
                                       AX.X, ALU.add))
                dve.tensor_tensor(sidx[:, :, tiles], slot[:, :].rearrange("p (k t) -> p k t", k=TOPK),
                                  const("trash").rearrange("p (k t) -> p k t", k=TOPK)[:, :, tiles],
                                  ALU.add).then_inc(idx_ready, 1)

            stages([a1, nothing, a3, a4, nothing, a6, nothing, a8], [nothing, b2, b3, b4, b5, b6, nothing, b8],
                   {1: choose, 4: place})
            choose(1)
            place(1)

            then(dve.tensor_tensor(cnt[:, :], cum[:, TILES, :], const("expert_slots"), ALU.subtract))
            then(dve.tensor_tensor(over_step, cnt[:, :].unsqueeze(2).to_broadcast([128, E, MOST]),
                                   const("steps").unsqueeze(1).to_broadcast([128, E, MOST]), ALU.is_gt))
            then(dve.tensor_reduce(etl[:, :], over_step, AX.X, ALU.add))
            dve.tensor_scalar(spare[:, :], etl[:, :], -1.0, float(MOST), ALU.mult, ALU.add)
            then(dve.tensor_tensor(lessed, etl[:, :].unsqueeze(1).to_broadcast([128, E, E]),
                                   const("less").rearrange("p (a b) -> p a b", a=E), ALU.mult))
            then(dve.tensor_reduce(est[:, :], lessed, AX.X, ALU.add))
            then(dve.tensor_tensor(een[:, :], est[:, :], etl[:, :], ALU.add))
            then(dve.tensor_tensor(le, een[0:1, :].unsqueeze(1).to_broadcast([1, LISTED, E]),
                                   const("tile_iota", 1).unsqueeze(2).to_broadcast([1, LISTED, E]), ALU.is_le))
            e0, e1, place_of = [ef[:, LISTED * n:LISTED * n + LISTED] for n in range(3)]
            dve.tensor_reduce(e0, le, AX.X, ALU.add)
            then(dve.tensor_tensor(skip, le, spare[0:1, :].unsqueeze(1).to_broadcast([1, LISTED, E]), ALU.mult))
            then(dve.tensor_reduce(place_of, skip, AX.X, ALU.add))
            dve.tensor_scalar(e0, e0, float(E - 1), None, ALU.min)
            then(dve.tensor_tensor(place_of, place_of, const("tile_iota", 1), ALU.add))
            dve.tensor_scalar(place_of, place_of, float(E * MOST), None, ALU.min)
            then(dve.tensor_scalar(le[:, 0:SLOT_TILES // 2 - 1, 1], const("even_tiles", 1), een[0:1, E - 1:E], None,
                                   ALU.is_lt))
            dve.tensor_reduce(ef[:, 3 * LISTED:], le[:, 0:SLOT_TILES // 2 - 1, 1], AX.X, ALU.add)
            then(dve.tensor_scalar(e1, e0, -1.0, float(E - 1), ALU.mult, ALU.add))
            dve.tensor_copy(ei[:, :], ef[:, :]).then_inc(eid_ready, 1)
            dve.wait_ge(eid_ready, 1)
            further = further_pairs(dve)

            def keep(b, loads):
                dve.wait_ge(tb_in[b], loads)
                dve.tensor_copy(held_gate[:, b:b + 1], tb[:, b, 0:1])
                dve.tensor_copy(held_row[:, b:b + 1], tb[:, b, 1:2].bitcast(I32)).then_inc(kept, 1)

            def gated(j, b):
                dve.wait_ge(up_done, j + 1)
                dve.wait_ge(sg_ready, j + 1)
                dve.tensor_tensor(hh[:, b, :], ps[2 + b][:, 0:FF], sg[:, b, :], ALU.mult).then_inc(hh_ready, 1)

            def take(j, b):
                dve.wait_ge(kept, j + 1)
                if not isinstance(j, int):
                    dve.wait_ge(added, j * 16 - 16)
                dve.tensor_copy(gate[:, b:b + 1], held_gate[:, b:b + 1])
                dve.tensor_copy(row[:, b:b + 1], held_row[:, b:b + 1]).then_inc(taken, 1)

            def scaled_y(j, b):
                dve.wait_ge(y_done, j + 1)
                dve.wait_ge(taken, j + 1)
                dve.tensor_scalar(yo[:, b, :], ps[5][:, 0:D], gate[:, b:b + 1], None, ALU.mult).then_inc(y_ready, 1)

            keep(0, 16)
            keep(1, 16)
            gated(0, 0)
            take(0, 0)
            dve.wait_ge(taken, 1)
            keep(0, 32)
            gated(1, 1)
            scaled_y(0, 0)
            take(1, 1)
            with dve.Fori(1, SLOT_TILES // 2 + 1) as jj:
                with dve.If(jj <= further + 1):
                    with dve.If(jj <= further):
                        dve.wait_ge(taken, jj * 2)
                        keep(1, jj * 16 + 16)
                        gated(jj * 2, 0)
                        scaled_y(jj * 2 - 1, 1)
                        take(jj * 2, 0)
                        dve.wait_ge(taken, jj * 2 + 1)
                        keep(0, jj * 16 + 32)
                        gated(jj * 2 + 1, 1)
                        scaled_y(jj * 2, 0)
                        take(jj * 2 + 1, 1)
                    with dve.If(jj == further + 1):
                        scaled_y(jj * 2 - 1, 1)

        @block.tensor
        def _(pe):
            mm = pe.matmul

            def turned(bank, src):
                for t in range(GT):
                    for c in range(2):
                        last = pe.transpose(bank[0:C, 256 * c + 128 * t:256 * c + 128 * t + 128],
                                            src[:, t, C * c:C * c + C], eye)
                return last

            def real(fT, c):
                return fT[:, 256 * c:256 * c + 256].rearrange("p (i q) -> p i q", q=32)[:, :, 0:S]

            def a1(g):
                w = A[g]
                if g >= 2:
                    pe.wait_ge(pt_ready, g * 2)
                for t in range(GT):
                    n = g * GT + t
                    pe.wait_ge(x_in[n % 4], (n // 4 + 1) * 16)
                    for k in range(PK):
                        last = mm(w.ps[0][:, D * t:D * t + D], patches(n)[:, 128 * k:128 * k + 128], wpatch[:, k, :],
                                  start=(k == 0), stop=(k == PK - 1))
                    last.then_inc(patch_done, 1)

            def a2(g):
                w = A[g]
                pe.wait_ge(z_ready[0], g + 1)
                turned(w.ps[1], w.z).then_inc(zt_done, 1)

            def a3(g):
                w = A[g]
                if g == 0:
                    pe.wait_ge(attn_w_in, 16)
                pe.wait_ge(zt_ready, g + 1)
                for c in range(2):
                    for k in range(2):
                        last = mm(w.ps[2][0:C, CT * c:CT * c + CT], wqkv1[:, k, D + C * c:D + C * c + C], real(w.fTa, k),
                                  start=(k == 0), stop=(k == 1))
                last.then_inc(k_done, 1)
                for t in range(GT):
                    for k in range(2):
                        last = mm(w.ps[0][:, D * t:D * t + D], w.fTa[:, 256 * k + 128 * t:256 * k + 128 * t + 128],
                                  wqkv1[:, k, 2 * D:3 * D], start=(k == 0), stop=(k == 1))
                last.then_inc(v_done, 1)
                if g >= 2:
                    pe.wait_ge(h1_ready, g)
                for c in range(2):
                    for k in range(2):
                        last = mm(w.ps[3][0:C, 256 * c:256 * c + 256], wqkv1[:, k, C * c:C * c + C],
                                  w.fTa[:, 256 * k:256 * k + 256], start=(k == 0), stop=(k == 1))
                last.then_inc(q_done, 1)

            def a4(g):
                w = A[g]
                pe.wait_ge(q_ready, g * 2 + 2)
                pe.wait_ge(kbd_ready, g + 1)
                for t in range(GT):
                    for i in range(IPT):
                        for c in range(2):
                            last = mm(w.ps[1 + t][32 * i:32 * i + 32, HC * S * c:HC * S * (c + 1)],
                                      w.q1[:, c, 128 * t + 32 * i:128 * t + 32 * i + 32],
                                      w.kbd[:, c, IPT * t + i].rearrange("p h k -> p (h k)"), start=True, stop=True,
                                      tile_position=(0, 32 * i))
                    last.then_inc(s_done[0], 1)

            def a5(g):
                w = A[g]
                pe.wait_ge(exp_ready[0], g + 1)
                pe.wait_ge(v_a, g + 1)
                pe.wait_ge(v_d, g + 1)
                for n in range(G):
                    for t in range(GT):
                        a = (12 * t + 4 * n) * 32
                        last = pe.transpose(w.ps[(3, 3, 0)[n]][:, 256 * (n % 2) + 128 * t:256 * (n % 2) + 128 * t + 128],
                                            w.scp[:, a:a + 128], eye)
                    if n:
                        last.then_inc(pt_done, 1)

            def a6(g):
                w = A[g]
                pe.wait_ge(pt_ready, g * 2 + 2)
                for t in range(GT):
                    for i in range(IPT):
                        for n in range(G):
                            a = 256 * n + 128 * t + 32 * i
                            last = mm(w.ps[1][32 * i:32 * i + 32, D * t + 64 * n:D * t + 64 * n + 64], w.pT[:, a:a + 32],
                                      w.vbd[:, t, i, n].rearrange("p r d -> p (r d)"), start=True, stop=True,
                                      tile_position=(0, 32 * i))
                last.then_inc(o_done, 1)

            def a7(g):
                w = A[g]
                pe.wait_ge(o_ready, g + 1)
                turned(w.ps[2], w.o1).then_inc(ot_done, 1)

            def a8(g):
                w = A[g]
                pe.wait_ge(ot_ready, g * 2 + 2)
                for t in range(GT):
                    for k in range(2):
                        last = mm(w.ps[3][:, D * t:D * t + D], w.fTa[:, 256 * k + 128 * t:256 * k + 128 * t + 128],
                                  wproj[:, k, :], start=(k == 0), stop=(k == 1))
                last.then_inc(proj_done, 1)

            def b1(g):
                w = B[g]
                pe.wait_ge(u_ready[0], g + 1)
                turned(w.ps[0], w.u).then_inc(ut_done, 1)

            def b2(g):
                w = B[g]
                pe.wait_ge(rest_w_in, 16)
                pe.wait_ge(ut_ready, g * 2 + 2)
                for t in range(GT):
                    for k in range(2):
                        last = mm(w.ps[1][:, D * t:D * t + D], w.fTb[:, 256 * k + 128 * t:256 * k + 128 * t + 128],
                                  wv2[:, k, :], start=(k == 0), stop=(k == 1))
                last.then_inc(v2_done, 1)
                if g in (1, 2):
                    pe.wait_ge(lg_ready, g)
                for n in range(5):
                    if n >= 3:
                        pe.wait_ge(rope_mul, g * 5 + (n - 2))
                    for e in range(2):
                        for k in range(2):
                            last = mm(w.ps[(2, 3, 0)[n % 3]][0:C, CT * e:CT * e + CT], wqk2[:, k, (n + 4) % 5, e, :],
                                      real(w.fTb, k), start=(k == 0), stop=(k == 1))
                    last.then_inc(eo_done, 1)

            def b3(g):
                w = B[g]
                pe.wait_ge(rope_add, g * 5 + 5)
                pe.wait_ge(kbd2_ready, g + 1)
                pe.wait_ge(v2_ready, g + 1)
                if g == 2:
                    pe.wait_ge(ranks_read, 1)
                for t in range(GT):
                    for i in range(IPT):
                        for e in range(2):
                            last = mm(w.ps[t][0:104, G * S * i:G * S * (i + 1)],
                                      w.qr[:, e, IPT * t + i].rearrange("p r q -> p (r q)"),
                                      w.kbd2[:, e, IPT * t + i].rearrange("p g k -> p (g k)"),
                                      start=(e == 0), stop=(e == 1))
                    last.then_inc(s_done[1], 1)

            def b4(g):
                w = B[g]
                pe.wait_ge(p2_ready, g + 1)
                for n in range(G):
                    for t in range(GT):
                        a = (n % 2) * GT * 104 + 104 * t
                        last = pe.transpose(w.ps[(2, 2, 3)[n]][:, a:a + 104], w.p2[:, t, n].rearrange("p i k -> p (i k)"),
                                            eye[0:104, 0:104])
                    if n:
                        last.then_inc(pt2_done, 1)

            def b5(g):
                w = B[g]
                pe.wait_ge(pbd_a, g + 1)
                pe.wait_ge(pbd_d, g + 1)
                for t in range(GT):
                    for n in range(2):
                        last = mm(w.ps[t][64 * n:64 * n + 64, 0:IPT * R * S], w.v2[:, t, 64 * n:64 * n + 64],
                                  w.pbd[:, n, t].rearrange("p i n -> p (i n)"), start=True, stop=True,
                                  tile_position=(0, 64 * n))
                    last.then_inc(pv2_done, 1)
                for t in range(GT):
                    for odd in range(2):
                        last = mm(w.ps[2][64 * odd:64 * odd + 64, CT * t:CT * t + CT], w.v2[:, t, 128:192],
                                  w.pbd[:, 2, t].rearrange("p i (r o q) -> p i r o q", r=2, o=2)[:, :, :, odd, :],
                                  start=True, stop=True, tile_position=(0, 64 * odd))
                last.then_inc(pv2_done, 1)

            def b6(g):
                w = B[g]
                pe.wait_ge(ot2_a, g * 2 + 2)
                pe.wait_ge(ot2_d, g + 1)
                for t in range(GT):
                    for k in range(6):
                        last = mm(w.ps[(3, 0)[t]][:, 0:D], w.ot2a[:, k, t, :] if k < R else w.ot2b[:, k - R, t, :],
                                  wout[:, k, :], start=(k == 0), stop=(k == 5))
                    last.then_inc(wo_done, 1)

            def b7(g):
                w = B[g]
                pe.wait_ge(u_ready[1], g + 1)
                turned(w.ps[1], w.u).then_inc(mt_done, 1)

            def b8(g):
                w = B[g]
                pe.wait_ge(mt_ready, g + 1)
                for t in range(GT):
                    for k in range(2):
                        last = mm(w.ps[2][:, E * t:E * t + E], w.fTb[:, 256 * k + 128 * t:256 * k + 128 * t + 128],
                                  wr[:, k, :], start=(k == 0), stop=(k == 1))
                last.then_inc(lg_done, 1)

            pe.wait_ge(first_in, 16)
            pe.wait_ge(patch_w_in, 16)
            mm(ps[0][:, 0:D], const("who", 2), bcls, start=True, stop=True).then_inc(base_done, 1)
            pe.wait_ge(base_ready, 1)
            def ranks(q):
                pe.wait_ge(ohs_ready, q + 1)
                if q == 0:
                    pe.wait_ge(v2_ready, 3)
                flat = ohs[:, :, :].rearrange("p t e -> p (t e)")
                mm(ps[5][:, RANKS:RANKS + RT * E], const("before"), flat, start=True, stop=True)
                mm(ps[5][:, RANKS + RT * E:RANKS + 2 * RT * E], const("ones"), flat,
                   start=True, stop=True).then_inc(ranks_done, 1)

            stages([a1, a2, a3, a4, a5, a6, a7, a8], [b1, b2, b3, b4, b5, b6, b7, b8], {2: ranks})
            ranks(1)

            def x_turn(b, loads):
                pe.wait_ge(gathered[b], loads)
                for c in range(2):
                    last = pe.transpose(ps[6][0:C, 128 * c:128 * c + 128], xin[:, b, C * c:C * c + C], eye)
                last.then_inc(xtr_done, 1)

            def gate_or_up(j, b, e, half, done):
                for k in range(2):
                    last = mm(ps[2 * half + b][:, 0:FF], xT[:, b, 128 * k:128 * k + 128],
                              big[0:C, bass.ds(e * (4 * FF) + (GU0 + 2 * FF * k + FF * half), FF)],
                              start=(k == 0), stop=(k == 1))
                last.then_inc(done, 1)

            def h_turn(j, b):
                pe.wait_ge(hh_ready, j + 1)
                for k in range(3):
                    last = pe.transpose(ps[4][:, 128 * k:128 * k + 128], hh[:, b, 128 * k:128 * k + 128], eye)
                last.then_inc(htr_done, 1)

            def down(j, b, first=False):
                e = pe.value_load(ei[0:1, bass.ds(j, 1)], min_val=0, max_val=E - 1)
                pe.wait_ge(hT_ready, j + 1)
                if not first:
                    pe.wait_ge(y_ready, j)
                for k in range(3):
                    last = mm(ps[5][:, 0:D], hT[:, b, 128 * k:128 * k + 128],
                              big[:, bass.ds(e * (3 * D) + D * k, D)], start=(k == 0), stop=(k == 2))
                last.then_inc(y_done, 1)

            def step(j, b, loads, prior=True, first=False):
                e = pe.value_load(ei[0:1, bass.ds(j + LISTED, 1)], min_val=0, max_val=E - 1)
                with pe.If(e < E // 2):
                    pe.wait_ge(late_in, 16 * 3 * LATE_PARTS)
                if prior:
                    h_turn(j - 1, 1 - b)
                pe.wait_ge(xT_ready, j + 1)
                gate_or_up(j, b, e, 0, gate_done)
                x_turn(1 - b, loads)
                gate_or_up(j, b, e, 1, up_done)
                if prior:
                    down(j - 1, 1 - b, first)

            pe.wait_ge(eid_ready, 1)
            further = further_pairs(pe)
            x_turn(0, 16)
            pe.wait_ge(early_in, 16 * 7)
            step(0, 0, 16, prior=False)
            step(1, 1, 32, first=True)
            with pe.Fori(1, SLOT_TILES // 2 + 1) as jj:
                with pe.If(jj <= further + 1):
                    with pe.If(jj <= further):
                        step(jj * 2, 0, jj * 16 + 16)
                        step(jj * 2 + 1, 1, jj * 16 + 32)
                    with pe.If(jj == further + 1):
                        h_turn(jj * 2 - 1, 1)
                        down(jj * 2 - 1, 1)


def table_of_constants():
    t = np.zeros((128, NCONST), np.float32)

    def put(name, a):
        a = np.asarray(a, np.float32)
        at, w = _C[name]
        t[:a.shape[0], at:at + w] = a.reshape(a.shape[0], w)

    row = np.arange(128)
    q = row % 32
    j = np.arange(D)
    i = np.arange(S - 1, dtype=np.float32)[:, None]
    angle = i / np.power(np.float32(10000.0), ((2 * (j // 2)).astype(np.float32) / np.float32(D)))
    pos = np.sin(angle + np.where(j % 2 == 1, np.float32(np.pi / 2), np.float32(0.0)).astype(np.float32))
    full = np.zeros((128, D), np.float32)
    for b in range(IPT):
        full[32 * b + 1:32 * b + S] = pos
    put("pos", full)
    key = np.arange(S)[None, :]
    put("mask1", np.where(key <= q[:, None], 0.0, MASKED))
    put("mask2", np.where(key <= (row[:104] % S)[:, None], 0.0, MASKED))
    put("head_of_row", row[:C, None] // HD1 == np.arange(HC))
    put("group_of_row", row[:C, None] // J == np.arange(G))
    inv = (1.0 / np.power(np.float32(10000.0), np.arange(0, HD2, 2, dtype=np.float32) / np.float32(HD2))).astype(np.float32)
    f = np.arange(S, dtype=np.float32)[None, :] * inv[row[:C] % J][:, None]
    put("turn", np.stack([np.cos(f), -np.sin(f), np.sin(f), np.cos(f)], 1))
    put("eye", np.eye(128))
    put("before", row[:, None] < row[None, :])
    put("ones", np.ones((128, 128)))
    put("unrouted", (99.0 * (q >= S))[:, None])
    trash = np.zeros((128, TOPK, TILES))
    pads = np.flatnonzero(q >= S)
    trash[pads] = (E * MOST + 1) * 128 + np.arange(TOPK * PADS).reshape(len(pads), TOPK, TILES)
    put("trash", trash)
    put("expert_slots", np.broadcast_to(MOST * 128 * np.arange(E), (128, E)))
    put("steps", np.broadcast_to(128.0 * np.arange(MOST), (128, MOST)))
    less = (np.arange(E)[None, :] < np.arange(E)[:, None]).reshape(1, -1)
    put("less", np.broadcast_to(less, (128, E * E)))
    put("iota", np.broadcast_to(np.arange(E), (128, E)))
    put("tile_iota", np.broadcast_to(np.arange(LISTED), (128, LISTED)))
    put("even_tiles", np.broadcast_to(2 * np.arange(1, SLOT_TILES // 2), (128, SLOT_TILES // 2 - 1)))
    put("neghalf", np.full((128, GT), -0.5))
    put("who", np.stack([(q >= 1) & (q < S), q == 0]))
    put("number", np.arange(TILES)[None, :] * IPT * S + ((row // 32) * S + np.minimum(q, S - 1))[:, None])
    put("spare", TOKENS + np.arange(128 * TABLE_TILES).reshape(128, TABLE_TILES) % 128)
    return t


def kernel(x, cls_tok, L0_tok_W, L0_tok_b, L0_attn_W_attn, L0_attn_b_attn, L0_attn_W_proj, L0_attn_b_proj,
           L0_ffn_norm1_w, L0_ffn_w_qkv, L0_ffn_w_out, L0_ffn_norm2_w, L0_ffn_w_router, L0_ffn_w_gate_up,
           L0_ffn_w_down):
    import concourse.bacc as bacc
    from concourse.bass_utils import run_bass_kernel_spmd

    f = lambda a: np.asarray(a, np.float32)
    edge = GRID * PATCH
    p = f(x)[:, :, :edge, :edge].reshape(IMAGES, CH, GRID, PATCH, GRID, PATCH).transpose(1, 3, 5, 0, 2, 4)
    padded = np.zeros((PK * 128, IMAGES, 32), np.float32)
    padded[:, :, 1:S] = p.reshape(PK * 128, IMAGES, S - 1)
    xp = padded.reshape(PK, 128, TILES, 128).transpose(2, 1, 0, 3).reshape(TILES, 128, PK * 128)

    fw = np.zeros((128, NFRONT), np.float32)

    def put(name, a):
        at, w = _F[name]
        fw[:a.shape[0], at:at + w] = a.reshape(a.shape[0], w)

    def chunks(a, n):
        return a.reshape(n, a.shape[0] // n, -1).transpose(1, 0, 2)

    put("wpatch", chunks(f(L0_tok_W).reshape(D, -1).T, PK))
    put("wqkv1", chunks(f(L0_attn_W_attn), 2))
    put("wproj", chunks(f(L0_attn_W_proj), 2))
    wq = f(L0_ffn_w_qkv)
    q = wq[:, :G * R * HD2].reshape(D, G, R, J, 2).transpose(0, 2, 4, 1, 3)
    k = wq[:, G * R * HD2:G * (R + 1) * HD2].reshape(D, G, J, 2).transpose(0, 3, 1, 2)[:, None]
    put("wqk2", chunks(np.concatenate([q, k], 1).reshape(D, -1), 2))
    put("wv2", chunks(wq[:, G * (R + 1) * HD2:], 2))
    wo = f(L0_ffn_w_out).reshape(G * R, HD2, D)
    put("wout", np.stack([wo[[r, R + r]].reshape(128, D) for r in range(R)]
                         + [wo[8 + 2 * r:10 + 2 * r].reshape(128, D) for r in range(2)], 1))
    put("wr", chunks(f(L0_ffn_w_router), 2))
    put("w2row", np.broadcast_to(f(L0_ffn_norm2_w)[None], (128, D)))
    cols = np.concatenate([f(L0_attn_b_attn).reshape(6, C), f(L0_ffn_norm1_w).reshape(2, C)]).T
    at = _F["small"][0]
    fw[:C, at:at + 8] = cols
    at = _F["bcls"][0]
    fw[0, at:at + D] = f(L0_tok_b)
    fw[1, at:at + D] = f(cls_tok).reshape(D)
    put("bprow", np.broadcast_to(f(L0_attn_b_proj)[None], (128, D)))

    wgu = f(L0_ffn_w_gate_up).reshape(E, 2, C, 2 * FF)[::-1].transpose(2, 0, 1, 3).reshape(C, -1)
    wdn = f(L0_ffn_w_down).reshape(E, 3, 128, D).transpose(2, 0, 1, 3).reshape(128, -1)
    arrays = {"xp": xp, "fw": fw, "cst": table_of_constants(), "wgu": wgu, "wdn": wdn}
    arrays = {n: np.ascontiguousarray(a) for n, a in arrays.items()}

    nc = bacc.Bacc("TRN2", target_bir_lowering=False, num_devices=1)
    args = [nc.dram_tensor(n, a.shape, F32, kind="ExternalInput").ap() for n, a in arrays.items()]
    moe_in = nc.dram_tensor("moe_in", (TOKENS + 128, D), F32, kind="Internal").ap()
    slots = nc.dram_tensor("slots", (TABLE_TILES * 128, 2), F32, kind="Internal").ap()
    out = nc.dram_tensor("out", (TOKENS + 128, D), F32, kind="ExternalOutput").ap()
    build_tower(nc, *args, moe_in, slots, out)
    r = run_bass_kernel_spmd(nc, [arrays], core_ids=[0])
    return r.results[0]["out"][:TOKENS].reshape(IMAGES, S, D)
```
